# Optimizing a Trainium2 kernel written in Bass

```python
import numpy as np
import jax
import jax.numpy as jnp

def _softmax(x, axis=-1):
    return jax.nn.softmax(x, axis=axis)

def _gelu(x):
    return jax.nn.gelu(x, approximate=True)

def _silu(x):
    return jax.nn.silu(x)

def _sigmoid(x):
    return jax.nn.sigmoid(x)

def _layernorm(x, axis=-1, eps=1e-05):
    m = jnp.mean(x, axis=axis, keepdims=True)
    v = jnp.var(x, axis=axis, keepdims=True)
    return (x - m) / jnp.sqrt(v + eps)

def _scatter_add(tgt, idx, src, axis=0):
    return tgt.at[idx].add(src)

def _segment_sum(src, seg, n):
    return jax.ops.segment_sum(src, seg, n)
kernel_name = 'mk_decoder_preln_d2_seqx_r8_80318d'

def setup_inputs(seed: int=0):
    np.random.seed(seed)
    _w = jnp.asarray

    def _rec_inputs():
        import jax
        import jax.numpy as jnp
        _rk = jax.random.key(seed)
        x = 7.22e-05 + 1 * jax.random.normal(jax.random.fold_in(_rk, 1), (8, 128, 512), jnp.float32)
        _lenS = 128 - jax.random.randint(jax.random.fold_in(_rk, 7), (8,), 0, max(1, 128 // 4) + 1, jnp.int32)
        _lenS2 = 128 - jax.random.randint(jax.random.fold_in(_rk, 8), (8,), 0, max(1, 128 // 4) + 1, jnp.int32)
        _ctx_4096P = jax.random.normal(jax.random.fold_in(_rk, 11), (8, 16, 512), jnp.float32)
        _ctx_4096c = jax.random.dirichlet(jax.random.fold_in(_rk, 511), 0.3 * jnp.ones((16,), jnp.float32), (8, 128))
        _ctx_4096t = jnp.einsum('bsk,bkd->bsd', _ctx_4096c, _ctx_4096P)
        _ctx_4096t = _ctx_4096t * jax.lax.rsqrt(jnp.mean(jnp.square(_ctx_4096t)) + 1e-12) * 0.953939
        ctx_4096 = 4.13588e-05 + 0.999923 * (_ctx_4096t + 0.3 * jax.random.normal(jax.random.fold_in(_rk, 611), (8, 128, 512), jnp.float32))
        _validS = jnp.arange(128)[None, :] < _lenS[:, None]
        _validS2 = jnp.arange(128)[None, :] < _lenS2[:, None]
        _causal = jnp.tril(jnp.ones((128, 128), dtype=bool))
        mask_BxSxS2_bk0 = jnp.logical_not(jnp.broadcast_to(_validS2[:, None, :], (8, 128, 128)))
        return (x, ctx_4096, mask_BxSxS2_bk0)
    x, ctx_4096, mask_BxSxS2_bk0 = _rec_inputs()

    def _L0_attn_setup():
        import jax, jax.numpy as jnp
        import numpy as np
        HIDDEN = 512
        NH = 32
        NKV = 8
        HD = 128
        GS = 128
        BASE = 10000.0
        B, S = (2, 256)

        def _dequant(codes, scales):
            w = codes.astype(jnp.float32) - 8.0
            return w * jnp.repeat(scales, GS, axis=0)

        def _rope(x):
            s, d = (x.shape[2], x.shape[3])
            pos = jnp.arange(s, dtype=jnp.float32)
            inv_freq = 1.0 / BASE ** (jnp.arange(0, d, 2, dtype=jnp.float32) / d)
            f = pos[:, None] * inv_freq[None, :]
            cos = jnp.cos(f)[None, None]
            sin = jnp.sin(f)[None, None]
            xe = x[..., ::2]
            xo = x[..., 1::2]
            re = xe * cos - xo * sin
            ro = xo * cos + xe * sin
            return jnp.stack([re, ro], axis=-1).reshape(x.shape)
        key = jax.random.key(seed)
        ks = jax.random.split(key, 9)

        def codes(k, i, o):
            return jax.random.randint(k, (i, o), 0, 16, dtype=jnp.int32)

        def scales(k, i, o):
            return jax.random.uniform(k, (i // GS, o), dtype=jnp.float32) * 0.02
        return {'hidden_states': jax.random.normal(ks[0], (B, S, HIDDEN), jnp.float32), 'q_codes': codes(ks[1], HIDDEN, NH * HD), 'q_scales': scales(ks[2], HIDDEN, NH * HD), 'k_codes': codes(ks[3], HIDDEN, NKV * HD), 'k_scales': scales(ks[4], HIDDEN, NKV * HD), 'v_codes': codes(ks[5], HIDDEN, NKV * HD), 'v_scales': scales(ks[6], HIDDEN, NKV * HD), 'o_codes': codes(ks[7], NH * HD, HIDDEN), 'o_scales': scales(ks[8], NH * HD, HIDDEN)}
    _L0_attn_all = _L0_attn_setup()
    _L0_attn_in = {k: v for k, v in _L0_attn_all.items() if k in ('q_codes', 'q_scales', 'k_codes', 'k_scales', 'v_codes', 'v_scales', 'o_codes', 'o_scales')}
    del _L0_attn_all

    def _L0_xattn_setup():
        import jax, jax.numpy as jnp
        import numpy as np
        B, LQ, LK, D, H, DH = (2, 128, 128, 512, 32, 128)
        EPS = 1e-05

        def _rmsnorm(x, weight):
            var = jnp.mean(jnp.square(x), axis=-1, keepdims=True)
            return x * jax.lax.rsqrt(var + EPS) * weight
        key = jax.random.key(seed)
        ks = jax.random.split(key, 8)
        scale = 0.02
        return {'hidden_states': jax.random.normal(ks[0], (B, LQ, D), jnp.float32), 'key_value_states': jax.random.normal(ks[1], (B, LK, D), jnp.float32), 'attention_mask': jax.random.randint(ks[2], (B, LQ, LK), 0, 2) > 0, 'position_bias': jax.random.normal(ks[3], (H, LQ, LK), jnp.float32), 'ln_weight': jnp.ones((D,), jnp.float32), 'w_q': jax.random.normal(ks[4], (H * DH, D), jnp.float32) * scale, 'w_k': jax.random.normal(ks[5], (H * DH, D), jnp.float32) * scale, 'w_v': jax.random.normal(ks[6], (H * DH, D), jnp.float32) * scale, 'w_out': jax.random.normal(ks[7], (D, H * DH), jnp.float32) * scale}
    _L0_xattn_all = _L0_xattn_setup()
    _L0_xattn_in = {k: v for k, v in _L0_xattn_all.items() if k in ('position_bias', 'ln_weight', 'w_q', 'w_k', 'w_v', 'w_out')}
    del _L0_xattn_all

    def _L0_ffn_setup():
        import jax, jax.numpy as jnp
        import numpy as np
        N_EXPERTS = 8
        TOP_K = 2
        D_MODEL = 512
        RANK = 64
        key = jax.random.key(seed)
        k0, k1, k2, k3 = jax.random.split(key, 4)
        inputs = jax.random.normal(k0, (4, 256, D_MODEL), dtype=jnp.float32)
        gate_w = jax.random.normal(k1, (N_EXPERTS, D_MODEL), dtype=jnp.float32) * 0.02
        lora_A = jax.random.normal(k2, (N_EXPERTS, RANK, D_MODEL), dtype=jnp.float32) * 0.02
        lora_B = jax.random.normal(k3, (N_EXPERTS, D_MODEL, RANK), dtype=jnp.float32) * 0.02
        return {'inputs': inputs, 'gate_w': gate_w, 'lora_A': lora_A, 'lora_B': lora_B}
    _L0_ffn_all = _L0_ffn_setup()
    _L0_ffn_in = {k: v for k, v in _L0_ffn_all.items() if k in ('gate_w', 'lora_A', 'lora_B')}
    del _L0_ffn_all

    def _L1_attn_setup():
        import math
        import jax, jax.numpy as jnp
        import numpy as np
        D_MODEL = 512
        N_HEADS = 32
        N_KV_HEADS = 8
        D_HEAD = D_MODEL // N_HEADS
        GROUP = N_HEADS // N_KV_HEADS
        ROPE = dict(rope_theta=500000.0, factor=32.0, hi_freq_factor=4.0, lo_freq_factor=1.0, original_context_length=1024)

        def _rope_cos_sin(head_dim, pos, dtype):
            idx = jnp.arange(0, head_dim, 2, dtype=jnp.float32) / head_dim
            freq = 1.0 / (2.0 * math.pi) * ROPE['rope_theta'] ** (-idx)
            factor, lo, hi = (ROPE['factor'], ROPE['lo_freq_factor'], ROPE['hi_freq_factor'])
            L0 = ROPE['original_context_length']
            freq_low, freq_high = (lo / L0, hi / L0)
            freq_scaled = jnp.where(freq < freq_low, freq / factor, freq)
            smooth = jnp.clip((L0 * freq - lo) / (hi - lo), 0.0, 1.0)
            freq_smooth = (1.0 - smooth) * (freq / factor) + smooth * freq
            is_mid = (freq >= freq_low) & (freq <= freq_high)
            freq = jnp.where(is_mid, freq_smooth, freq_scaled)
            phase = 2.0 * math.pi * pos.astype(jnp.float32)[:, None] * freq[None, :]
            emb = jnp.concatenate([phase, phase], axis=-1)
            return (jnp.cos(emb).astype(dtype), jnp.sin(emb).astype(dtype))

        def _rotate_half(x):
            h = x.shape[-1] // 2
            return jnp.concatenate([-x[..., h:], x[..., :h]], axis=-1)
        key = jax.random.key(seed)
        ks = jax.random.split(key, 5)
        B, T = (1, 256)
        s = 0.02
        return {'resid': jax.random.normal(ks[0], (B, T, D_MODEL), jnp.float32), 'Wq': jax.random.normal(ks[1], (D_MODEL, D_MODEL), jnp.float32) * s, 'Wk': jax.random.normal(ks[2], (D_MODEL, N_KV_HEADS * D_HEAD), jnp.float32) * s, 'Wv': jax.random.normal(ks[3], (D_MODEL, N_KV_HEADS * D_HEAD), jnp.float32) * s, 'Wo': jax.random.normal(ks[4], (D_MODEL, D_MODEL), jnp.float32) * s}
    _L1_attn_all = _L1_attn_setup()
    _L1_attn_in = {k: v for k, v in _L1_attn_all.items() if k in ('Wq', 'Wk', 'Wv', 'Wo')}
    del _L1_attn_all

    def _L1_xattn_setup():
        import jax, jax.numpy as jnp
        import numpy as np
        HID = 512
        NHEAD = 32
        NKV = 8
        HDIM = 128
        G = NHEAD // NKV
        key = jax.random.key(seed)
        ks = jax.random.split(key, 6)
        s = 0.02
        B, L = (2, 256)
        return {'query': jax.random.normal(ks[0], (B, L, HID), jnp.float32), 'kv': jax.random.normal(ks[1], (B, L, HID), jnp.float32), 'Wq': jax.random.normal(ks[2], (HID, NHEAD * HDIM), jnp.float32) * s, 'bq': jnp.zeros((NHEAD * HDIM,), jnp.float32), 'Wkv': jax.random.normal(ks[3], (HID, 2 * NKV * HDIM), jnp.float32) * s, 'bkv': jnp.zeros((2 * NKV * HDIM,), jnp.float32), 'Wo': jax.random.normal(ks[4], (NHEAD * HDIM, HID), jnp.float32) * s, 'bo': jnp.zeros((HID,), jnp.float32)}
    _L1_xattn_all = _L1_xattn_setup()
    _L1_xattn_in = {k: v for k, v in _L1_xattn_all.items() if k in ('Wq', 'bq', 'Wkv', 'bkv', 'Wo', 'bo')}
    del _L1_xattn_all

    def _L1_ffn_setup():
        import jax, jax.numpy as jnp
        import numpy as np
        LORA_RANK = 16
        LORA_ALPHA = 16
        LORA_SCALE = LORA_ALPHA / LORA_RANK
        key = jax.random.key(seed)
        k1, k2, k3, k4, k5 = jax.random.split(key, 5)
        B, S, D_IN, D_OUT, N_LORA, R = (8, 256, 512, 512, 3, LORA_RANK)
        std = 1.0 / np.sqrt(D_IN)
        x = jax.random.normal(k1, (B, S, D_IN), dtype=jnp.float32)
        weight = jax.random.truncated_normal(k2, -3.0, 3.0, (D_OUT, D_IN), dtype=jnp.float32) * std
        bias = jax.random.normal(k3, (D_OUT,), dtype=jnp.float32) * 0.01
        lora_A = jax.random.normal(k4, (N_LORA, R, D_IN), dtype=jnp.float32) * std
        lora_B = jax.random.normal(k5, (N_LORA, D_OUT, R), dtype=jnp.float32) * 0.02
        lora_start_indices = jnp.arange(4, dtype=jnp.int64) * 2
        return {'x': x, 'weight': weight, 'bias': bias, 'lora_A': lora_A, 'lora_B': lora_B, 'lora_start_indices': lora_start_indices}
    _L1_ffn_all = _L1_ffn_setup()
    _L1_ffn_in = {k: v for k, v in _L1_ffn_all.items() if k in ('weight', 'bias', 'lora_A', 'lora_B', 'lora_start_indices')}
    del _L1_ffn_all
    return {'x': x, 'ctx_4096': ctx_4096, 'mask_BxSxS2_bk0': mask_BxSxS2_bk0, 'L0_attn_q_codes': _L0_attn_in['q_codes'], 'L0_attn_q_scales': _L0_attn_in['q_scales'], 'L0_attn_k_codes': _L0_attn_in['k_codes'], 'L0_attn_k_scales': _L0_attn_in['k_scales'], 'L0_attn_v_codes': _L0_attn_in['v_codes'], 'L0_attn_v_scales': _L0_attn_in['v_scales'], 'L0_attn_o_codes': _L0_attn_in['o_codes'], 'L0_attn_o_scales': _L0_attn_in['o_scales'], 'L0_xattn_position_bias': _L0_xattn_in['position_bias'], 'L0_xattn_ln_weight': _L0_xattn_in['ln_weight'], 'L0_xattn_w_q': _L0_xattn_in['w_q'], 'L0_xattn_w_k': _L0_xattn_in['w_k'], 'L0_xattn_w_v': _L0_xattn_in['w_v'], 'L0_xattn_w_out': _L0_xattn_in['w_out'], 'L0_ffn_gate_w': _L0_ffn_in['gate_w'], 'L0_ffn_lora_A': _L0_ffn_in['lora_A'], 'L0_ffn_lora_B': _L0_ffn_in['lora_B'], 'L1_attn_Wq': _L1_attn_in['Wq'], 'L1_attn_Wk': _L1_attn_in['Wk'], 'L1_attn_Wv': _L1_attn_in['Wv'], 'L1_attn_Wo': _L1_attn_in['Wo'], 'L1_xattn_Wq': _L1_xattn_in['Wq'], 'L1_xattn_bq': _L1_xattn_in['bq'], 'L1_xattn_Wkv': _L1_xattn_in['Wkv'], 'L1_xattn_bkv': _L1_xattn_in['bkv'], 'L1_xattn_Wo': _L1_xattn_in['Wo'], 'L1_xattn_bo': _L1_xattn_in['bo'], 'L1_ffn_weight': _L1_ffn_in['weight'], 'L1_ffn_bias': _L1_ffn_in['bias'], 'L1_ffn_lora_A': _L1_ffn_in['lora_A'], 'L1_ffn_lora_B': _L1_ffn_in['lora_B'], 'L1_ffn_lora_start_indices': _L1_ffn_in['lora_start_indices']}

def reference(x, ctx_4096, mask_BxSxS2_bk0, L0_attn_q_codes, L0_attn_q_scales, L0_attn_k_codes, L0_attn_k_scales, L0_attn_v_codes, L0_attn_v_scales, L0_attn_o_codes, L0_attn_o_scales, L0_xattn_position_bias, L0_xattn_ln_weight, L0_xattn_w_q, L0_xattn_w_k, L0_xattn_w_v, L0_xattn_w_out, L0_ffn_gate_w, L0_ffn_lora_A, L0_ffn_lora_B, L1_attn_Wq, L1_attn_Wk, L1_attn_Wv, L1_attn_Wo, L1_xattn_Wq, L1_xattn_bq, L1_xattn_Wkv, L1_xattn_bkv, L1_xattn_Wo, L1_xattn_bo, L1_ffn_weight, L1_ffn_bias, L1_ffn_lora_A, L1_ffn_lora_B, L1_ffn_lora_start_indices):
    import jax
    import jax.numpy as jnp

    def _L0_attn_ref(hidden_states, q_codes, q_scales, k_codes, k_scales, v_codes, v_scales, o_codes, o_scales):
        import jax, jax.numpy as jnp
        import numpy as np
        HIDDEN = 512
        NH = 32
        NKV = 8
        HD = 128
        GS = 128
        BASE = 10000.0
        B, S = (2, 256)

        def _dequant(codes, scales):
            w = codes.astype(jnp.float32) - 8.0
            return w * jnp.repeat(scales, GS, axis=0)

        def _rope(x):
            s, d = (x.shape[2], x.shape[3])
            pos = jnp.arange(s, dtype=jnp.float32)
            inv_freq = 1.0 / BASE ** (jnp.arange(0, d, 2, dtype=jnp.float32) / d)
            f = pos[:, None] * inv_freq[None, :]
            cos = jnp.cos(f)[None, None]
            sin = jnp.sin(f)[None, None]
            xe = x[..., ::2]
            xo = x[..., 1::2]
            re = xe * cos - xo * sin
            ro = xo * cos + xe * sin
            return jnp.stack([re, ro], axis=-1).reshape(x.shape)
        b, s, _ = hidden_states.shape
        q = hidden_states @ _dequant(q_codes, q_scales)
        k = hidden_states @ _dequant(k_codes, k_scales)
        v = hidden_states @ _dequant(v_codes, v_scales)
        q = q.reshape(b, s, NH, HD).transpose(0, 2, 1, 3)
        k = k.reshape(b, s, NKV, HD).transpose(0, 2, 1, 3)
        v = v.reshape(b, s, NKV, HD).transpose(0, 2, 1, 3)
        q = _rope(q)
        k = _rope(k)
        rf = NH // NKV
        k = jnp.repeat(k, rf, axis=1)
        v = jnp.repeat(v, rf, axis=1)
        scale = HD ** (-0.5)
        causal = jnp.tril(jnp.ones((s, s), dtype=bool))
        mask = jnp.where(causal, 0.0, -jnp.inf).astype(q.dtype)
        scores = jnp.einsum('bhqd,bhkd->bhqk', q, k) * scale + mask[None, None]
        attn = jax.nn.softmax(scores, axis=-1)
        out = jnp.einsum('bhqk,bhkd->bhqd', attn, v)
        out = out.transpose(0, 2, 1, 3).reshape(b, s, NH * HD)
        return out @ _dequant(o_codes, o_scales)

    def _L0_xattn_ref(hidden_states, key_value_states, attention_mask, position_bias, ln_weight, w_q, w_k, w_v, w_out):
        import jax, jax.numpy as jnp
        import numpy as np
        B, LQ, LK, D, H, DH = (2, 128, 128, 512, 32, 128)
        EPS = 1e-05

        def _rmsnorm(x, weight):
            var = jnp.mean(jnp.square(x), axis=-1, keepdims=True)
            return x * jax.lax.rsqrt(var + EPS) * weight
        x = _rmsnorm(hidden_states, ln_weight)
        b, lq, _ = x.shape
        lk = key_value_states.shape[1]
        h_q = (x @ w_q.T).reshape(b, lq, H, DH)
        h_k = (key_value_states @ w_k.T).reshape(b, lk, H, DH)
        h_v = (key_value_states @ w_v.T).reshape(b, lk, H, DH)
        score = jnp.einsum('bqhd,bkhd->bhqk', h_q, h_k)
        score = score + position_bias[None]
        m = attention_mask[:, None]
        score = jnp.where(m, score, -jnp.inf)
        score = jax.nn.softmax(score, axis=-1)
        score = jnp.where(m, score, 0.0)
        attn = jnp.einsum('bhqk,bkhd->bqhd', score, h_v).reshape(b, lq, H * DH)
        out = attn @ w_out.T
        return hidden_states + out

    def _L0_ffn_ref(inputs, gate_w, lora_A, lora_B):
        import jax, jax.numpy as jnp
        import numpy as np
        N_EXPERTS = 8
        TOP_K = 2
        D_MODEL = 512
        RANK = 64
        x = inputs.reshape(-1, inputs.shape[-1])
        T = x.shape[0]
        gate_probs = jax.nn.softmax(x @ gate_w.T, axis=-1)
        weights, sel = jax.lax.top_k(gate_probs, TOP_K)
        weights = weights / jnp.sum(weights, axis=-1, keepdims=True)
        w_full = jnp.zeros((T, N_EXPERTS), dtype=x.dtype).at[jnp.arange(T)[:, None], sel].add(weights)
        out = jnp.zeros((T, D_MODEL), dtype=x.dtype)
        for e in range(N_EXPERTS):
            y = x @ lora_A[e].T @ lora_B[e].T
            out = out + w_full[:, e:e + 1] * y
        return out.reshape(inputs.shape[:-1] + (D_MODEL,))

    def _L1_attn_ref(resid, Wq, Wk, Wv, Wo):
        import math
        import jax, jax.numpy as jnp
        import numpy as np
        D_MODEL = 512
        N_HEADS = 32
        N_KV_HEADS = 8
        D_HEAD = D_MODEL // N_HEADS
        GROUP = N_HEADS // N_KV_HEADS
        ROPE = dict(rope_theta=500000.0, factor=32.0, hi_freq_factor=4.0, lo_freq_factor=1.0, original_context_length=1024)

        def _rope_cos_sin(head_dim, pos, dtype):
            idx = jnp.arange(0, head_dim, 2, dtype=jnp.float32) / head_dim
            freq = 1.0 / (2.0 * math.pi) * ROPE['rope_theta'] ** (-idx)
            factor, lo, hi = (ROPE['factor'], ROPE['lo_freq_factor'], ROPE['hi_freq_factor'])
            L0 = ROPE['original_context_length']
            freq_low, freq_high = (lo / L0, hi / L0)
            freq_scaled = jnp.where(freq < freq_low, freq / factor, freq)
            smooth = jnp.clip((L0 * freq - lo) / (hi - lo), 0.0, 1.0)
            freq_smooth = (1.0 - smooth) * (freq / factor) + smooth * freq
            is_mid = (freq >= freq_low) & (freq <= freq_high)
            freq = jnp.where(is_mid, freq_smooth, freq_scaled)
            phase = 2.0 * math.pi * pos.astype(jnp.float32)[:, None] * freq[None, :]
            emb = jnp.concatenate([phase, phase], axis=-1)
            return (jnp.cos(emb).astype(dtype), jnp.sin(emb).astype(dtype))

        def _rotate_half(x):
            h = x.shape[-1] // 2
            return jnp.concatenate([-x[..., h:], x[..., :h]], axis=-1)
        B, T, _ = resid.shape
        q = (resid @ Wq).reshape(B, T, N_HEADS, D_HEAD).transpose(0, 2, 1, 3)
        k = (resid @ Wk).reshape(B, T, N_KV_HEADS, D_HEAD).transpose(0, 2, 1, 3)
        v = (resid @ Wv).reshape(B, T, N_KV_HEADS, D_HEAD).transpose(0, 2, 1, 3)
        cos, sin = _rope_cos_sin(D_HEAD, jnp.arange(T), resid.dtype)
        cos = cos[None, None]
        sin = sin[None, None]
        q = q * cos + _rotate_half(q) * sin
        k = k * cos + _rotate_half(k) * sin
        qg = q.reshape(B, N_KV_HEADS, GROUP, T, D_HEAD)
        att = jnp.einsum('bhgqd,bhkd->bhgqk', qg.astype(jnp.float32), k.astype(jnp.float32)) / math.sqrt(D_HEAD)
        causal = jnp.tril(jnp.ones((T, T), dtype=bool))
        att = jnp.where(causal[None, None, None], att, -jnp.inf)
        probs = jax.nn.softmax(att, axis=-1).astype(resid.dtype)
        ctx = jnp.einsum('bhgqk,bhkd->bhgqd', probs, v)
        out = ctx.reshape(B, N_HEADS, T, D_HEAD).transpose(0, 2, 1, 3).reshape(B, T, D_MODEL)
        return out @ Wo

    def _L1_xattn_ref(query, kv, Wq, bq, Wkv, bkv, Wo, bo):
        import jax, jax.numpy as jnp
        import numpy as np
        HID = 512
        NHEAD = 32
        NKV = 8
        HDIM = 128
        G = NHEAD // NKV
        B, L, _ = query.shape
        Lk = kv.shape[1]
        scale = jnp.asarray(1.0 / np.sqrt(HDIM), query.dtype)
        q = (query @ Wq + bq).reshape(B, L, NKV, G, HDIM)
        k_, v_ = jnp.split(kv @ Wkv + bkv, 2, axis=-1)
        k = k_.reshape(B, Lk, NKV, HDIM)
        v = v_.reshape(B, Lk, NKV, HDIM)
        scores = jnp.einsum('blkgd,bmkd->bkglm', q, k) * scale
        attn = jax.nn.softmax(scores, axis=-1)
        o = jnp.einsum('bkglm,bmkd->blkgd', attn, v).reshape(B, L, NHEAD * HDIM)
        return o @ Wo + bo

    def _L1_ffn_ref(x, weight, bias, lora_A, lora_B, lora_start_indices):
        import jax, jax.numpy as jnp
        import numpy as np
        LORA_RANK = 16
        LORA_ALPHA = 16
        LORA_SCALE = LORA_ALPHA / LORA_RANK
        y = jnp.einsum('bsd,od->bso', x, weight) + bias
        B = x.shape[0]
        seg = jnp.searchsorted(lora_start_indices, jnp.arange(B), side='right') - 1
        adapter_idx = jnp.clip(seg - 1, 0, lora_A.shape[0] - 1)
        A = lora_A[adapter_idx]
        Bw = lora_B[adapter_idx]
        lo = jnp.einsum('bsr,bor->bso', jnp.einsum('bsd,brd->bsr', x, A), Bw) * LORA_SCALE
        use_lora = (seg > 0)[:, None, None]
        return y + jnp.where(use_lora, lo, jnp.zeros((), dtype=y.dtype))
    x = x + _L0_attn_ref(_layernorm(x, axis=-1), L0_attn_q_codes, L0_attn_q_scales, L0_attn_k_codes, L0_attn_k_scales, L0_attn_v_codes, L0_attn_v_scales, L0_attn_o_codes, L0_attn_o_scales)
    x = x + _L0_xattn_ref(_layernorm(x, axis=-1), ctx_4096, mask_BxSxS2_bk0, L0_xattn_position_bias, L0_xattn_ln_weight, L0_xattn_w_q, L0_xattn_w_k, L0_xattn_w_v, L0_xattn_w_out)
    x = x + _L0_ffn_ref(_layernorm(x, axis=-1), L0_ffn_gate_w, L0_ffn_lora_A, L0_ffn_lora_B)
    x = x + _L1_attn_ref(_layernorm(x, axis=-1), L1_attn_Wq, L1_attn_Wk, L1_attn_Wv, L1_attn_Wo)
    x = x + _L1_xattn_ref(_layernorm(x, axis=-1), ctx_4096, L1_xattn_Wq, L1_xattn_bq, L1_xattn_Wkv, L1_xattn_bkv, L1_xattn_Wo, L1_xattn_bo)
    x = x + _L1_ffn_ref(_layernorm(x, axis=-1), L1_ffn_weight, L1_ffn_bias, L1_ffn_lora_A, L1_ffn_lora_B, L1_ffn_lora_start_indices)
    return x

_drawn_inputs = setup_inputs


def setup_inputs(seed=0):
    import zlib

    import numpy as np

    out = dict(_drawn_inputs(seed))
    spreads = {'L0_xattn_ln_weight': (1.0, 0.6),
     'L1_xattn_bq': (0.0, 2.0),
     'L1_xattn_bkv': (0.0, 0.1),
     'L1_xattn_bo': (0.0, 0.1)}
    factors = {'L0_ffn_gate_w': 3.6,
     'L0_ffn_lora_A': 3.064,
     'L0_ffn_lora_B': 3.068,
     'L1_attn_Wq': 8.0,
     'L1_attn_Wk': 8.0,
     'L1_xattn_Wq': 7.247,
     'L1_ffn_bias': 8.0}
    for name, (base, spread) in spreads.items():
        noise = np.random.default_rng([zlib.crc32(name.encode()), seed]).standard_normal(out[name].shape)
        drawn = base * np.exp(spread * noise) if base else spread * noise
        out[name] = jnp.asarray(drawn.astype(out[name].dtype))
    for name, factor in factors.items():
        out[name] = (out[name] * factor).astype(out[name].dtype)
    return out
```

```python
from contextlib import ExitStack

import numpy as np

import concourse.bass as bass
from concourse import mybir

F32 = mybir.dt.float32
F32R = mybir.dt.float32r
I32 = mybir.dt.int32
U8 = mybir.dt.uint8
ALU = mybir.AluOpType
ACT = mybir.ActivationFunctionType
AX = mybir.AxisListType

B = 8
S = 128
D = 512
KT = D // 128
NH = 32
HD = 128
HALF = 4
TOK = HALF * S
EPS = 1e-5
MASKED = -1e30
HI, LO = 0, 1


def matmul3(pe, out, stationary, moving, first, last):
    pe.matmul(out, stationary(HI), moving(HI), start=first, stop=False, skip_group_check=True)
    pe.matmul(out, stationary(HI), moving(LO), start=False, stop=False, skip_group_check=True)
    return pe.matmul(out, stationary(LO), moving(HI), start=False, stop=last, skip_group_check=True)


def wait_count(eng, sem, count):
    if isinstance(count, int) and count <= 0:
        return
    eng.wait_ge(sem, count)


class Semaphores:

    def __init__(self, nc):
        self.nc, self.handles = nc, []

    def new(self, name):
        self.handles.append(self.nc.alloc_semaphore(name=name))
        return self.handles[-1]

    def clear(self):
        self.nc.clear_and_free_semaphores(self.handles)
        self.handles = []
        self.nc.all_engine_barrier()


def as_f32(ap):
    return ap.bitcast(F32)


class Norm:

    def __init__(self, ctx, sems, nc, name, x, xT, scratch, banks, ident, rms_weight=None):
        self.nc, self.x, self.xT, self.scratch, self.banks, self.ident = nc, x, xT, scratch, banks, ident
        self.rms_weight = rms_weight

        def small(n, shape):
            return ctx.enter_context(nc.sbuf_tensor(f"{name}_{n}", shape, F32))

        def sem(n):
            return sems.new(f"{name}_{n}")

        self.stats = small("stats", [128, B, 6])
        self.mean_var = small("mean_var", [128, B, 2])
        self.var_eps = small("var_eps", [128, B])
        self.minus_half = small("minus_half", [128, B])
        self.rstd = small("rstd", [128, B])
        if rms_weight is not None:
            self.square_sum = small("square_sum", [128, B])
            self.ms_eps = small("ms_eps", [128, B])
            self.rrms = small("rrms", [128, B])
            self.both = small("both", [128, B])
            self.one_plus = small("one_plus", [128, B])
            self.mean_rstd = small("mean_rstd", [128, B])
            self.h_ready = sem("h_ready")
            self.squared = sem("squared")
            self.rrms_ready = sem("rrms_ready")
        self.stats_ready = sem("stats_ready")
        self.var_ready = sem("var_ready")
        self.half_set = sem("half_set")
        self.rstd_ready = sem("rstd_ready")
        self.small_done = sem("small_done")
        self.normed = sem("normed")
        self.transposed = sem("transposed")
        self.hi_ready = sem("xt_hi_ready")
        self.ready = sem("xt_ready")

    def vector(self, dve, x_ready=None):
        for b in range(B):
            if x_ready is not None and b % HALF == 0:
                dve.wait_ge(x_ready[b // HALF], 16)
            dve.bn_stats(self.stats[:, b, :], self.x[:, b, :]).then_inc(self.stats_ready, 1)
        for b in range(B):
            dve.wait_ge(self.stats_ready, b + 1)
            last = dve.bn_aggr(self.mean_var[:, b, :], self.stats[:, b, :])
        last.then_inc(self.small_done, 1)
        dve.wait_ge(self.small_done, 1)
        dve.tensor_scalar(self.var_eps[:], self.mean_var[:, :, 1], EPS, None, ALU.add).then_inc(self.var_ready, 1)
        dve.wait_ge(self.rstd_ready, 1)
        scale = self.rstd
        if self.rms_weight is not None:
            for b in range(B):
                if b >= 2:
                    dve.wait_ge(self.squared, b - 1)
                dve.tensor_scalar(self.scratch[:, b % 2, :], self.x[:, b, :], self.mean_var[:, b, 0:1],
                                  self.rstd[:, b:b + 1], ALU.subtract, ALU.mult).then_inc(self.h_ready, 1)
            dve.wait_ge(self.squared, B)
            dve.tensor_scalar(self.ms_eps[:], self.square_sum[:], 1.0 / D, EPS, ALU.mult, ALU.add)\
               .then_inc(self.var_ready, 1)
            dve.tensor_scalar(self.one_plus[:], self.rstd[:], 1.0, None, ALU.add)
            dve.tensor_tensor(self.mean_rstd[:], self.mean_var[:, :, 0], self.rstd[:], ALU.mult)\
               .then_inc(self.small_done, 1)
            dve.wait_ge(self.rrms_ready, 1)
            dve.tensor_tensor(self.both[:], self.rstd[:], self.rrms[:], ALU.mult).then_inc(self.small_done, 1)
            dve.wait_ge(self.small_done, 3)
            scale = self.both
        for b in range(B + 1):
            if b < B:
                if b >= 2:
                    dve.wait_ge(self.transposed, b - 1)
                dve.tensor_scalar(self.scratch[:, b % 2, :], self.x[:, b, :], self.mean_var[:, b, 0:1],
                                  scale[:, b:b + 1], ALU.subtract, ALU.mult).then_inc(self.normed, 1)
                if self.rms_weight is not None:
                    dve.wait_ge(self.normed, b + 1)
                    dve.tensor_scalar(self.x[:, b, :], self.x[:, b, :], self.one_plus[:, b:b + 1],
                                      self.mean_rstd[:, b:b + 1], ALU.mult, ALU.subtract)
            if b >= 1:
                self.vector_low(dve, b - 1)

    def vector_low(self, dve, b):
        bank = self.banks[:, b % 2, :].rearrange("p (k t) -> p k t", k=KT)
        tokens = slice(b * S, (b + 1) * S)
        dve.wait_ge(self.hi_ready, b + 1)
        if self.rms_weight is None:
            dve.tensor_tensor(self.xT[:, LO, :, tokens], bank, as_f32(self.xT[:, HI, :, tokens]), ALU.subtract)\
               .then_inc(self.ready, 1)
        else:
            for k in range(KT):
                last = dve.scalar_tensor_tensor(self.xT[:, LO, k, tokens], bank[:, k, :],
                                                self.rms_weight[:, k:k + 1],
                                                as_f32(self.xT[:, HI, k, tokens]), ALU.mult, ALU.subtract)
            last.then_inc(self.ready, 1)

    def gpsimd(self, pool):
        pool.memset(self.minus_half[:], -0.5).then_inc(self.half_set, 1)
        pool.wait_ge(self.half_set, 1)
        pool.wait_ge(self.var_ready, 1)
        pool.tensor_tensor(self.rstd[:], self.var_eps[:], self.minus_half[:], ALU.pow).then_inc(self.rstd_ready, 1)
        if self.rms_weight is not None:
            pool.wait_ge(self.var_ready, 2)
            pool.tensor_tensor(self.rrms[:], self.ms_eps[:], self.minus_half[:], ALU.pow)\
                .then_inc(self.rrms_ready, 1)

    def tensor(self, pe):
        for b in range(B):
            pe.wait_ge(self.normed, b + 1)
            if b >= 2:
                pe.wait_ge(self.ready, b - 1)
            for k in range(KT):
                last = pe.transpose(self.banks[:, b % 2, k * 128:(k + 1) * 128],
                                    self.scratch[:, b % 2, k * 128:(k + 1) * 128], self.ident[:])
            last.then_inc(self.transposed, 1)

    def scalar(self, act):
        if self.rms_weight is not None:
            for b in range(B):
                act.wait_ge(self.h_ready, b + 1)
                act.activation(self.banks[:, b % 2, :], self.scratch[:, b % 2, :], ACT.Square,
                               accum_out=self.square_sum[:, b:b + 1]).then_inc(self.squared, 1)
        for b in range(B):
            act.wait_ge(self.transposed, b + 1)
            bank = self.banks[:, b % 2, :].rearrange("p (k t) -> p k t", k=KT)
            tokens = slice(b * S, (b + 1) * S)
            if self.rms_weight is None:
                act.activation(self.xT[:, HI, :, tokens], bank, ACT.Copy).then_inc(self.hi_ready, 1)
            else:
                for k in range(KT):
                    last = act.activation(self.xT[:, HI, k, tokens], bank[:, k, :], ACT.Copy,
                                          scale=self.rms_weight[:, k:k + 1])
                last.then_inc(self.hi_ready, 1)


class Plan:

    PER_HALF = 6

    def __init__(self, shared_kv):
        self.shared_kv = shared_kv
        if shared_kv:
            self.heads, self.kv_heads, self.unit_batches = 4, 1, 1
            self.tasks = [("q", 0), ("k", 0), ("q", 1), ("q", 2), ("q", 3), ("v", 0)]
            self.phases = [[0, 1], [2, 3], [4], [5]]
            self.splits = {1: [("q", 0), ("k", 0)], 2: [("q", 1)], 3: [("q", 2)], 4: [("q", 3), ("v", 0)],
                           5: [("o", 0)], 6: [("o", 1), ("o", 2)], 7: [("o", 3)]}
        else:
            self.heads, self.kv_heads, self.unit_batches = 2, 2, 2
            self.tasks = [("q", 0), ("k", 0), ("q", 1), ("k", 1), ("v", 0), ("v", 1)]
            self.phases = [[0, 1, 2], [3, 4, 5]]
            self.splits = {0: [("q", 0), ("k", 0), ("q", 1)], 1: [("k", 1), ("v", 0), ("v", 1)],
                           2: [("o", 0)], 3: [("o", 1)]}
        self.groups = NH // self.heads
        self.half_units = HALF // self.unit_batches
        self.group_units = 2 * self.half_units
        self.units = self.groups * self.group_units
        self.order = [c for j in sorted(self.splits) for c in self.splits[j]]
        self.chunks = len(self.order)
        self.slots = self.chunks // 2
        self.first_step = self.group_units - self.half_units - 1
        self.qk_per_half = sum(kind != "v" for kind, _ in self.tasks)

    def chunk_number(self, chunk, cycle):
        return self.chunks * (cycle + 1) + self.order.index(chunk)

    def chunk_slot(self, chunk):
        return self.order.index(chunk) % self.slots

    def pairs(self, j):
        first = (j % self.half_units) * self.unit_batches
        if self.shared_kv:
            return [(first, h) for h in range(self.heads)]
        return [(first + b, h) for b in range(self.unit_batches) for h in range(self.heads)]

    def half_of(self, j):
        return (j // self.half_units) % 2

    def target(self, j):
        return (j + 1) // self.half_units + 1, self.phases[(j + 1) % self.half_units]

    def bank_of(self, task):
        return task % 3


def each_step(eng, plan, step):
    for j in range(plan.first_step, plan.group_units):
        step(-1, j, True, 1)
    for j in range(plan.group_units):
        step(0, j, True, 0)
    with eng.Fori(0, plan.groups // 2 - 1) as turn:
        for odd in (1, 0):
            for j in range(plan.group_units):
                step(turn * 2 + (2 - odd), j, False, odd)
    for j in range(plan.group_units):
        step(plan.groups - 1, j, True, (plan.groups - 1) % 2)
    step(plan.groups, 0, True, plan.groups % 2)


def attention(nc, sems, name, plan, x, ident, weights, source, rope=None, causal=None, pad_mask=None,
              position_bias=None, rms_weight=None, codes=False, out_bias=None,
              scale=1.0, x_dram=None):
    P = plan
    H, NK, BU, UG, UH = P.heads, P.kv_heads, P.unit_batches, P.group_units, P.half_units
    biases = out_bias
    masked = causal is not None or pad_mask is not None
    with ExitStack() as ctx:
        def sb(n, shape, dt=F32):
            return ctx.enter_context(nc.sbuf_tensor(f"{name}_{n}", shape, dt))

        def pb(n, shape):
            return ctx.enter_context(nc.psum_tensor(f"{name}_{n}", shape, F32))

        def sem(n):
            return sems.new(f"{name}_{n}")

        xT = sb("xT", [128, 2, KT, B * S], F32R)
        scratch = sb("scratch", [128, 2, D])
        probs = scratch[:, 0, :]
        masked_scores = scratch[:, 1, :]
        w_q = sb("w_q", [128, 2, H, D], F32R)
        w_k = sb("w_k", [128, 2, NK, D], F32R)
        w_v = sb("w_v", [128, 2, NK, D], F32R)
        w_o = sb("w_o", [128, 2, 2, H, D], F32R)

        def weight(kind, i, part, odd):
            if kind == "o":
                return w_o[:, part, 1 - odd, i, :]
            return {"q": w_q, "k": w_k, "v": w_v}[kind][:, part, i, :]
        staged = sb("staged", [128, P.slots, D + (biases is not None)], I32 if codes else F32)
        qT = sb("qT", [128, 2, 2, H, TOK], F32R)
        kT = sb("kT", [128, 2, 2, NK, TOK], F32R)
        v_tok = sb("v_tok", [128, 2, 2, HALF, NK * HD], F32R)
        probsT = sb("probsT", [128, 2, TOK], F32R)
        outT = sb("outT", [128, 2, TOK], F32R)
        vT = [sb(f"vT{i}", [128, TOK])[:] for i in range(NK)] if masked else [scratch[:, 1, :]]
        neg_max = sb("neg_max", [128, 4])
        exp_bias = sb("exp_bias", [128, 4]) if scale != 1.0 else neg_max
        exp_sum = sb("exp_sum", [128, 4])
        inv_sum = sb("inv_sum", [128, 4])

        proj_bank = pb("proj_bank", [128, 3, 512])
        score_bank = pb("score_bank", [128, 512])
        probsT_bank = pb("probsT_bank", [128, 512])
        outT_bank = pb("outT_bank", [128, 512])
        out_bank = pb("out_bank", [128, 2, 512])

        norm = Norm(ctx, sems, nc, f"{name}_norm", x, xT, scratch, out_bank, ident, rms_weight)

        chunk_loaded = [sem(f"chunk_loaded{i}") for i in range(P.slots)]
        chunk_hi = sem("chunk_hi")
        chunk_ready = sem("chunk_ready")
        projected = sem("projected")
        v_projected = sem("v_projected")
        v_copied = sem("v_copied")
        task_hi = sem("task_hi")
        task_read = sem("task_read")
        scored = sem("scored")
        biased = sem("biased")
        row_max = sem("row_max")
        bias_ready = sem("exp_bias_ready") if scale != 1.0 else row_max
        exped = sem("exped")
        summed = sem("sum_inverted")
        inv_ready = sem("inv_ready") if pad_mask is not None else summed
        probs_ready = sem("probs_ready")
        probs_transposed = sem("probs_transposed")
        probsT_hi = sem("probsT_hi")
        probsT_ready = sem("probsT_ready")
        attended = sem("attended")
        outT_hi = sem("outT_hi")
        outT_ready = sem("outT_ready")
        out_done = sem("out_done")
        out_added = sem("out_added")
        x_loaded = [sem(f"x_loaded{h}") for h in range(2)] if x_dram is not None else None
        const_loaded = sem("const_loaded")
        parts = 1
        if codes:
            scales = sb("scales", [128, P.slots, D])
            converted, dequantized = sem("converted"), sem("dequantized")
            parts = 2
        if rope is not None:
            cosine, sine = sb("cosine", [128, S]), sb("sine", [128, S])
            direct = sb("direct", [128, 2, TOK])
            crossed = sb("crossed", [128, 2, TOK])
            rotated, qk_ready = sem("rotated"), sem("qk_ready")
        if causal is not None:
            causal_add = sb("causal_add", [128, S])
        if biases is not None:
            columns = {"q": sb("bias_q", [128, H]), "k": sb("bias_k", [128, NK]), "v": sb("bias_v", [128, NK])}
            bias_o = staged[:, 0, 0:D]
            out_bias_loaded = sem("out_bias_loaded")
        if pad_mask is not None:
            mask_bytes = sb("mask_bytes", [128, B, S], U8)
            pad_add = sb("pad_add", [128, B, S])
            row_any = sb("row_any", [128, B])
            head_bias = sb("head_bias", [128, H, S])
            mask_ready, head_bias_loaded = sem("mask_ready"), sem("head_bias_loaded")
        if source is not None:
            kvT = sb("kvT", [128, 2, KT, B * S], F32R)
            context_loaded = [sem(f"context_loaded{i}") for i in range(2)]
            context_hi, context_ready = sem("context_hi"), sem("context_ready")
            early = len(P.splits[1]) + len(P.splits[2]) if P.shared_kv else P.slots
            context_raw = (staged[:, early:early + 2, 0:512] if early + 2 <= P.slots
                           else sb("context_raw", [128, 2, 512])[:])
        else:
            kvT = xT
        if rms_weight is not None:
            rms_cols = sb("rms_cols", [128, KT])
            norm.rms_weight = rms_cols
        CONTEXT_PIECES = KT * 2
        n_consts = (rms_weight is not None) + 2 * (rope is not None) + (causal is not None) + (pad_mask is not None)

        block = ctx.enter_context(nc.Block())

        def unit_there(s, fixed):
            return not fixed or 0 <= s < P.units

        def half_there(h, fixed):
            return not fixed or 0 <= h < 2 * P.groups

        def splits_at(g, j, fixed):
            for kind, i in P.splits.get(j, []):
                of = g + 1
                if fixed and not 0 <= of < P.groups:
                    continue
                yield kind, i, P.chunk_number((kind, i), g), P.chunk_slot((kind, i)), of

        def first_splits():
            for j in sorted(P.splits):
                if j < P.first_step:
                    for kind, i in P.splits[j]:
                        yield kind, i, P.chunk_number((kind, i), -1), P.chunk_slot((kind, i)), 0

        def tasks_at(g, j, fixed):
            ahead, places = P.target(j)
            half = 2 * g + ahead
            if not half_there(half, fixed):
                return
            for k in places:
                yield P.tasks[k][0], P.tasks[k][1], k, half, P.PER_HALF * half + k, ahead % 2

        def last_task_use(kind, i, of):
            return P.PER_HALF * (2 * of - 1) + P.tasks.index((kind, i)) + 1

        def chunk_load_count(kind, i, cycle):
            return 16 * parts * (2 * (cycle + 1) + P.order.index((kind, i)) // P.slots + 1)

        def turns_at(g, j, fixed):
            half = 2 * g + j // UH + 1
            if (j + 1) % UH == 0 and half_there(half, fixed):
                for k, (kind, i) in enumerate(P.tasks):
                    if kind == "v":
                        yield kind, i, k, half, P.PER_HALF * half + k, (j // UH + 1) % 2

        @block.sync
        def _(sp):
            if x_dram is not None:
                for h in range(2):
                    sp.dma_start(x[:, h * HALF:(h + 1) * HALF, :], x_dram[h * HALF:(h + 1) * HALF]
                                 .rearrange("b p n -> p b n")).then_inc(x_loaded[h], 16)
            if rms_weight is not None:
                sp.dma_start(rms_cols[:], rms_weight).then_inc(const_loaded, 16)
            if rope is not None:
                sp.dma_start(cosine[:], rope[0]).then_inc(const_loaded, 16)
                sp.dma_start(sine[:], rope[1]).then_inc(const_loaded, 16)
            if causal is not None:
                sp.dma_start(causal_add[:], causal).then_inc(const_loaded, 16)
            if pad_mask is not None:
                sp.dma_start(mask_bytes[:], pad_mask).then_inc(const_loaded, 16)

            def load_head_bias(g):
                wait_count(sp, biased, 2 * UG * g)
                sp.dma_start(head_bias[:], position_bias[bass.ds(g * H, H)].rearrange("h q k -> q h k"))\
                  .then_inc(head_bias_loaded, 16)

            def load(kind, i, number, slot, of):
                wait_count(sp, chunk_ready, number - P.slots + 1)
                per_group = H if kind in "qo" else NK
                at = of * per_group + i
                width = weights[kind].shape[2]
                sp.dma_start(staged[:, slot, 0:width], weights[kind][bass.ds(at, 1)].rearrange("o p n -> (o p) n"))\
                  .then_inc(chunk_loaded[slot], 16)
                if codes:
                    sp.dma_start(scales[:, slot, :], weights[kind + "_scales"][bass.ds(at, 1)]
                                 .rearrange("o n -> (o n)").partition_broadcast(128))\
                      .then_inc(chunk_loaded[slot], 16)

            for args in first_splits():
                load(*args)
            if source is not None:
                for n in range(CONTEXT_PIECES):
                    if n >= 2:
                        sp.wait_ge(context_ready, n - 1)
                    sp.dma_start(context_raw[:, n % 2, :], source[n]).then_inc(context_loaded[n % 2], 16)
                sp.wait_ge(context_ready, CONTEXT_PIECES)
            if position_bias is not None:
                load_head_bias(0)

            def step(g, j, fixed, odd):
                for args in splits_at(g, j, fixed):
                    load(*args)
                if position_bias is not None and j == UG - 1 and (not fixed or 0 <= g < P.groups - 1):
                    load_head_bias(g + 1)
            each_step(sp, P, step)
            if biases is not None:
                sp.wait_ge(chunk_ready, P.chunks * P.groups)
                sp.dma_start(bias_o, out_bias.partition_broadcast(128)).then_inc(out_bias_loaded, 16)

        @block.tensor
        def _(pe):
            wait_count(pe, const_loaded, 16 * n_consts)
            norm.tensor(pe)

            def step(g, j, fixed, odd):
                s = g * UG + j
                if unit_there(s, fixed):
                    wait_count(pe, probs_ready, s + 1)
                    for i in range(4):
                        last = pe.transpose(probsT_bank[:, i * S:(i + 1) * S], probs[:, i * S:(i + 1) * S], ident[:])
                    last.then_inc(probs_transposed, 1)
                if unit_there(s + 1, fixed):
                    j1 = (j + 1) % UG
                    g1 = g + (j + 1) // UG
                    if j1 % UH == 0:
                        half = 2 * g1 + P.half_of(j1)
                        if rope is not None:
                            wait_count(pe, qk_ready, P.qk_per_half * (half + 1))
                        else:
                            wait_count(pe, task_read, P.PER_HALF * half + P.qk_per_half)
                    slot = P.half_of(j1)
                    for i, (b, h) in enumerate(P.pairs(j1)):
                        tok = slice(b * S, (b + 1) * S)
                        last = matmul3(pe, score_bank[:, i * S:(i + 1) * S], lambda p: qT[:, p, slot, h, tok],
                                       lambda p: kT[:, p, slot, 0 if P.shared_kv else h, tok], True, True)
                    last.then_inc(scored, 1)
                if unit_there(s - 1, fixed):
                    wait_count(pe, outT_ready, s)
                    if j == 1:
                        wait_count(pe, chunk_ready, P.chunk_number(("o", H - 1), g - 1) + 1)
                    slot = odd if j > 0 else 1 - odd
                    pairs = P.pairs((j - 1) % UG)
                    for bi in range(BU):
                        number = (s - 1) * BU + bi
                        bank = (j - 1 + bi) % 2 if BU == 1 else bi
                        wait_count(pe, out_added, number - 1)
                        mine = [i for i, (b, h) in enumerate(pairs) if b == pairs[0][0] + bi]
                        for n, i in enumerate(mine):
                            h = pairs[i][1]
                            last = matmul3(pe, out_bank[:, bank, :], lambda p: outT[:, p, i * S:(i + 1) * S],
                                           lambda p: w_o[:, p, slot, h, :], n == 0, n == len(mine) - 1)
                        last.then_inc(out_done, 1)
                if unit_there(s, fixed):
                    wait_count(pe, probsT_ready, s + 1)
                    slot = P.half_of(j)
                    if j % UH == 0:
                        wait_count(pe, task_read, P.PER_HALF * (2 * g + slot + 1))
                    if P.shared_kv:
                        b = P.pairs(j)[0][0]
                        last = matmul3(pe, outT_bank[:], lambda p: v_tok[:, p, slot, b, :],
                                       lambda p: probsT[:, p, :], True, True)
                    else:
                        for i, (b, h) in enumerate(P.pairs(j)):
                            last = matmul3(pe, outT_bank[:, i * S:(i + 1) * S],
                                           lambda p: v_tok[:, p, slot, b, h * HD:(h + 1) * HD],
                                           lambda p: probsT[:, p, i * S:(i + 1) * S], True, True)
                    last.then_inc(attended, 1)
                for kind, i, k, half, number, slot in turns_at(g, j, fixed):
                    wait_count(pe, v_copied, P.kv_heads * half + i + 1)
                    for b in range(HALF):
                        last = pe.transpose(proj_bank[:, P.bank_of(k), b * S:(b + 1) * S],
                                            vT[i][:, b * S:(b + 1) * S], ident[:])
                    last.then_inc(projected, 1)
                for kind, i, k, half, number, slot in tasks_at(g, j, fixed):
                    bank = proj_bank[:, P.bank_of(k), :]
                    wait_count(pe, task_read, number - 2)
                    if slot == 0:
                        of = g + P.target(j)[0] // 2
                        wait_count(pe, chunk_ready, P.chunk_number((kind, i), of - 1) + 1)
                    if fixed and half < 2:
                        if k == 0:
                            pe.wait_ge(norm.ready, HALF * (half + 1))
                        if source is not None and half == 0 and k == 1:
                            pe.wait_ge(context_ready, CONTEXT_PIECES)
                    src, w = {"q": (xT, w_q), "k": (kvT, w_k), "v": (kvT, w_v)}[kind]
                    for kt in range(KT):
                        last = matmul3(pe, bank, lambda p: w[:, p, i, kt * 128:(kt + 1) * 128],
                                       lambda p: src[:, p, kt, slot * TOK:(slot + 1) * TOK], kt == 0, kt == KT - 1)
                    last.then_inc(v_projected if kind == "v" else projected, 1)
            each_step(pe, P, step)

        def v_part(part, slot, i):
            return v_tok[:, part, slot, :, i * HD:(i + 1) * HD]

        def v_bank(k):
            return proj_bank[:, P.bank_of(k), :].rearrange("p (b n) -> p b n", n=HD)

        @block.scalar
        def _(act):
            def split_high(args, cycle, odd):
                kind, i, number, slot, of = args
                if kind == "o":
                    wait_count(act, out_done, cycle * UG * BU)
                else:
                    wait_count(act, projected, last_task_use(kind, i, of))
                if codes:
                    wait_count(act, dequantized, number + 1)
                else:
                    act.wait_ge(chunk_loaded[slot], chunk_load_count(kind, i, cycle))
                raw = as_f32(staged[:, slot, 0:D]) if codes else staged[:, slot, 0:D]
                if biases is not None and kind != "o":
                    wait_count(act, task_read, last_task_use(kind, i, of))
                    act.activation(columns[kind][:, i:i + 1], staged[:, slot, D:D + 1], ACT.Copy)
                act.activation(weight(kind, i, HI, odd), raw, ACT.Copy).then_inc(chunk_hi, 1)

            def convert(args, cycle):
                kind, i, number, slot, of = args
                act.wait_ge(chunk_loaded[slot], chunk_load_count(kind, i, cycle))
                act.activation(as_f32(staged[:, slot, :]), staged[:, slot, :], ACT.Copy, bias=-8.0)\
                   .then_inc(converted, 1)

            def split_all(chunks, cycle, odd):
                if codes:
                    for args in chunks:
                        convert(args, cycle)
                for args in chunks:
                    split_high(args, cycle, odd)

            wait_count(act, const_loaded, 16 * n_consts)
            split_all(list(first_splits()), -1, 1)
            if source is not None:
                for n in range(CONTEXT_PIECES):
                    act.wait_ge(context_loaded[n % 2], 16 * (n // 2 + 1))
                    act.activation(kvT[:, HI, n // 2, (n % 2) * 512:(n % 2 + 1) * 512], context_raw[:, n % 2, :],
                                   ACT.Copy).then_inc(context_hi, 1)
            norm.scalar(act)

            def tasks_high(g, j, fixed):
                for kind, i, k, half, number, slot in tasks_at(g, j, fixed):
                    bank = proj_bank[:, P.bank_of(k), :]
                    if kind in "qk":
                        out = (qT if kind == "q" else kT)[:, HI, slot, i, :]
                        if rope is not None:
                            place = [n for n, t in enumerate(P.tasks) if t[0] != "v"].index(k)
                            act.wait_ge(rotated, P.qk_per_half * half + place + 1)
                            act.activation(out, direct[:, (P.qk_per_half * slot + place) % 2, :], ACT.Copy)\
                               .then_inc(task_hi, 1)
                            continue
                        act.wait_ge(projected, number + 1)
                        done = task_hi
                    else:
                        out, done = vT[i], v_copied
                        act.wait_ge(v_projected, P.kv_heads * half + i + 1)
                    if biases is not None:
                        act.activation(out, bank, ACT.Identity, bias=columns[kind][:, i:i + 1]).then_inc(done, 1)
                    else:
                        act.activation(out, bank, ACT.Copy).then_inc(done, 1)

            def step(g, j, fixed, odd):
                s = g * UG + j
                if unit_there(s, fixed):
                    act.wait_ge(probs_transposed, s + 1)
                    act.activation(probsT[:, HI, :], probsT_bank[:], ACT.Copy).then_inc(probsT_hi, 1)
                if rope is not None:
                    tasks_high(g - (j == 0), (j - 1) % UG, fixed)
                if unit_there(s + 1, fixed):
                    wait_count(act, bias_ready, s + 2)
                    scores = masked_scores if masked else score_bank[:]
                    for i in range(4):
                        last = act.activation(probs[:, i * S:(i + 1) * S], scores[:, i * S:(i + 1) * S], ACT.Exp,
                                              bias=exp_bias[:, i:i + 1], scale=scale, accum_out=exp_sum[:, i:i + 1])
                    last.then_inc(exped, 1)
                for kind, i, k, half, number, slot in turns_at(g, j, fixed):
                    act.wait_ge(projected, number + 1)
                    act.activation(v_part(HI, slot, i), v_bank(k), ACT.Copy).then_inc(task_hi, 1)
                if unit_there(s, fixed):
                    act.wait_ge(attended, s + 1)
                    wait_count(act, out_done, s * BU)
                    act.activation(outT[:, HI, :], outT_bank[:], ACT.Copy).then_inc(outT_hi, 1)
                if rope is None:
                    tasks_high(g, j, fixed)
                split_all(list(splits_at(g, j, fixed)), g, odd)
            each_step(act, P, step)

        @block.vector
        def _(dve):
            wait_count(dve, const_loaded, 16 * n_consts)
            if pad_mask is not None:
                dve.tensor_scalar(pad_add[:], mask_bytes[:], 1.0, -MASKED, ALU.subtract, ALU.mult)
                dve.tensor_reduce(row_any[:], mask_bytes[:], AX.X, ALU.max).then_inc(mask_ready, 1)
                dve.wait_ge(mask_ready, 1)
            norm.vector(dve, x_loaded)

            def step(g, j, fixed, odd):
                s = g * UG + j
                if unit_there(s, fixed):
                    dve.wait_ge(probsT_hi, s + 1)
                    dve.tensor_tensor(probsT[:, LO, :], probsT_bank[:], as_f32(probsT[:, HI, :]), ALU.subtract)\
                       .then_inc(probsT_ready, 1)
                if unit_there(s + 1, fixed):
                    j1 = (j + 1) % UG
                    pairs = P.pairs(j1)
                    batch = P.half_of(j1) * HALF + pairs[0][0]
                    dve.wait_ge(scored, s + 2)
                    scores = score_bank[:].rearrange("p (i k) -> p i k", i=4)
                    out = masked_scores.rearrange("p (i k) -> p i k", i=4)
                    if causal is not None:
                        dve.tensor_tensor(out, scores, causal_add[:].unsqueeze(1).broadcast_to([128, 4, S]), ALU.add)\
                           .then_inc(biased, 1)
                        dve.wait_ge(biased, s + 2)
                        scores = out
                    if pad_mask is not None:
                        if j1 == 0:
                            dve.wait_ge(head_bias_loaded, 16 * (g + (j + 1) // UG + 1))
                        b4 = [128, BU, H, S]
                        dve.tensor_tensor(out.rearrange("p (b h) k -> p b h k", b=BU),
                                          scores.rearrange("p (b h) k -> p b h k", b=BU),
                                          head_bias[:].unsqueeze(1).broadcast_to(b4), ALU.add).then_inc(biased, 1)
                        wait_count(dve, biased, 2 * s + 3)
                        o4 = out.rearrange("p (b h) k -> p b h k", b=BU)
                        dve.tensor_tensor(o4, o4, pad_add[:, batch:batch + BU, :].unsqueeze(2).broadcast_to(b4),
                                          ALU.add).then_inc(biased, 1)
                        dve.wait_ge(biased, 2 * s + 4)
                        scores = out
                    dve.tensor_reduce(neg_max[:], scores, AX.X, ALU.max, negate=True).then_inc(row_max, 1)
                    if scale != 1.0:
                        dve.wait_ge(row_max, s + 2)
                        dve.tensor_scalar(exp_bias[:], neg_max[:], scale, None, ALU.mult).then_inc(bias_ready, 1)
                if unit_there(s - 1, fixed):
                    first = P.half_of((j - 1) % UG) * HALF + P.pairs((j - 1) % UG)[0][0]
                    for bi in range(BU):
                        bank = (j - 1 + bi) % 2 if BU == 1 else bi
                        dve.wait_ge(out_done, (s - 1) * BU + bi + 1)
                        xb = x[:, first + bi, :]
                        dve.tensor_tensor(xb, out_bank[:, bank, :], xb, ALU.add).then_inc(out_added, 1)
                if unit_there(s + 1, fixed):
                    dve.wait_ge(exped, s + 2)
                    dve.reciprocal(inv_sum[:], exp_sum[:]).then_inc(summed, 1)
                    if pad_mask is not None:
                        dve.wait_ge(summed, s + 2)
                        inv2 = inv_sum[:].rearrange("p (b h) -> p b h", b=BU)
                        dve.tensor_tensor(inv2, inv2, row_any[:, batch:batch + BU].unsqueeze(2)
                                          .broadcast_to([128, BU, H]), ALU.mult).then_inc(inv_ready, 1)
                    wait_count(dve, inv_ready, s + 2)
                    dve_probs = probs.rearrange("p (i k) -> p i k", i=4)
                    dve.tensor_tensor(dve_probs, dve_probs, inv_sum[:].unsqueeze(2).broadcast_to([128, 4, S]),
                                      ALU.mult).then_inc(probs_ready, 1)
                for kind, i, k, half, number, slot in turns_at(g, j, fixed):
                    dve.wait_ge(task_hi, number + 1)
                    dve.tensor_tensor(v_part(LO, slot, i), v_bank(k), as_f32(v_part(HI, slot, i)),
                                      ALU.subtract).then_inc(task_read, 1)
                if unit_there(s, fixed):
                    dve.wait_ge(outT_hi, s + 1)
                    dve.tensor_tensor(outT[:, LO, :], outT_bank[:], as_f32(outT[:, HI, :]), ALU.subtract)\
                       .then_inc(outT_ready, 1)
                for kind, i, k, half, number, slot in tasks_at(g, j, fixed):
                    bank = proj_bank[:, P.bank_of(k), :]
                    if kind in "qk" and rope is not None:
                        place = [n for n, t in enumerate(P.tasks) if t[0] != "v"].index(k)
                        count = P.qk_per_half * half + place
                        ring = (P.qk_per_half * slot + place) % 2
                        wait_count(dve, qk_ready, count - 1)
                        dve.wait_ge(projected, number + 1)

                        def four(ap):
                            return ap.rearrange("p (b t) -> p b t", b=HALF)
                        for a, z, out in ((0, 128, direct), (64, 128, crossed), (0, 64, crossed)):
                            to = (a, z) if out is direct else ((a + 64) % 128, (a + 64) % 128 + 64)
                            table = cosine if out is direct else sine
                            last = dve.tensor_tensor(four(out[to[0]:to[1], ring, :]), four(bank[a:z]),
                                                     table[a:z, :].unsqueeze(1).broadcast_to([z - a, HALF, S]),
                                                     ALU.mult)
                        last.then_inc(task_read, 1)
                        continue
                    if kind == "v":
                        continue
                    dve.wait_ge(task_hi, number + 1)
                    out = qT if kind == "q" else kT
                    if biases is not None:
                        dve.scalar_tensor_tensor(out[:, LO, slot, i, :], bank, columns[kind][:, i:i + 1],
                                                 as_f32(out[:, HI, slot, i, :]), ALU.add, ALU.subtract)\
                           .then_inc(task_read, 1)
                    else:
                        dve.tensor_tensor(out[:, LO, slot, i, :], bank, as_f32(out[:, HI, slot, i, :]),
                                          ALU.subtract).then_inc(task_read, 1)
            each_step(dve, P, step)
            if out_bias is not None:
                dve.wait_ge(out_added, P.units * BU)
                dve.wait_ge(out_bias_loaded, 16)
                for b in range(B):
                    dve.tensor_tensor(x[:, b, :], x[:, b, :], bias_o, ALU.add)

        @block.gpsimd
        def _(pool):
            def split_low(args, odd):
                kind, i, number, slot, of = args
                raw = as_f32(staged[:, slot, 0:D]) if codes else staged[:, slot, 0:D]
                wait_count(pool, chunk_hi, number + 1)
                pool.tensor_tensor(weight(kind, i, LO, odd), raw, as_f32(weight(kind, i, HI, odd)), ALU.subtract).then_inc(chunk_ready, 1)

            def split_all(chunks, odd):
                if codes:
                    for kind, i, number, slot, of in chunks:
                        wait_count(pool, converted, number + 1)
                        raw = as_f32(staged[:, slot, :])
                        pool.tensor_tensor(raw, raw, scales[:, slot, :], ALU.mult).then_inc(dequantized, 1)
                for args in chunks:
                    split_low(args, odd)

            split_all(list(first_splits()), 1)
            if source is not None:
                for n in range(CONTEXT_PIECES):
                    pool.wait_ge(context_hi, n + 1)
                    tok = slice((n % 2) * 512, (n % 2 + 1) * 512)
                    pool.tensor_tensor(kvT[:, LO, n // 2, tok], context_raw[:, n % 2, :],
                                       as_f32(kvT[:, HI, n // 2, tok]), ALU.subtract).then_inc(context_ready, 1)
            norm.gpsimd(pool)

            def step(g, j, fixed, odd):
                s = g * UG + j
                if rope is not None:
                    places = [n for n, t in enumerate(P.tasks) if t[0] != "v"]
                    mine = [t for t in tasks_at(g, j, fixed) if t[0] in "qk"]
                    for kind, i, k, half, number, slot in mine:
                        ring = (P.qk_per_half * slot + places.index(k)) % 2
                        pool.wait_ge(task_read, number + 1)
                        pool.tensor_tensor(direct[:, ring, :], direct[:, ring, :], crossed[:, ring, :], ALU.add)\
                            .then_inc(rotated, 1)
                split_all(list(splits_at(g, j, fixed)), odd)
                if rope is not None:
                    for kind, i, k, half, number, slot in mine:
                        ring = (P.qk_per_half * slot + places.index(k)) % 2
                        out = qT if kind == "q" else kT
                        pool.wait_ge(task_hi, number + 1)
                        pool.tensor_tensor(out[:, LO, slot, i, :], direct[:, ring, :],
                                           as_f32(out[:, HI, slot, i, :]), ALU.subtract).then_inc(qk_ready, 1)
            each_step(pool, P, step)


class Splitter:

    def __init__(self, sems, nc, name):
        self.pieces = []
        self.high_done = sems.new(f"{name}_weight_hi")
        self.ready = sems.new(f"{name}_weight_ready")

    def add(self, loaded, count, raw, high, low):
        self.pieces.append((loaded, count, raw, high, low))

    def scalar(self, act, first=0, end=None):
        for loaded, count, raw, high, _ in self.pieces[first:end]:
            act.wait_ge(loaded, count)
            act.activation(high, raw, ACT.Copy).then_inc(self.high_done, 1)

    def gpsimd(self, pool, first=0, end=None):
        for n, (_, _, raw, high, low) in list(enumerate(self.pieces))[first:end]:
            pool.wait_ge(self.high_done, n + 1)
            pool.tensor_tensor(low, raw, as_f32(high), ALU.subtract).then_inc(self.ready, 1)


def expert_layer(nc, sems, x, ident, gate_w, lora_a, lora_b):
    name, E = "moe", 8
    with ExitStack() as ctx:
        def sb(n, shape, dt=F32):
            return ctx.enter_context(nc.sbuf_tensor(f"{name}_{n}", shape, dt))

        def pb(n, shape):
            return ctx.enter_context(nc.psum_tensor(f"{name}_{n}", shape, F32))

        def sem(n):
            return sems.new(f"{name}_{n}")

        xT = sb("xT", [128, 2, KT, B * S], F32R)
        scratch = sb("scratch", [128, 2, D])
        gate_raw, gate = sb("gate_raw", [128, KT, E]), sb("gate", [128, 2, KT, E], F32R)
        a_raw, a = sb("a_raw", [128, KT, D]), sb("a", [128, 2, KT, D], F32R)
        b_raw, b_w = sb("b_raw", [128, KT, D]), sb("b_w", [128, 2, KT, D], F32R)
        rank_first = sb("rank_first", [128, B, E])
        shifted, prob = sb("shifted", [128, B, E]), sb("prob", [128, B, E])
        equal, key, rest = sb("equal", [128, B, E]), sb("key", [128, B, E]), sb("rest", [128, B, E])
        chosen = [sb("chosen0", [128, B, E]), sb("chosen1", [128, B, E])]
        expert_weight = sb("expert_weight", [128, B, E])
        best = [sb("best0", [128, B]), sb("best1", [128, B])]
        top, total, inverse, best_key = (sb(n, [128, B]) for n in ("top", "total", "inverse", "best_key"))
        hidden = sb("hidden", [128, 2, D])
        hiddenT = sb("hiddenT", [128, 2, 2, D], F32R)

        norm_bank = pb("norm_bank", [128, 2, 512])
        gate_bank = pb("gate_bank", [128, 512])
        hidden_bank = pb("hidden_bank", [128, 512])
        hiddenT_bank = pb("hiddenT_bank", [128, 512])
        y_bank = pb("y_bank", [128, 2, 512])

        norm = Norm(ctx, sems, nc, f"{name}_norm", x, xT, scratch, norm_bank, ident)
        split = Splitter(sems, nc, name)
        loaded = [sem(f"loaded{i}") for i in range(3)]
        split.add(loaded[0], 16, gate_raw[:], gate[:, HI], gate[:, LO])
        for k in range(KT):
            split.add(loaded[1], 16, a_raw[:, k, :], a[:, HI, k, :], a[:, LO, k, :])
        for k in range(KT):
            split.add(loaded[2], 16, b_raw[:, k, :], b_w[:, HI, k, :], b_w[:, LO, k, :])
        rank_set, gated, exped, small, weighted_ready = (sem(n) for n in (
            "rank_set", "gated", "exped", "small", "weighted_ready"))
        hidden_done, hidden_scaled, hidden_transposed = sem("hidden_done"), sem("hidden_scaled"), sem("hiddenT_done")
        hiddenT_hi, hiddenT_ready, y_done, y_added = (sem(n) for n in ("hiddenT_hi", "hiddenT_ready", "y_done", "y_added"))
        shifted_ready = sem("shifted_ready")
        block = ctx.enter_context(nc.Block())

        @block.sync
        def _(sp):
            sp.dma_start(gate_raw[:], gate_w).then_inc(loaded[0], 16)
            sp.dma_start(a_raw[:], lora_a).then_inc(loaded[1], 16)
            sp.dma_start(b_raw[:], lora_b).then_inc(loaded[2], 16)

        @block.gpsimd
        def _(pool):
            pool.iota(rank_first[:], pattern=[[0, B], [-1, E]], base=E, channel_multiplier=0,
                      allow_small_or_imprecise_dtypes=True).then_inc(rank_set, 1)
            split.gpsimd(pool)
            norm.gpsimd(pool)

        @block.scalar
        def _(act):
            split.scalar(act)
            norm.scalar(act)
            act.wait_ge(shifted_ready, 1)
            act.activation(prob[:], shifted[:], ACT.Exp).then_inc(exped, 1)
            for b in range(B):
                act.wait_ge(hidden_transposed, b + 1)
                act.activation(hiddenT[:, HI, b % 2, :], hiddenT_bank[:], ACT.Copy).then_inc(hiddenT_hi, 1)

        @block.tensor
        def _(pe):
            norm.tensor(pe)
            pe.wait_ge(split.ready, 1)
            pe.wait_ge(norm.ready, B)
            for b in range(B):
                tok = slice(b * S, (b + 1) * S)
                for k in range(KT):
                    last = matmul3(pe, gate_bank[:, b * E:(b + 1) * E], lambda p: xT[:, p, k, tok],
                                   lambda p: gate[:, p, k, :], k == 0, k == KT - 1)
            last.then_inc(gated, 1)
            pe.wait_ge(split.ready, 1 + 2 * KT)
            for b in range(B + 1):
                if b < B:
                    tok = slice(b * S, (b + 1) * S)
                    if b >= 1:
                        pe.wait_ge(hidden_scaled, b)
                    for k in range(KT):
                        last = matmul3(pe, hidden_bank[:], lambda p: xT[:, p, k, tok],
                                       lambda p: a[:, p, k, :], k == 0, k == KT - 1)
                    last.then_inc(hidden_done, 1)
                if b >= 1:
                    c = b - 1
                    pe.wait_ge(hiddenT_ready, c + 1)
                    if c >= 2:
                        pe.wait_ge(y_added, c - 1)
                    for k in range(KT):
                        last = matmul3(pe, y_bank[:, c % 2, :], lambda p: hiddenT[:, p, c % 2, k * 128:(k + 1) * 128],
                                       lambda p: b_w[:, p, k, :], k == 0, k == KT - 1)
                    last.then_inc(y_done, 1)
                if b < B:
                    pe.wait_ge(hidden_scaled, b + 1)
                    for k in range(KT):
                        last = pe.transpose(hiddenT_bank[:, k * 128:(k + 1) * 128],
                                            hidden[:, b % 2, k * 128:(k + 1) * 128], ident[:])
                    last.then_inc(hidden_transposed, 1)

        @block.vector
        def _(dve):
            norm.vector(dve)
            done = 0

            def chain(instruction):
                nonlocal done
                done += 1
                instruction.then_inc(small, 1)
                dve.wait_ge(small, done)

            def wide(ap):
                return ap[:].unsqueeze(2).broadcast_to([128, B, E])
            logits = gate_bank[:, 0:B * E].rearrange("p (b e) -> p b e", e=E)
            dve.wait_ge(gated, 1)
            chain(dve.tensor_reduce(top[:], logits, AX.X, ALU.max))
            dve.tensor_tensor(shifted[:], logits, wide(top), ALU.subtract).then_inc(shifted_ready, 1)
            dve.wait_ge(exped, 1)
            chain(dve.tensor_reduce(total[:], prob[:], AX.X, ALU.add))
            chain(dve.reciprocal(inverse[:], total[:]))
            chain(dve.tensor_tensor(prob[:], prob[:], wide(inverse), ALU.mult))
            dve.wait_ge(rank_set, 1)
            left = prob
            for n in range(2):
                chain(dve.tensor_reduce(best[n][:], left[:], AX.X, ALU.max))
                chain(dve.tensor_tensor(equal[:], left[:], wide(best[n]), ALU.is_equal))
                chain(dve.tensor_tensor(key[:], equal[:], rank_first[:], ALU.mult))
                chain(dve.tensor_reduce(best_key[:], key[:], AX.X, ALU.max))
                chain(dve.tensor_tensor(chosen[n][:], key[:], wide(best_key), ALU.is_equal))
                if n == 0:
                    chain(dve.scalar_tensor_tensor(rest[:], chosen[0][:], -2.0, prob[:], ALU.mult, ALU.add))
                    left = rest
            chain(dve.tensor_tensor(total[:], best[0][:], best[1][:], ALU.add))
            chain(dve.reciprocal(inverse[:], total[:]))
            for n in range(2):
                chain(dve.tensor_tensor(best[n][:], best[n][:], inverse[:], ALU.mult))
                chain(dve.tensor_tensor(chosen[n][:], chosen[n][:], wide(best[n]), ALU.mult))
            chain(dve.tensor_tensor(expert_weight[:], chosen[0][:], chosen[1][:], ALU.add))
            for b in range(B + 1):
                if b < B:
                    dve.wait_ge(hidden_done, b + 1)
                    if b >= 2:
                        dve.wait_ge(hidden_transposed, b - 1)
                    dve.tensor_tensor(hidden[:, b % 2, :].rearrange("p (e r) -> p e r", e=E),
                                      hidden_bank[:].rearrange("p (e r) -> p e r", e=E),
                                      expert_weight[:, b, :].unsqueeze(2).broadcast_to([128, E, D // E]),
                                      ALU.mult).then_inc(hidden_scaled, 1)
                    dve.wait_ge(hiddenT_hi, b + 1)
                    dve.tensor_tensor(hiddenT[:, LO, b % 2, :], hiddenT_bank[:], as_f32(hiddenT[:, HI, b % 2, :]),
                                      ALU.subtract).then_inc(hiddenT_ready, 1)
                if b >= 1:
                    dve.wait_ge(y_done, b)
                    dve.tensor_tensor(x[:, b - 1, :], y_bank[:, (b - 1) % 2, :], x[:, b - 1, :], ALU.add)\
                       .then_inc(y_added, 1)


def adapter_layer(nc, sems, x, ident, weight, bias, lora_a, lora_b, starts, out):
    name, N, R = "ffn", 3, 16
    with ExitStack() as ctx:
        def sb(n, shape, dt=F32):
            return ctx.enter_context(nc.sbuf_tensor(f"{name}_{n}", shape, dt))

        def pb(n, shape):
            return ctx.enter_context(nc.psum_tensor(f"{name}_{n}", shape, F32))

        def sem(n):
            return sems.new(f"{name}_{n}")

        n_starts = starts.shape[0]
        xT = sb("xT", [128, 2, KT, B * S], F32R)
        scratch = sb("scratch", [128, 2, D])
        w_raw, w = sb("w_raw", [128, KT, D]), sb("w", [128, 2, KT, D], F32R)
        a_raw, a = sb("a_raw", [128, KT, N * R]), sb("a", [128, 2, KT, N * R], F32R)
        b_w = sb("b_w", [N * R, D])
        bias_all = sb("bias_all", [128, D])
        starts_all = sb("starts_all", [128, n_starts], I32)
        starts_f = sb("starts_f", [128, n_starts])
        batch_number = sb("batch_number", [128, B, n_starts])
        begun = sb("begun", [128, B, n_starts])
        segment = sb("segment", [128, B])
        adapter_on = sb("adapter_on", [128, B, N])
        adapter_number = sb("adapter_number", [128, B, N])
        low = sb("low", [128, 2, N * R])
        lowT = sb("lowT", [N * R, 2, S])
        norm_bank = pb("norm_bank", [128, 2, 512])
        y_bank = pb("y_bank", [128, 2, 512])
        low_bank = pb("low_bank", [128, 2, 512])
        lowT_bank = pb("lowT_bank", [128, 2, 512])

        norm = Norm(ctx, sems, nc, f"{name}_norm", x, xT, scratch, norm_bank, ident)
        split = Splitter(sems, nc, name)
        loaded = [sem(f"loaded{i}") for i in range(2)]
        split.add(loaded[0], 16, a_raw[:], a[:, HI], a[:, LO])
        for k in range(KT):
            split.add(loaded[1], 16, w_raw[:, k, :], w[:, HI, k, :], w[:, LO, k, :])
        small_loaded, numbers_set, small = sem("small_loaded"), sem("numbers_set"), sem("small")
        low_done, low_scaled, low_transposed, lowT_ready = (sem(n) for n in (
            "low_done", "low_scaled", "low_transposed", "lowT_ready"))
        y_done, y_added, stored, biased = sem("y_done"), sem("y_added"), sem("stored"), sem("x_biased")
        block = ctx.enter_context(nc.Block())

        @block.sync
        def _(sp):
            sp.dma_start(starts_all[:], starts.partition_broadcast(128)).then_inc(small_loaded, 16)
            sp.dma_start(bias_all[:], bias.partition_broadcast(128)).then_inc(small_loaded, 16)
            sp.dma_start(b_w[:], lora_b).then_inc(small_loaded, 16)
            sp.dma_start(a_raw[:], lora_a).then_inc(loaded[0], 16)
            sp.dma_start(w_raw[:], weight).then_inc(loaded[1], 16)
            for b in range(B):
                sp.wait_ge(y_added, b + 1)
                sp.dma_start(out[b], x[:, b, :]).then_inc(stored, 16)
            sp.wait_ge(stored, 16 * B)

        @block.gpsimd
        def _(pool):
            pool.iota(batch_number[:], pattern=[[1, B], [0, n_starts]], base=0, channel_multiplier=0,
                      allow_small_or_imprecise_dtypes=True).then_inc(numbers_set, 1)
            pool.iota(adapter_number[:], pattern=[[0, B], [1, N]], base=2, channel_multiplier=0,
                      allow_small_or_imprecise_dtypes=True).then_inc(numbers_set, 1)
            norm.gpsimd(pool)
            split.gpsimd(pool)

        @block.scalar
        def _(act):
            split.scalar(act)
            norm.scalar(act)
            for b in range(B):
                act.wait_ge(low_transposed, b + 1)
                if b >= 2:
                    act.wait_ge(y_done, b - 1)
                act.activation(lowT[:, b % 2, :], lowT_bank[0:N * R, b % 2, 0:S], ACT.Copy).then_inc(lowT_ready, 1)

        @block.tensor
        def _(pe):
            norm.tensor(pe)
            pe.wait_ge(small_loaded, 48)
            pe.wait_ge(split.ready, 1 + KT)
            pe.wait_ge(norm.ready, B)

            def down(b):
                tok = slice(b * S, (b + 1) * S)
                for k in range(KT):
                    last = matmul3(pe, low_bank[:, b % 2, 0:N * R], lambda p: xT[:, p, k, tok],
                                   lambda p: a[:, p, k, :], k == 0, k == KT - 1)
                last.then_inc(low_done, 1)
            down(0)
            for b in range(B):
                tok = slice(b * S, (b + 1) * S)
                if b + 1 < B:
                    if b >= 1:
                        pe.wait_ge(low_scaled, b)
                    down(b + 1)
                pe.wait_ge(low_scaled, b + 1)
                if b >= 2:
                    pe.wait_ge(lowT_ready, b - 1)
                pe.transpose(lowT_bank[0:N * R, b % 2, 0:S], low[:, b % 2, :], ident[:]).then_inc(low_transposed, 1)
                if b >= 2:
                    pe.wait_ge(y_added, b - 1)
                for k in range(KT):
                    matmul3(pe, y_bank[:, b % 2, :], lambda p: xT[:, p, k, tok], lambda p: w[:, p, k, :], k == 0, False)
                pe.wait_ge(lowT_ready, b + 1)
                pe.matmul(y_bank[:, b % 2, :], lowT[:, b % 2, :], b_w[:], start=False, stop=True,
                          skip_group_check=True).then_inc(y_done, 1)

        @block.vector
        def _(dve):
            norm.vector(dve)
            dve.wait_ge(small_loaded, 48)
            dve.tensor_copy(starts_f[:], starts_all[:]).then_inc(small, 1)
            dve.wait_ge(small, 1)
            dve.wait_ge(numbers_set, 2)
            dve.tensor_tensor(begun[:], batch_number[:], starts_f[:].unsqueeze(1).broadcast_to([128, B, n_starts]),
                              ALU.is_ge).then_inc(small, 1)
            dve.wait_ge(small, 2)
            dve.tensor_reduce(segment[:], begun[:], AX.X, ALU.add).then_inc(small, 1)
            dve.wait_ge(small, 3)
            dve.tensor_tensor(adapter_on[:], segment[:].unsqueeze(2).broadcast_to([128, B, N]), adapter_number[:],
                              ALU.is_equal).then_inc(small, 1)
            dve.wait_ge(small, 4)
            for b in range(B):
                dve.tensor_tensor(x[:, b, :], x[:, b, :], bias_all[:], ALU.add).then_inc(biased, 1)

            def scale_low(b):
                dve.wait_ge(low_done, b + 1)
                if b >= 2:
                    dve.wait_ge(low_transposed, b - 1)
                dve.tensor_tensor(low[:, b % 2, :].rearrange("p (n r) -> p n r", n=N),
                                  low_bank[:, b % 2, 0:N * R].rearrange("p (n r) -> p n r", n=N),
                                  adapter_on[:, b, :].unsqueeze(2).broadcast_to([128, N, R]), ALU.mult)\
                   .then_inc(low_scaled, 1)
            scale_low(0)
            for b in range(B):
                if b + 1 < B:
                    scale_low(b + 1)
                dve.wait_ge(y_done, b + 1)
                dve.wait_ge(biased, b + 1)
                dve.tensor_tensor(x[:, b, :], y_bank[:, b % 2, :], x[:, b, :], ALU.add).then_inc(y_added, 1)


def small_attention(nc, sems, x, ident, w_q_dram, w_k_dram, w_v_dram, w_o_dram, rope_q, rope_k, causal, parities):
    name, T, HW, KV = "small", 4, 16, 8
    UNITS_OF_PAIR = 16
    BATCH_PAIRS = B // 2
    UNITS = UNITS_OF_PAIR * BATCH_PAIRS
    with ExitStack() as ctx:
        def sb(n, shape, dt=F32):
            return ctx.enter_context(nc.sbuf_tensor(f"{name}_{n}", shape, dt))

        def pb(n, shape):
            return ctx.enter_context(nc.psum_tensor(f"{name}_{n}", shape, F32))

        def sem(n):
            return sems.new(f"{name}_{n}")

        xT = sb("xT", [128, 2, KT, B * S], F32R)
        scratch = sb("scratch", [128, 2, D])
        probs = scratch
        masked_scores = sb("masked_scores", [128, 2, D])
        raw = sb("raw", [128, KT, D])
        k_raw, v_raw = sb("k_raw", [128, KT, 128]), sb("v_raw", [128, KT, 128])
        w_q = sb("w_q", [128, 2, 2, KT, T * 128], F32R)
        w_k = sb("w_k", [128, 2, 2, KT, 128], F32R)
        w_v = sb("w_v", [128, 2, KT, 128], F32R)
        w_o = sb("w_o", [128, 2, KT, D], F32R)
        qT = sb("qT", [128, 2, T, B * S], F32R)
        kT = sb("kT", [128, 2, 2, B * S], F32R)
        v_tok = sb("v_tok", [128, B, KV * HW])
        cos_q, sin_q, cos_k, sin_k = (sb(n, [128, S]) for n in ("cos_q", "sin_q", "cos_k", "sin_k"))
        causal_add, parity = sb("causal_add", [128, S]), sb("parity", [128, 2])
        direct, crossed = sb("direct", [128, TOK]), sb("crossed", [128, TOK])
        neg_max, exp_sum = sb("neg_max", [128, 2, 4]), sb("exp_sum", [128, 2, 2, NH])
        inv_sum = sb("inv_sum", [128, 2, NH])
        probsT = sb("probsT", [128, 2, 512])
        heads_out = sb("heads_out", [128, 2, D])
        heads_outT = sb("heads_outT", [128, 2, D], F32R)

        pair_banks = [pb("proj_bank", [128, 2, 512]), pb("score_bank", [128, 2, 512]), pb("probsT_bank", [128, 2, 512])]
        proj_bank, score_bank, probsT_bank = pair_banks
        out_bank = pb("out_bank", [128, 2, 512])

        norm = Norm(ctx, sems, nc, f"{name}_norm", x, xT, scratch, proj_bank, ident)
        split = Splitter(sems, nc, name)
        k_loaded, v_loaded, q_loaded, o_loaded, const_loaded = (sem(n) for n in (
            "k_loaded", "v_loaded", "q_loaded", "o_loaded", "const_loaded"))
        half = HW // 2

        def rows(ap):
            return ap.rearrange("p k (j s d) -> p k j s d", s=2, d=half)
        split.add(k_loaded, 16, k_raw[:], w_k[:, HI, 0], w_k[:, LO, 0])
        for s in range(2):
            split.add(k_loaded, 16, rows(k_raw[:])[:, :, :, 1 - s], rows(w_k[:, HI, 1])[:, :, :, s],
                      rows(w_k[:, LO, 1])[:, :, :, s])
        split.add(v_loaded, 16, v_raw[:], w_v[:, HI], w_v[:, LO])
        for k in range(KT):
            def tiles(ap):
                return ap.rearrange("p (t j d) -> p t j d", t=T, j=KV)
            source = raw[:, k, :].rearrange("p (j t d) -> p t j d", t=T, j=KV)
            split.add(q_loaded, 16, source, tiles(w_q[:, HI, 0, k]), tiles(w_q[:, LO, 0, k]))
            for s in range(2):
                part = slice(s * half, (s + 1) * half)
                other = slice((1 - s) * half, (2 - s) * half)
                split.add(q_loaded, 16, source[..., other], tiles(w_q[:, HI, 1, k])[..., part],
                          tiles(w_q[:, LO, 1, k])[..., part])
        N_EARLY = len(split.pieces)
        for k in range(KT):
            split.add(o_loaded, 16, raw[:, k, :], w_o[:, HI, k], w_o[:, LO, k])
        tasks = [("k", 0, h) for h in range(2)] + [("q", t, h) for h in range(2) for t in range(T)]
        projected, products, rotated, part_hi, part_ready = (sem(n) for n in (
            "projected", "products", "rotated", "part_hi", "part_ready"))
        v_done, v_ready = sem("v_done"), sem("v_ready")
        scored, biased, maxed, exped, transposed, probsT_ready, attended = (sem(n) for n in (
            "scored", "biased", "maxed", "exped", "transposed", "probsT_ready", "attended"))
        inverted, out_scaled, outT_done, outT_hi, outT_ready, y_done, y_added = (sem(n) for n in (
            "inverted", "out_scaled", "outT_done", "outT_hi", "outT_ready", "y_done", "y_added"))
        block = ctx.enter_context(nc.Block())

        def unit(u):
            return u // UNITS_OF_PAIR, u // 4 % 4, u % 4

        def head(t, group, par):
            return 4 * (2 * group + par) + t

        def steps(step, finish):
            for u in range(-2, UNITS + 1):
                step(u)
                if u > 0 and u % UNITS_OF_PAIR == 0:
                    finish(u // UNITS_OF_PAIR - 1)

        @block.sync
        def _(sp):
            sp.dma_start(k_raw[:], w_k_dram).then_inc(k_loaded, 16)
            sp.dma_start(v_raw[:], w_v_dram).then_inc(v_loaded, 16)
            sp.dma_start(raw[:], w_q_dram).then_inc(q_loaded, 16)
            for to, of in ((cos_q, rope_q[0]), (sin_q, rope_q[1]), (cos_k, rope_k[0]), (sin_k, rope_k[1]),
                           (causal_add, causal), (parity, parities)):
                sp.dma_start(to[:], of).then_inc(const_loaded, 16)
            sp.wait_ge(split.ready, N_EARLY)
            sp.dma_start(raw[:], w_o_dram).then_inc(o_loaded, 16)

        @block.tensor
        def _(pe):
            norm.tensor(pe)
            pe.wait_ge(norm.ready, B)
            pe.wait_ge(split.ready, N_EARLY)
            for b in range(B):
                for k in range(KT):
                    last = matmul3(pe, out_bank[:, b // HALF, (b % HALF) * 128:(b % HALF + 1) * 128],
                                   lambda p: xT[:, p, k, b * S:(b + 1) * S], lambda p: w_v[:, p, k, :],
                                   k == 0, k == KT - 1)
            last.then_inc(v_done, 1)
            for n, (kind, t, h) in enumerate(tasks):
                if n >= 3:
                    pe.wait_ge(products, n - 2)
                for swapped in range(2):
                    for k in range(KT):
                        last = matmul3(pe, pair_banks[n % 3][:, swapped, :],
                                       (lambda p: w_k[:, p, swapped, k, :]) if kind == "k" else
                                       (lambda p: w_q[:, p, swapped, k, t * 128:(t + 1) * 128]),
                                       lambda p: xT[:, p, k, h * TOK:(h + 1) * TOK], k == 0, k == KT - 1)
                last.then_inc(projected, 1)
            pe.wait_ge(v_ready, 2)
            pe.wait_ge(part_ready, len(tasks))

            def step(u):
                if u + 2 < UNITS:
                    pair, t, group = unit(u + 2)
                    rows32 = slice(32 * group, 32 * group + 32)
                    wait_count(pe, biased, u + 1)
                    for bi in range(2):
                        tok = slice((2 * pair + bi) * S, (2 * pair + bi + 1) * S)
                        last = matmul3(pe, score_bank[:, u % 2, bi * 256:(bi + 1) * 256],
                                       lambda p: qT[rows32, p, t, tok], lambda p: kT[rows32, p, :, tok], True, True)
                    last.then_inc(scored, 1)
                if 0 <= u < UNITS:
                    pe.wait_ge(exped, u + 1)
                    wait_count(pe, probsT_ready, u - 1)
                    for i in range(4):
                        last = pe.transpose(probsT_bank[:, u % 2, i * S:(i + 1) * S],
                                            probs[:, u % 2, i * S:(i + 1) * S], ident[:])
                    last.then_inc(transposed, 1)
                v = u - 1
                if 0 <= v:
                    pair, t, group = unit(v)
                    pe.wait_ge(probsT_ready, v + 1)
                    if v % UNITS_OF_PAIR == 0:
                        wait_count(pe, out_scaled, 2 * pair)
                    for i in range(4):
                        bi, par = i // 2, i % 2
                        h, kv = head(t, group, par), 2 * group + par
                        last = pe.matmul(out_bank[:, bi, h * HW:(h + 1) * HW], probsT[:, v % 2, i * S:(i + 1) * S],
                                         v_tok[:, 2 * pair + bi, kv * HW:(kv + 1) * HW], start=True, stop=True)
                    last.then_inc(attended, 1)

            def finish(pair):
                for bi in range(2):
                    n = 2 * pair + bi
                    pe.wait_ge(out_scaled, n + 1)
                    for k in range(KT):
                        last = pe.transpose(proj_bank[:, 0, k * 128:(k + 1) * 128],
                                            heads_out[:, bi, k * 128:(k + 1) * 128], ident[:])
                    last.then_inc(outT_done, 1)
                    pe.wait_ge(outT_ready, n + 1)
                    wait_count(pe, y_added, n)
                    pe.wait_ge(split.ready, N_EARLY + KT)
                    for k in range(KT):
                        last = matmul3(pe, proj_bank[:, 1, :], lambda p: heads_outT[:, p, k * 128:(k + 1) * 128],
                                       lambda p: w_o[:, p, k, :], k == 0, k == KT - 1)
                    last.then_inc(y_done, 1)
            steps(step, finish)

        @block.scalar
        def _(act):
            split.scalar(act, 0, N_EARLY)
            norm.scalar(act)
            act.wait_ge(const_loaded, 16 * 6)
            for n, (kind, t, h) in enumerate(tasks):
                tok = slice(h * TOK, (h + 1) * TOK)
                act.wait_ge(rotated, n + 1)
                if kind == "q":
                    last = act.activation(qT[:, HI, t, tok], direct[:], ACT.Copy)
                else:
                    for par in range(2):
                        last = act.activation(kT[:, HI, par, tok], direct[:], ACT.Copy, scale=parity[:, par:par + 1])
                last.then_inc(part_hi, 1)
                if n == 1:
                    act.wait_ge(v_done, 1)
                    for i in range(2):
                        act.activation(v_tok[:, i * HALF:(i + 1) * HALF, :],
                                       out_bank[:, i, :].rearrange("p (b n) -> p b n", b=HALF), ACT.Copy)\
                           .then_inc(v_ready, 1)
            split.scalar(act, N_EARLY)

            def step(u):
                if u + 2 < UNITS:
                    pair, t, group = unit(u + 2)
                    act.wait_ge(maxed, u + 3)
                    wait_count(act, transposed, u + 1)
                    for i in range(4):
                        h = head(t, group, i % 2)
                        last = act.activation(probs[:, u % 2, i * S:(i + 1) * S],
                                              masked_scores[:, u % 2, i * S:(i + 1) * S], ACT.Exp,
                                              bias=neg_max[:, u % 2, i:i + 1],
                                              accum_out=exp_sum[:, pair % 2, i // 2, h:h + 1])
                    last.then_inc(exped, 1)

            def finish(pair):
                for bi in range(2):
                    act.wait_ge(outT_done, 2 * pair + bi + 1)
                    act.activation(heads_outT[:, HI, :], proj_bank[:, 0, :], ACT.Copy).then_inc(outT_hi, 1)
            steps(step, finish)

        @block.vector
        def _(dve):
            norm.vector(dve)
            dve.wait_ge(const_loaded, 16 * 6)

            def four(ap):
                return ap.rearrange("p (b t) -> p b t", b=HALF)

            def table(ap):
                return ap[:].unsqueeze(1).broadcast_to([128, HALF, S])
            for n, (kind, t, h) in enumerate(tasks):
                cos, sin = (cos_q, sin_q) if kind == "q" else (cos_k, sin_k)
                dve.wait_ge(projected, n + 1)
                wait_count(dve, part_ready, n)
                dve.tensor_tensor(four(direct[:]), four(pair_banks[n % 3][:, 0, :]), table(cos), ALU.mult)
                dve.tensor_tensor(four(crossed[:]), four(pair_banks[n % 3][:, 1, :]), table(sin), ALU.mult)\
                   .then_inc(products, 1)
                tok = slice(h * TOK, (h + 1) * TOK)
                dve.wait_ge(part_hi, n + 1)
                if kind == "q":
                    dve.tensor_tensor(qT[:, LO, t, tok], direct[:], as_f32(qT[:, HI, t, tok]), ALU.subtract)\
                       .then_inc(part_ready, 1)
                else:
                    for par in range(2):
                        last = dve.scalar_tensor_tensor(kT[:, LO, par, tok], direct[:], parity[:, par:par + 1],
                                                        as_f32(kT[:, HI, par, tok]), ALU.mult, ALU.subtract)
                    last.then_inc(part_ready, 1)

            def step(u):
                if u + 2 < UNITS:
                    dve.wait_ge(scored, u + 3)
                    wait_count(dve, exped, u + 1)
                    scores = score_bank[:, u % 2, :].rearrange("p (i k) -> p i k", i=4)
                    out = masked_scores[:, u % 2, :].rearrange("p (i k) -> p i k", i=4)
                    dve.tensor_tensor(out, scores, causal_add[:].unsqueeze(1).broadcast_to([128, 4, S]), ALU.add)\
                       .then_inc(biased, 1)
                    dve.wait_ge(biased, u + 3)
                    dve.tensor_reduce(neg_max[:, u % 2, :], out, AX.X, ALU.max, negate=True).then_inc(maxed, 1)
                if 0 <= u < UNITS:
                    dve.wait_ge(transposed, u + 1)
                    wait_count(dve, attended, u - 1)
                    dve.tensor_copy(probsT[:, u % 2, :], probsT_bank[:, u % 2, :]).then_inc(probsT_ready, 1)

            def finish(pair):
                dve.wait_ge(attended, UNITS_OF_PAIR * (pair + 1))
                dve.reciprocal(inv_sum[:], exp_sum[:, pair % 2]).then_inc(inverted, 1)
                dve.wait_ge(inverted, pair + 1)
                for bi in range(2):
                    wait_count(dve, outT_done, 2 * pair + bi - 1)
                    dve.tensor_tensor(heads_out[:, bi, :].rearrange("p (h d) -> p h d", h=NH),
                                      out_bank[:, bi, :].rearrange("p (h d) -> p h d", h=NH),
                                      inv_sum[:, bi, :].unsqueeze(2).broadcast_to([128, NH, HW]), ALU.mult)\
                       .then_inc(out_scaled, 1)
                for bi in range(2):
                    n = 2 * pair + bi
                    dve.wait_ge(outT_hi, n + 1)
                    dve.tensor_tensor(heads_outT[:, LO, :], proj_bank[:, 0, :], as_f32(heads_outT[:, HI, :]),
                                      ALU.subtract).then_inc(outT_ready, 1)
                    dve.wait_ge(y_done, n + 1)
                    dve.tensor_tensor(x[:, n, :], proj_bank[:, 1, :], x[:, n, :], ALU.add).then_inc(y_added, 1)
            steps(step, finish)

        @block.gpsimd
        def _(pool):
            norm.gpsimd(pool)
            split.gpsimd(pool, 0, N_EARLY)
            for n in range(len(tasks)):
                pool.wait_ge(products, n + 1)
                pool.tensor_tensor(direct[:], direct[:], crossed[:], ALU.add).then_inc(rotated, 1)
            split.gpsimd(pool, N_EARLY)


def decoder(nc, a, out):
    with ExitStack() as ctx:
        x = ctx.enter_context(nc.sbuf_tensor("x_stream", [128, B, D], F32))
        ident = ctx.enter_context(nc.sbuf_tensor("ident", [128, 128], F32))
        ident_loaded = ctx.enter_context(nc.semaphore("ident_loaded"))
        sems = Semaphores(nc)
        with nc.Block() as block:
            @block.sync
            def _(sp):
                sp.dma_start(ident[:], a["ident"]).then_inc(ident_loaded, 16)
                sp.wait_ge(ident_loaded, 16)
        attention(nc, sems, "a0", Plan(shared_kv=True), x, ident,
                  {"q": a["q0"], "k": a["k0"], "v": a["v0"], "o": a["o0"], "q_scales": a["q0_scales"],
                   "k_scales": a["k0_scales"], "v_scales": a["v0_scales"], "o_scales": a["o0_scales"]},
                  None, rope=(a["cos0"], a["sin0"]), causal=a["causal"], codes=True, scale=HD ** -0.5,
                  x_dram=a["x"])
        sems.clear()
        attention(nc, sems, "c0", Plan(shared_kv=False), x, ident,
                  {"q": a["cq0"], "k": a["ck0"], "v": a["cv0"], "o": a["co0"]}, a["context"],
                  pad_mask=a["mask"], position_bias=a["position_bias"], rms_weight=a["ln_weight"])
        sems.clear()
        expert_layer(nc, sems, x, ident, a["gate"], a["moe_a"], a["moe_b"])
        sems.clear()
        small_attention(nc, sems, x, ident, a["q1"], a["k1"], a["v1"], a["o1"], (a["cos1q"], a["sin1q"]),
                        (a["cos1k"], a["sin1k"]), a["causal"], a["parities"])
        sems.clear()
        attention(nc, sems, "c1", Plan(shared_kv=True), x, ident,
                  {"q": a["cq1"], "k": a["ck1"], "v": a["cv1"], "o": a["co1"]}, a["context"],
                  out_bias=a["bo1"], scale=HD ** -0.5)
        sems.clear()
        adapter_layer(nc, sems, x, ident, a["ffn_w"], a["ffn_bias"], a["ffn_a"], a["ffn_b"], a["starts"], out)


def _tables(np):
    f = np.float32
    pos = np.arange(S, dtype=f)
    inv = (f(1.0) / f(10000.0) ** (np.arange(0, HD, 2, dtype=f) / f(HD))).astype(f)
    angle = inv[:, None] * pos[None, :]
    cos0 = np.concatenate([np.cos(angle), np.cos(angle)]).astype(f)
    sin0 = np.concatenate([np.sin(angle), -np.sin(angle)]).astype(f)
    width = 16
    idx = np.arange(0, width, 2, dtype=f) / f(width)
    freq = (f(1.0 / (2.0 * np.pi)) * f(500000.0) ** (-idx)).astype(f)
    low, high, length, factor = 1.0, 4.0, 1024, 32.0
    scaled = np.where(freq < low / length, freq / f(factor), freq)
    smooth = np.clip((f(length) * freq - f(low)) / f(high - low), 0.0, 1.0).astype(f)
    mixed = (f(1.0) - smooth) * (freq / f(factor)) + smooth * freq
    freq = np.where((freq >= low / length) & (freq <= high / length), mixed, scaled).astype(f)
    phase = (f(2.0 * np.pi) * pos[:, None] * freq[None, :]).astype(f).T
    cos1 = np.tile(np.concatenate([np.cos(phase), np.cos(phase)]), (8, 1)).astype(f)
    sin1 = np.tile(np.concatenate([-np.sin(phase), np.sin(phase)]), (8, 1)).astype(f)
    causal = np.where(np.tril(np.ones((S, S), bool)), 0.0, MASKED).astype(f)
    kv = np.arange(128) // width
    parities = np.stack([kv % 2 == 0, kv % 2 == 1], axis=1).astype(f)
    quarter = f(width ** -0.5)
    return {"cos0": cos0, "sin0": sin0, "cos1q": cos1 * quarter, "sin1q": sin1 * quarter, "cos1k": cos1,
            "sin1k": sin1, "causal": causal, "ident": np.eye(128, dtype=f), "parities": parities}


def _layout(np, t):
    c = np.ascontiguousarray

    def chunks(w, heads):
        return c(w.reshape(KT, 128, heads, HD).transpose(2, 1, 0, 3).reshape(heads, 128, KT * HD))

    def rotary(w, heads):
        return w.reshape(w.shape[0], heads, HD // 2, 2).transpose(0, 1, 3, 2).reshape(w.shape[0], heads * HD)

    def scale_rows(s, heads):
        return c(s.reshape(KT, heads, HD).transpose(1, 0, 2).reshape(heads, KT * HD))

    def whole(w):
        return c(w.reshape(-1, 128, w.shape[1]).transpose(1, 0, 2))

    def with_bias(w, bias):
        return c(np.concatenate([w, bias.reshape(w.shape[0], 128, 1)], axis=2))
    wkv, bkv = t["L1_xattn_Wkv"], t["L1_xattn_bkv"]
    kv = wkv.shape[1] // 2
    context = t["ctx_4096"].transpose(2, 0, 1).reshape(KT, 128, 2, TOK)
    return {
        "x": c(t["x"]),
        "context": c(context.transpose(0, 2, 1, 3).reshape(KT * 2, 128, TOK)),
        "mask": c(t["mask_BxSxS2_bk0"].transpose(1, 0, 2)),
        "q0": chunks(rotary(t["L0_attn_q_codes"], NH), NH), "k0": chunks(rotary(t["L0_attn_k_codes"], 8), 8),
        "v0": chunks(t["L0_attn_v_codes"], 8), "o0": c(t["L0_attn_o_codes"].reshape(NH, 128, D)),
        "q0_scales": scale_rows(rotary(t["L0_attn_q_scales"], NH), NH),
        "k0_scales": scale_rows(rotary(t["L0_attn_k_scales"], 8), 8),
        "v0_scales": scale_rows(t["L0_attn_v_scales"], 8), "o0_scales": c(t["L0_attn_o_scales"]),
        "position_bias": c(t["L0_xattn_position_bias"]),
        "ln_weight": c(t["L0_xattn_ln_weight"].reshape(KT, 128).T),
        "cq0": chunks(t["L0_xattn_w_q"].T, NH), "ck0": chunks(t["L0_xattn_w_k"].T, NH),
        "cv0": chunks(t["L0_xattn_w_v"].T, NH), "co0": c(t["L0_xattn_w_out"].T.reshape(NH, 128, D)),
        "gate": whole(t["L0_ffn_gate_w"].T), "moe_a": whole(t["L0_ffn_lora_A"].reshape(-1, D).T),
        "moe_b": whole(t["L0_ffn_lora_B"].transpose(0, 2, 1).reshape(-1, D)),
        "q1": whole(t["L1_attn_Wq"]), "k1": whole(t["L1_attn_Wk"]), "v1": whole(t["L1_attn_Wv"]),
        "o1": whole(t["L1_attn_Wo"]),
        "cq1": with_bias(chunks(t["L1_xattn_Wq"], NH), t["L1_xattn_bq"]),
        "ck1": with_bias(chunks(wkv[:, :kv], 8), bkv[:kv]), "cv1": with_bias(chunks(wkv[:, kv:], 8), bkv[kv:]),
        "co1": c(t["L1_xattn_Wo"].reshape(NH, 128, D)),
        "bo1": c(t["L1_xattn_bo"]),
        "ffn_w": whole(t["L1_ffn_weight"].T), "ffn_bias": c(t["L1_ffn_bias"]),
        "ffn_a": whole(t["L1_ffn_lora_A"].reshape(-1, D).T),
        "ffn_b": c(t["L1_ffn_lora_B"].transpose(0, 2, 1).reshape(-1, D)),
        "starts": c(t["L1_ffn_lora_start_indices"]),
    }


def kernel(**inputs):
    import numpy as _np
    import concourse.bacc as _bacc
    from concourse import mybir as _mybir
    from concourse.bass_utils import run_bass_kernel_spmd as _run

    arrays = _layout(_np, {name: _np.asarray(v) for name, v in inputs.items()})
    arrays.update(_tables(_np))
    nc = _bacc.Bacc("TRN2", target_bir_lowering=False, num_devices=1)
    handles = {name: nc.dram_tensor(f"in_{name}", v.shape, _mybir.dt.from_np(v.dtype), kind="ExternalInput").ap()
               for name, v in arrays.items()}
    out = nc.dram_tensor("out_x", (B, S, D), _mybir.dt.float32, kind="ExternalOutput").ap()
    decoder(nc, handles, out)
    r = _run(nc, [{f"in_{name}": v for name, v in arrays.items()}], core_ids=[0])
    return r.results[0]["out_x"]
```

```python
from contextlib import ExitStack

import numpy as np

import concourse.bass as bass
from concourse import mybir

F32 = mybir.dt.float32
F32R = mybir.dt.float32r
I32 = mybir.dt.int32
U8 = mybir.dt.uint8
ALU = mybir.AluOpType
ACT = mybir.ActivationFunctionType
AX = mybir.AxisListType

B = 8
S = 128
D = 512
KT = D // 128
NH = 32
HD = 128
HALF = 4
TOK = HALF * S
EPS = 1e-5
MASKED = -1e30
HI, LO = 0, 1


def matmul3(pe, out, stationary, moving, first, last):
    pe.matmul(out, stationary(HI), moving(HI), start=first, stop=False, skip_group_check=True)
    pe.matmul(out, stationary(HI), moving(LO), start=False, stop=False, skip_group_check=True)
    return pe.matmul(out, stationary(LO), moving(HI), start=False, stop=last, skip_group_check=True)


def wait_count(eng, sem, count):
    if isinstance(count, int) and count <= 0:
        return
    eng.wait_ge(sem, count)


class Semaphores:

    def __init__(self, nc):
        self.nc, self.handles = nc, []

    def new(self, name):
        self.handles.append(self.nc.alloc_semaphore(name=name))
        return self.handles[-1]

    def clear(self):
        self.nc.clear_and_free_semaphores(self.handles)
        self.handles = []
        self.nc.all_engine_barrier()


def as_f32(ap):
    return ap.bitcast(F32)


class Norm:

    def __init__(self, ctx, sems, nc, name, x, xT, scratch, banks, ident, rms_weight=None, rms_loaded=None):
        self.nc, self.x, self.xT, self.scratch, self.banks, self.ident = nc, x, xT, scratch, banks, ident
        self.rms_weight, self.rms_loaded = rms_weight, rms_loaded
        self.factors = 1 if rms_weight is None else 2

        def small(n, shape):
            return ctx.enter_context(nc.sbuf_tensor(f"{name}_{n}", shape, F32))

        def sem(n):
            return sems.new(f"{name}_{n}")

        self.stats = small("stats", [128, B, 6])
        self.mean_var = small("mean_var", [128, B, 2])
        self.radicand = small("radicand", [128, self.factors, B])
        self.minus_half = small("minus_half", [128, self.factors, B])
        self.factor = small("factor", [128, self.factors, B])
        if rms_weight is not None:
            self.one_plus = small("one_plus", [128, B])
            self.mean_rstd = small("mean_rstd", [128, B])
            self.update_ready = sem("update_ready")
        self.stats_ready = sem("stats_ready")
        self.moments_ready = sem("moments_ready")
        self.var_ready = sem("var_ready")
        self.radicand_ready = sem("radicand_ready") if rms_weight is not None else self.var_ready
        self.half_set = sem("half_set")
        self.factor_ready = sem("factor_ready")
        self.normed = sem("normed")
        self.transposed = sem("transposed")
        self.hi_ready = sem("xt_hi_ready")
        self.ready = sem("xt_ready")

    def statistics(self, dve, x_ready=None):
        for h in range(2):
            some = slice(h * HALF, (h + 1) * HALF)
            if x_ready is not None:
                dve.wait_ge(x_ready[h], 16)
            for b in range(h * HALF, (h + 1) * HALF):
                dve.bn_stats(self.stats[:, b, :], self.x[:, b, :]).then_inc(self.stats_ready, 1)
            for b in range(h * HALF, (h + 1) * HALF):
                dve.wait_ge(self.stats_ready, b + 1)
                last = dve.bn_aggr(self.mean_var[:, b, :], self.stats[:, b, :])
            last.then_inc(self.moments_ready, 1)
            dve.wait_ge(self.moments_ready, h + 1)
            var, var_eps = self.mean_var[:, some, 1], self.radicand[:, 0, some]
            dve.tensor_scalar(var_eps, var, EPS, None, ALU.add).then_inc(self.var_ready, 1)
            if self.rms_weight is not None:
                dve.wait_ge(self.var_ready, h + 1)
                dve.scalar_tensor_tensor(self.radicand[:, 1, some], var_eps, EPS, var, ALU.mult, ALU.add)\
                   .then_inc(self.radicand_ready, 1)

    def vector(self, dve):
        if self.rms_weight is not None:
            dve.wait_ge(self.rms_loaded, 16)
        for b in range(B + 1):
            if b < B:
                if b % HALF == 0:
                    dve.wait_ge(self.factor_ready, b // HALF + 1)
                if b >= 2:
                    dve.wait_ge(self.transposed, b - 1)
                dve.tensor_scalar(self.scratch[:, b % 2, :], self.x[:, b, :], self.mean_var[:, b, 0:1],
                                  self.factor[:, self.factors - 1, b:b + 1], ALU.subtract, ALU.mult)\
                   .then_inc(self.normed, 1)
            if b >= 1:
                self.vector_low(dve, b - 1)

    def vector_low(self, dve, b):
        bank = self.banks[:, b % 2, :].rearrange("p (k t) -> p k t", k=KT)
        tokens = slice(b * S, (b + 1) * S)
        dve.wait_ge(self.hi_ready, b + 1)
        if self.rms_weight is None:
            dve.tensor_tensor(self.xT[:, LO, :, tokens], bank, as_f32(self.xT[:, HI, :, tokens]), ALU.subtract)\
               .then_inc(self.ready, 1)
        else:
            for k in range(KT):
                last = dve.scalar_tensor_tensor(self.xT[:, LO, k, tokens], bank[:, k, :],
                                                self.rms_weight[:, k:k + 1],
                                                as_f32(self.xT[:, HI, k, tokens]), ALU.mult, ALU.subtract)
            last.then_inc(self.ready, 1)

    def update_x(self, dve):
        rstd = self.factor[:, 0, :]
        dve.tensor_scalar(self.one_plus[:], rstd, 1.0, None, ALU.add)
        dve.tensor_tensor(self.mean_rstd[:], self.mean_var[:, :, 0], rstd, ALU.mult).then_inc(self.update_ready, 1)
        dve.wait_ge(self.update_ready, 1)
        for b in range(B):
            last = dve.tensor_scalar(self.x[:, b, :], self.x[:, b, :], self.one_plus[:, b:b + 1],
                                     self.mean_rstd[:, b:b + 1], ALU.mult, ALU.subtract)
        last.then_inc(self.update_ready, 1)
        dve.wait_ge(self.update_ready, 2)

    def gpsimd(self, pool):
        pool.memset(self.minus_half[:], -0.5).then_inc(self.half_set, 1)
        pool.wait_ge(self.half_set, 1)
        for h in range(2):
            some = slice(h * HALF, (h + 1) * HALF)
            pool.wait_ge(self.radicand_ready, h + 1)
            pool.tensor_tensor(self.factor[:, :, some], self.radicand[:, :, some], self.minus_half[:, :, some],
                               ALU.pow).then_inc(self.factor_ready, 1)

    def tensor(self, pe, batches=range(B)):
        for b in batches:
            pe.wait_ge(self.normed, b + 1)
            if b >= 2:
                pe.wait_ge(self.ready, b - 1)
            for k in range(KT):
                last = pe.transpose(self.banks[:, b % 2, k * 128:(k + 1) * 128],
                                    self.scratch[:, b % 2, k * 128:(k + 1) * 128], self.ident[:])
            last.then_inc(self.transposed, 1)

    def scalar(self, act, batches=range(B)):
        if self.rms_weight is not None and batches[0] == 0:
            act.wait_ge(self.rms_loaded, 16)
        for b in batches:
            act.wait_ge(self.transposed, b + 1)
            bank = self.banks[:, b % 2, :].rearrange("p (k t) -> p k t", k=KT)
            tokens = slice(b * S, (b + 1) * S)
            if self.rms_weight is None:
                act.activation(self.xT[:, HI, :, tokens], bank, ACT.Copy).then_inc(self.hi_ready, 1)
            else:
                for k in range(KT):
                    last = act.activation(self.xT[:, HI, k, tokens], bank[:, k, :], ACT.Copy,
                                          scale=self.rms_weight[:, k:k + 1])
                last.then_inc(self.hi_ready, 1)


class Plan:

    PER_HALF = 6

    def __init__(self, shared_kv):
        self.shared_kv = shared_kv
        if shared_kv:
            self.heads, self.kv_heads, self.unit_batches = 4, 1, 1
            self.tasks = [("q", 0), ("k", 0), ("q", 1), ("q", 2), ("q", 3), ("v", 0)]
            self.phases = [[0, 1], [2, 3], [4], [5]]
            self.splits = {1: [("q", 0), ("k", 0)], 2: [("q", 1)], 3: [("q", 2)], 4: [("q", 3), ("v", 0)],
                           5: [("o", 0)], 6: [("o", 1), ("o", 2)], 7: [("o", 3)]}
        else:
            self.heads, self.kv_heads, self.unit_batches = 2, 2, 2
            self.tasks = [("q", 0), ("k", 0), ("q", 1), ("k", 1), ("v", 0), ("v", 1)]
            self.phases = [[0, 1, 2], [3, 4, 5]]
            self.splits = {0: [("q", 0), ("k", 0), ("q", 1)], 1: [("k", 1), ("v", 0), ("v", 1)],
                           2: [("o", 0)], 3: [("o", 1)]}
        self.groups = NH // self.heads
        self.half_units = HALF // self.unit_batches
        self.group_units = 2 * self.half_units
        self.units = self.groups * self.group_units
        self.order = [c for j in sorted(self.splits) for c in self.splits[j]]
        self.chunks = len(self.order)
        self.slots = self.chunks // 2
        self.first_step = self.group_units - self.half_units - 1
        self.qk_per_half = sum(kind != "v" for kind, _ in self.tasks)

    def chunk_number(self, chunk, cycle):
        return self.chunks * (cycle + 1) + self.order.index(chunk)

    def chunk_slot(self, chunk):
        return self.order.index(chunk) % self.slots

    def pairs(self, j):
        first = (j % self.half_units) * self.unit_batches
        if self.shared_kv:
            return [(first, h) for h in range(self.heads)]
        return [(first + b, h) for b in range(self.unit_batches) for h in range(self.heads)]

    def half_of(self, j):
        return (j // self.half_units) % 2

    def target(self, j):
        return (j + 1) // self.half_units + 1, self.phases[(j + 1) % self.half_units]

    def bank_of(self, task):
        return task % 3


def each_step(eng, plan, step):
    for j in range(plan.first_step, plan.group_units):
        step(-1, j, True, 1)
    for j in range(plan.group_units):
        step(0, j, True, 0)
    with eng.Fori(0, plan.groups // 2 - 1) as turn:
        for odd in (1, 0):
            for j in range(plan.group_units):
                step(turn * 2 + (2 - odd), j, False, odd)
    for j in range(plan.group_units):
        step(plan.groups - 1, j, True, (plan.groups - 1) % 2)
    step(plan.groups, 0, True, plan.groups % 2)


def attention(nc, sems, name, plan, x, ident, weights, source, rope=None, causal=None, pad_mask=None,
              position_bias=None, rms_weight=None, codes=False, out_bias=None,
              scale=1.0, x_dram=None):
    P = plan
    H, NK, BU, UG, UH = P.heads, P.kv_heads, P.unit_batches, P.group_units, P.half_units
    biases = out_bias
    masked = causal is not None or pad_mask is not None
    with ExitStack() as ctx:
        def sb(n, shape, dt=F32):
            return ctx.enter_context(nc.sbuf_tensor(f"{name}_{n}", shape, dt))

        def pb(n, shape):
            return ctx.enter_context(nc.psum_tensor(f"{name}_{n}", shape, F32))

        def sem(n):
            return sems.new(f"{name}_{n}")

        xT = sb("xT", [128, 2, KT, B * S], F32R)
        scratch = sb("scratch", [128, 2, D])
        probs = scratch[:, 0, :]
        masked_scores = scratch[:, 1, :]
        w_q = sb("w_q", [128, 2, H, D], F32R)
        w_k = sb("w_k", [128, 2, NK, D], F32R)
        w_v = sb("w_v", [128, 2, NK, D], F32R)
        w_o = sb("w_o", [128, 2, 2, H, D], F32R)

        def weight(kind, i, part, odd):
            if kind == "o":
                return w_o[:, part, 1 - odd, i, :]
            return {"q": w_q, "k": w_k, "v": w_v}[kind][:, part, i, :]
        staged = sb("staged", [128, P.slots, D + (biases is not None)], I32 if codes else F32)
        qT = sb("qT", [128, 2, 2, H, TOK], F32R)
        kT = sb("kT", [128, 2, 2, NK, TOK], F32R)
        v_tok = sb("v_tok", [128, 2, 2, HALF, NK * HD], F32R)
        probsT = sb("probsT", [128, 2, TOK], F32R)
        outT = sb("outT", [128, 2, TOK], F32R)
        vT = [sb(f"vT{i}", [128, TOK])[:] for i in range(NK)] if masked else [scratch[:, 1, :]]
        neg_max = sb("neg_max", [128, 4])
        exp_bias = sb("exp_bias", [128, 4]) if scale != 1.0 else neg_max
        exp_sum = sb("exp_sum", [128, 4])
        inv_sum = sb("inv_sum", [128, 4])

        proj_bank = pb("proj_bank", [128, 3, 512])
        score_bank = pb("score_bank", [128, 512])
        probsT_bank = pb("probsT_bank", [128, 512])
        outT_bank = pb("outT_bank", [128, 512])
        out_bank = pb("out_bank", [128, 2, 512])

        rms_cols = sb("rms_cols", [128, KT]) if rms_weight is not None else None
        rms_loaded = sem("rms_loaded") if rms_weight is not None else None
        norm = Norm(ctx, sems, nc, f"{name}_norm", x, xT, scratch, out_bank, ident, rms_cols, rms_loaded)

        chunk_loaded = [sem(f"chunk_loaded{i}") for i in range(P.slots)]
        chunk_hi = sem("chunk_hi")
        chunk_ready = sem("chunk_ready")
        projected = sem("projected")
        v_projected = sem("v_projected")
        v_copied = sem("v_copied")
        task_hi = sem("task_hi")
        task_read = sem("task_read")
        scored = sem("scored")
        biased = sem("biased")
        row_max = sem("row_max")
        bias_ready = sem("exp_bias_ready") if scale != 1.0 else row_max
        exped = sem("exped")
        summed = sem("sum_inverted")
        inv_ready = sem("inv_ready") if pad_mask is not None else summed
        probs_ready = sem("probs_ready")
        probs_transposed = sem("probs_transposed")
        probsT_hi = sem("probsT_hi")
        probsT_ready = sem("probsT_ready")
        attended = sem("attended")
        outT_hi = sem("outT_hi")
        outT_ready = sem("outT_ready")
        out_done = sem("out_done")
        out_added = sem("out_added")
        x_loaded = [sem(f"x_loaded{h}") for h in range(2)] if x_dram is not None else None
        const_loaded = sem("const_loaded")
        parts = 1
        if codes:
            scales = sb("scales", [128, P.slots, D])
            dequantized = sem("dequantized")
            parts = 2
        if rope is not None:
            cosine, sine = sb("cosine", [128, S]), sb("sine", [128, S])
            direct = sb("direct", [128, 2, TOK])
            crossed = sb("crossed", [128, 2, TOK])
            rotated, qk_ready = sem("rotated"), sem("qk_ready")
        if causal is not None:
            causal_add = sb("causal_add", [128, S])
        if biases is not None:
            columns = {"q": sb("bias_q", [128, H]), "k": sb("bias_k", [128, NK]), "v": sb("bias_v", [128, NK])}
            bias_o = staged[:, 0, 0:D]
            out_bias_loaded = sem("out_bias_loaded")
        if pad_mask is not None:
            mask_bytes = sb("mask_bytes", [128, B, S], U8)
            pad_add = sb("pad_add", [128, B, S])
            row_any = sb("row_any", [128, B])
            head_bias = sb("head_bias", [128, H, S])
            mask_ready, head_bias_loaded = sem("mask_ready"), sem("head_bias_loaded")
        if source is not None:
            kvT = sb("kvT", [128, 2, KT, B * S], F32R)
            context_loaded = [sem(f"context_loaded{n}") for n in range(2 * KT)]
            context_hi, context_ready = sem("context_hi"), sem("context_ready")
        else:
            kvT = xT

        if source is not None:
            if pad_mask is not None:
                context_ring = vT + [pad_add[:, h * HALF:(h + 1) * HALF, :].rearrange("p b k -> p (b k)")
                                     for h in range(2)]
            else:
                context_ring = [staged[:, slot, 0:TOK] for slot in range(len(P.splits[1] + P.splits[2]), P.slots)]
            RING = len(context_ring)
        context_late = source is not None and pad_mask is not None

        def context_piece(n):
            return context_ring[n % RING], (n % KT, slice(n // KT * TOK, (n // KT + 1) * TOK))
        n_consts = 2 * (rope is not None) + (causal is not None) + (pad_mask is not None)

        block = ctx.enter_context(nc.Block())

        def unit_there(s, fixed):
            return not fixed or 0 <= s < P.units

        def half_there(h, fixed):
            return not fixed or 0 <= h < 2 * P.groups

        def splits_at(g, j, fixed):
            for kind, i in P.splits.get(j, []):
                of = g + 1
                if fixed and not 0 <= of < P.groups:
                    continue
                yield kind, i, P.chunk_number((kind, i), g), P.chunk_slot((kind, i)), of

        def first_splits():
            for j in sorted(P.splits):
                if j < P.first_step:
                    for kind, i in P.splits[j]:
                        yield kind, i, P.chunk_number((kind, i), -1), P.chunk_slot((kind, i)), 0

        def tasks_at(g, j, fixed):
            ahead, places = P.target(j)
            half = 2 * g + ahead
            if not half_there(half, fixed):
                return
            for k in places:
                yield P.tasks[k][0], P.tasks[k][1], k, half, P.PER_HALF * half + k, ahead % 2

        def last_task_use(kind, i, of):
            return P.PER_HALF * (2 * of - 1) + P.tasks.index((kind, i)) + 1

        def chunk_load_count(kind, i, cycle):
            return 16 * parts * (2 * (cycle + 1) + P.order.index((kind, i)) // P.slots + 1)

        def turns_at(g, j, fixed):
            half = 2 * g + j // UH + 1
            if (j + 1) % UH == 0 and half_there(half, fixed):
                for k, (kind, i) in enumerate(P.tasks):
                    if kind == "v":
                        yield kind, i, k, half, P.PER_HALF * half + k, (j // UH + 1) % 2

        def qk_place(k):
            return [n for n, task in enumerate(P.tasks) if task[0] != "v"].index(k)

        def ring_of(k, slot):
            return (P.qk_per_half * slot + qk_place(k)) % 2

        @block.sync
        def _(sp):
            def load(kind, i, number, slot, of):
                wait_count(sp, chunk_ready, number - P.slots + 1)
                per_group = H if kind in "qo" else NK
                at = of * per_group + i
                width = weights[kind].shape[2]
                sp.dma_start(staged[:, slot, 0:width], weights[kind][bass.ds(at, 1)].rearrange("o p n -> (o p) n"))\
                  .then_inc(chunk_loaded[slot], 16)
                if codes:
                    sp.dma_start(scales[:, slot, :], weights[kind + "_scales"][bass.ds(at, 1)]
                                 .rearrange("o n -> (o n)").partition_broadcast(128))\
                      .then_inc(chunk_loaded[slot], 16)

            if x_dram is not None:
                for h in range(2):
                    sp.dma_start(x[:, h * HALF:(h + 1) * HALF, :], x_dram[h * HALF:(h + 1) * HALF]
                                 .rearrange("b p n -> p b n")).then_inc(x_loaded[h], 16)
            for args in first_splits():
                load(*args)
            if rms_weight is not None:
                sp.dma_start(rms_cols[:], rms_weight).then_inc(rms_loaded, 16)
            if source is not None:
                for n in range(2 * KT):
                    if n >= RING:
                        sp.wait_ge(context_ready, n - RING + 1)
                    sp.dma_start(context_piece(n)[0], source[n // KT, n % KT]).then_inc(context_loaded[n], 16)
                if pad_mask is None:
                    sp.wait_ge(context_ready, 2 * KT)
            if rope is not None:
                sp.dma_start(cosine[:], rope[0]).then_inc(const_loaded, 16)
                sp.dma_start(sine[:], rope[1]).then_inc(const_loaded, 16)
            if causal is not None:
                sp.dma_start(causal_add[:], causal).then_inc(const_loaded, 16)
            if pad_mask is not None:
                sp.dma_start(mask_bytes[:], pad_mask).then_inc(const_loaded, 16)

            def load_head_bias(g):
                wait_count(sp, biased, 2 * UG * g)
                sp.dma_start(head_bias[:], position_bias[bass.ds(g * H, H)].rearrange("h q k -> q h k"))\
                  .then_inc(head_bias_loaded, 16)

            if position_bias is not None:
                load_head_bias(0)

            def step(g, j, fixed, odd):
                for args in splits_at(g, j, fixed):
                    load(*args)
                if position_bias is not None and j == UG - 1 and (not fixed or 0 <= g < P.groups - 1):
                    load_head_bias(g + 1)
            each_step(sp, P, step)
            if biases is not None:
                sp.wait_ge(chunk_ready, P.chunks * P.groups)
                sp.dma_start(bias_o, out_bias.partition_broadcast(128)).then_inc(out_bias_loaded, 16)

        @block.tensor
        def _(pe):
            norm.tensor(pe, range(HALF))

            def step(g, j, fixed, odd):
                s = g * UG + j
                if unit_there(s, fixed):
                    wait_count(pe, probs_ready, s + 1)
                    for i in range(4):
                        last = pe.transpose(probsT_bank[:, i * S:(i + 1) * S], probs[:, i * S:(i + 1) * S], ident[:])
                    last.then_inc(probs_transposed, 1)
                if unit_there(s + 1, fixed):
                    j1 = (j + 1) % UG
                    g1 = g + (j + 1) // UG
                    if j1 % UH == 0:
                        half = 2 * g1 + P.half_of(j1)
                        if rope is not None:
                            wait_count(pe, qk_ready, P.qk_per_half * (half + 1))
                        else:
                            wait_count(pe, task_read, P.PER_HALF * half + P.qk_per_half)
                    slot = P.half_of(j1)
                    for i, (b, h) in enumerate(P.pairs(j1)):
                        tok = slice(b * S, (b + 1) * S)
                        last = matmul3(pe, score_bank[:, i * S:(i + 1) * S], lambda p: qT[:, p, slot, h, tok],
                                       lambda p: kT[:, p, slot, 0 if P.shared_kv else h, tok], True, True)
                    last.then_inc(scored, 1)
                if unit_there(s - 1, fixed):
                    wait_count(pe, outT_ready, s)
                    if j == 1:
                        wait_count(pe, chunk_ready, P.chunk_number(("o", H - 1), g - 1) + 1)
                    slot = odd if j > 0 else 1 - odd
                    pairs = P.pairs((j - 1) % UG)
                    for bi in range(BU):
                        number = (s - 1) * BU + bi
                        bank = (j - 1 + bi) % 2 if BU == 1 else bi
                        wait_count(pe, out_added, number - 1)
                        mine = [i for i, (b, h) in enumerate(pairs) if b == pairs[0][0] + bi]
                        for n, i in enumerate(mine):
                            h = pairs[i][1]
                            last = matmul3(pe, out_bank[:, bank, :], lambda p: outT[:, p, i * S:(i + 1) * S],
                                           lambda p: w_o[:, p, slot, h, :], n == 0, n == len(mine) - 1)
                        last.then_inc(out_done, 1)
                if unit_there(s, fixed):
                    wait_count(pe, probsT_ready, s + 1)
                    slot = P.half_of(j)
                    if j % UH == 0:
                        wait_count(pe, task_read, P.PER_HALF * (2 * g + slot + 1))
                    if P.shared_kv:
                        b = P.pairs(j)[0][0]
                        last = matmul3(pe, outT_bank[:], lambda p: v_tok[:, p, slot, b, :],
                                       lambda p: probsT[:, p, :], True, True)
                    else:
                        for i, (b, h) in enumerate(P.pairs(j)):
                            last = matmul3(pe, outT_bank[:, i * S:(i + 1) * S],
                                           lambda p: v_tok[:, p, slot, b, h * HD:(h + 1) * HD],
                                           lambda p: probsT[:, p, i * S:(i + 1) * S], True, True)
                    last.then_inc(attended, 1)
                for kind, i, k, half, number, slot in turns_at(g, j, fixed):
                    wait_count(pe, v_copied, P.kv_heads * half + i + 1)
                    for b in range(HALF):
                        last = pe.transpose(proj_bank[:, P.bank_of(k), b * S:(b + 1) * S],
                                            vT[i][:, b * S:(b + 1) * S], ident[:])
                    last.then_inc(projected, 1)
                for kind, i, k, half, number, slot in tasks_at(g, j, fixed):
                    bank = proj_bank[:, P.bank_of(k), :]
                    wait_count(pe, task_read, number - 2)
                    if slot == 0:
                        of = g + P.target(j)[0] // 2
                        wait_count(pe, chunk_ready, P.chunk_number((kind, i), of - 1) + 1)
                    if fixed and half < 2:
                        if k == 0:
                            pe.wait_ge(norm.ready, HALF * (half + 1))
                        if source is not None and k == 1:
                            pe.wait_ge(context_ready, KT * (half + 1))
                    src, w = {"q": (xT, w_q), "k": (kvT, w_k), "v": (kvT, w_v)}[kind]
                    for kt in range(KT):
                        last = matmul3(pe, bank, lambda p: w[:, p, i, kt * 128:(kt + 1) * 128],
                                       lambda p: src[:, p, kt, slot * TOK:(slot + 1) * TOK], kt == 0, kt == KT - 1)
                    last.then_inc(v_projected if kind == "v" else projected, 1)
                    if fixed and g < 0 and j == P.first_step and k < 2:
                        norm.tensor(pe, range(HALF + 2 * k, HALF + 2 * k + 2))
            each_step(pe, P, step)

        def v_part(part, slot, i):
            return v_tok[:, part, slot, :, i * HD:(i + 1) * HD]

        def v_bank(k):
            return proj_bank[:, P.bank_of(k), :].rearrange("p (b n) -> p b n", n=HD)

        @block.scalar
        def _(act):
            def split_high(args, cycle, odd):
                kind, i, number, slot, of = args
                if kind == "o":
                    wait_count(act, out_done, cycle * UG * BU)
                else:
                    wait_count(act, projected, last_task_use(kind, i, of))
                if codes:
                    wait_count(act, dequantized, number + 1)
                else:
                    act.wait_ge(chunk_loaded[slot], chunk_load_count(kind, i, cycle))
                raw = as_f32(staged[:, slot, 0:D]) if codes else staged[:, slot, 0:D]
                if biases is not None and kind != "o":
                    wait_count(act, task_read, last_task_use(kind, i, of))
                    act.activation(columns[kind][:, i:i + 1], staged[:, slot, D:D + 1], ACT.Copy)
                act.activation(weight(kind, i, HI, odd), raw, ACT.Copy).then_inc(chunk_hi, 1)

            def split_all(chunks, cycle, odd):
                for args in chunks:
                    split_high(args, cycle, odd)

            split_all(list(first_splits()), -1, 1)

            def split_context(h):
                for n in range(h * KT, (h + 1) * KT):
                    raw, (k, tokens) = context_piece(n)
                    act.wait_ge(context_loaded[n], 16)
                    act.activation(kvT[:, HI, k, tokens], raw, ACT.Copy).then_inc(context_hi, 1)

            norm.scalar(act, range(HALF))
            if source is not None:
                split_context(0)
            norm.scalar(act, range(HALF, B))
            if source is not None and not context_late:
                split_context(1)

            def tasks_high(g, j, fixed):
                for kind, i, k, half, number, slot in tasks_at(g, j, fixed):
                    bank = proj_bank[:, P.bank_of(k), :]
                    if kind in "qk":
                        out = (qT if kind == "q" else kT)[:, HI, slot, i, :]
                        if rope is not None:
                            act.wait_ge(rotated, P.qk_per_half * half + qk_place(k) + 1)
                            act.activation(out, direct[:, ring_of(k, slot), :], ACT.Copy)\
                               .then_inc(task_hi, 1)
                            continue
                        act.wait_ge(projected, number + 1)
                        done = task_hi
                    else:
                        out, done = vT[i], v_copied
                        act.wait_ge(v_projected, P.kv_heads * half + i + 1)
                        if context_late and fixed and half == 0:
                            act.wait_ge(context_ready, 2 * KT)
                    if biases is not None:
                        act.activation(out, bank, ACT.Identity, bias=columns[kind][:, i:i + 1]).then_inc(done, 1)
                    else:
                        act.activation(out, bank, ACT.Copy).then_inc(done, 1)

            def step(g, j, fixed, odd):
                s = g * UG + j
                if unit_there(s, fixed):
                    act.wait_ge(probs_transposed, s + 1)
                    act.activation(probsT[:, HI, :], probsT_bank[:], ACT.Copy).then_inc(probsT_hi, 1)
                if rope is not None:
                    tasks_high(g - (j == 0), (j - 1) % UG, fixed)
                if unit_there(s + 1, fixed):
                    wait_count(act, bias_ready, s + 2)
                    scores = masked_scores if masked else score_bank[:]
                    for i in range(4):
                        last = act.activation(probs[:, i * S:(i + 1) * S], scores[:, i * S:(i + 1) * S], ACT.Exp,
                                              bias=exp_bias[:, i:i + 1], scale=scale, accum_out=exp_sum[:, i:i + 1])
                    last.then_inc(exped, 1)
                for kind, i, k, half, number, slot in turns_at(g, j, fixed):
                    act.wait_ge(projected, number + 1)
                    act.activation(v_part(HI, slot, i), v_bank(k), ACT.Copy).then_inc(task_hi, 1)
                if unit_there(s, fixed):
                    act.wait_ge(attended, s + 1)
                    wait_count(act, out_done, s * BU)
                    act.activation(outT[:, HI, :], outT_bank[:], ACT.Copy).then_inc(outT_hi, 1)
                if rope is None:
                    tasks_high(g, j, fixed)
                split_all(list(splits_at(g, j, fixed)), g, odd)
                if context_late and fixed and g < 0 and j == P.first_step:
                    split_context(1)
            each_step(act, P, step)

        @block.vector
        def _(dve):
            def dequantize(chunks, cycle):
                for kind, i, number, slot, of in chunks:
                    dve.wait_ge(chunk_loaded[slot], chunk_load_count(kind, i, cycle))
                    dve.scalar_tensor_tensor(as_f32(staged[:, slot, :]), staged[:, slot, :], 8.0, scales[:, slot, :],
                                              ALU.subtract, ALU.mult).then_inc(dequantized, 1)

            norm.statistics(dve, x_loaded)
            if codes:
                dequantize(list(first_splits()), -1)
            norm.vector(dve)

            def set_up_mask():
                dve.wait_ge(context_ready, 2 * KT)
                dve.tensor_scalar(pad_add[:], mask_bytes[:], 1.0, -MASKED, ALU.subtract, ALU.mult)
                dve.tensor_reduce(row_any[:], mask_bytes[:], AX.X, ALU.max).then_inc(mask_ready, 1)
                dve.wait_ge(mask_ready, 1)

            wait_count(dve, const_loaded, 16 * n_consts)

            def step(g, j, fixed, odd):
                s = g * UG + j
                if unit_there(s, fixed):
                    dve.wait_ge(probsT_hi, s + 1)
                    dve.tensor_tensor(probsT[:, LO, :], probsT_bank[:], as_f32(probsT[:, HI, :]), ALU.subtract)\
                       .then_inc(probsT_ready, 1)
                if unit_there(s + 1, fixed):
                    j1 = (j + 1) % UG
                    pairs = P.pairs(j1)
                    batch = P.half_of(j1) * HALF + pairs[0][0]
                    dve.wait_ge(scored, s + 2)
                    scores = score_bank[:].rearrange("p (i k) -> p i k", i=4)
                    out = masked_scores.rearrange("p (i k) -> p i k", i=4)
                    if causal is not None:
                        dve.tensor_tensor(out, scores, causal_add[:].unsqueeze(1).broadcast_to([128, 4, S]), ALU.add)\
                           .then_inc(biased, 1)
                        dve.wait_ge(biased, s + 2)
                        scores = out
                    if pad_mask is not None:
                        if j1 == 0:
                            dve.wait_ge(head_bias_loaded, 16 * (g + (j + 1) // UG + 1))
                        b4 = [128, BU, H, S]
                        dve.tensor_tensor(out.rearrange("p (b h) k -> p b h k", b=BU),
                                          scores.rearrange("p (b h) k -> p b h k", b=BU),
                                          head_bias[:].unsqueeze(1).broadcast_to(b4), ALU.add).then_inc(biased, 1)
                        wait_count(dve, biased, 2 * s + 3)
                        o4 = out.rearrange("p (b h) k -> p b h k", b=BU)
                        dve.tensor_tensor(o4, o4, pad_add[:, batch:batch + BU, :].unsqueeze(2).broadcast_to(b4),
                                          ALU.add).then_inc(biased, 1)
                        dve.wait_ge(biased, 2 * s + 4)
                        scores = out
                    dve.tensor_reduce(neg_max[:], scores, AX.X, ALU.max, negate=True).then_inc(row_max, 1)
                    if scale != 1.0:
                        dve.wait_ge(row_max, s + 2)
                        dve.tensor_scalar(exp_bias[:], neg_max[:], scale, None, ALU.mult).then_inc(bias_ready, 1)
                if unit_there(s - 1, fixed):
                    first = P.half_of((j - 1) % UG) * HALF + P.pairs((j - 1) % UG)[0][0]
                    for bi in range(BU):
                        bank = (j - 1 + bi) % 2 if BU == 1 else bi
                        dve.wait_ge(out_done, (s - 1) * BU + bi + 1)
                        xb = x[:, first + bi, :]
                        dve.tensor_tensor(xb, out_bank[:, bank, :], xb, ALU.add).then_inc(out_added, 1)
                if codes:
                    dequantize(list(splits_at(g, j, fixed)), g)
                if unit_there(s + 1, fixed):
                    dve.wait_ge(exped, s + 2)
                    dve.reciprocal(inv_sum[:], exp_sum[:]).then_inc(summed, 1)
                    if pad_mask is not None:
                        dve.wait_ge(summed, s + 2)
                        inv2 = inv_sum[:].rearrange("p (b h) -> p b h", b=BU)
                        dve.tensor_tensor(inv2, inv2, row_any[:, batch:batch + BU].unsqueeze(2)
                                          .broadcast_to([128, BU, H]), ALU.mult).then_inc(inv_ready, 1)
                    wait_count(dve, inv_ready, s + 2)
                    dve_probs = probs.rearrange("p (i k) -> p i k", i=4)
                    dve.tensor_tensor(dve_probs, dve_probs, inv_sum[:].unsqueeze(2).broadcast_to([128, 4, S]),
                                      ALU.mult).then_inc(probs_ready, 1)
                for kind, i, k, half, number, slot in turns_at(g, j, fixed):
                    dve.wait_ge(task_hi, number + 1)
                    dve.tensor_tensor(v_part(LO, slot, i), v_bank(k), as_f32(v_part(HI, slot, i)),
                                      ALU.subtract).then_inc(task_read, 1)
                if unit_there(s, fixed):
                    dve.wait_ge(outT_hi, s + 1)
                    dve.tensor_tensor(outT[:, LO, :], outT_bank[:], as_f32(outT[:, HI, :]), ALU.subtract)\
                       .then_inc(outT_ready, 1)
                for kind, i, k, half, number, slot in tasks_at(g, j, fixed):
                    bank = proj_bank[:, P.bank_of(k), :]
                    if kind in "qk" and rope is not None:
                        ring = ring_of(k, slot)
                        wait_count(dve, qk_ready, P.qk_per_half * half + qk_place(k) - 1)
                        dve.wait_ge(projected, number + 1)

                        def four(ap):
                            return ap.rearrange("p (b t) -> p b t", b=HALF)
                        for a, z, out in ((0, 128, direct), (64, 128, crossed), (0, 64, crossed)):
                            to = (a, z) if out is direct else ((a + 64) % 128, (a + 64) % 128 + 64)
                            table = cosine if out is direct else sine
                            last = dve.tensor_tensor(four(out[to[0]:to[1], ring, :]), four(bank[a:z]),
                                                     table[a:z, :].unsqueeze(1).broadcast_to([z - a, HALF, S]),
                                                     ALU.mult)
                        last.then_inc(task_read, 1)
                        continue
                    if kind == "v":
                        continue
                    dve.wait_ge(task_hi, number + 1)
                    out = qT if kind == "q" else kT
                    if biases is not None:
                        dve.scalar_tensor_tensor(out[:, LO, slot, i, :], bank, columns[kind][:, i:i + 1],
                                                 as_f32(out[:, HI, slot, i, :]), ALU.add, ALU.subtract)\
                           .then_inc(task_read, 1)
                    else:
                        dve.tensor_tensor(out[:, LO, slot, i, :], bank, as_f32(out[:, HI, slot, i, :]),
                                          ALU.subtract).then_inc(task_read, 1)
                if fixed and g < 0 and j == P.first_step and rms_weight is not None:
                    norm.update_x(dve)
                if fixed and g < 0 and j == P.first_step + 1 and pad_mask is not None:
                    set_up_mask()
            each_step(dve, P, step)
            if out_bias is not None:
                dve.wait_ge(out_added, P.units * BU)
                dve.wait_ge(out_bias_loaded, 16)
                for b in range(B):
                    dve.tensor_tensor(x[:, b, :], x[:, b, :], bias_o, ALU.add)

        @block.gpsimd
        def _(pool):
            def split_low(args, odd):
                kind, i, number, slot, of = args
                raw = as_f32(staged[:, slot, 0:D]) if codes else staged[:, slot, 0:D]
                wait_count(pool, chunk_hi, number + 1)
                pool.tensor_tensor(weight(kind, i, LO, odd), raw, as_f32(weight(kind, i, HI, odd)), ALU.subtract).then_inc(chunk_ready, 1)

            norm.gpsimd(pool)
            for args in first_splits():
                split_low(args, 1)

            def split_context(h):
                for n in range(h * KT, (h + 1) * KT):
                    raw, (k, tokens) = context_piece(n)
                    pool.wait_ge(context_hi, n + 1)
                    pool.tensor_tensor(kvT[:, LO, k, tokens], raw, as_f32(kvT[:, HI, k, tokens]),
                                       ALU.subtract).then_inc(context_ready, 1)

            if source is not None:
                split_context(0)
                if not context_late:
                    split_context(1)

            def rotate_low(g, j, fixed):
                for kind, i, k, half, number, slot in tasks_at(g, j, fixed):
                    if kind in "qk":
                        out = qT if kind == "q" else kT
                        pool.wait_ge(task_hi, number + 1)
                        pool.tensor_tensor(out[:, LO, slot, i, :], direct[:, ring_of(k, slot), :],
                                           as_f32(out[:, HI, slot, i, :]), ALU.subtract).then_inc(qk_ready, 1)

            def step(g, j, fixed, odd):
                if rope is not None:
                    rotate_low(g - (j == 0), (j - 1) % UG, fixed)
                    for kind, i, k, half, number, slot in tasks_at(g, j, fixed):
                        if kind in "qk":
                            ring = ring_of(k, slot)
                            pool.wait_ge(task_read, number + 1)
                            pool.tensor_tensor(direct[:, ring, :], direct[:, ring, :], crossed[:, ring, :], ALU.add)\
                                .then_inc(rotated, 1)
                for args in splits_at(g, j, fixed):
                    split_low(args, odd)
                if context_late and fixed and g < 0 and j == P.first_step:
                    split_context(1)
            each_step(pool, P, step)


class Splitter:

    def __init__(self, sems, nc, name):
        self.pieces = []
        self.high_done = sems.new(f"{name}_weight_hi")
        self.ready = sems.new(f"{name}_weight_ready")

    def add(self, loaded, count, raw, high, low):
        self.pieces.append((loaded, count, raw, high, low))

    def scalar(self, act, first=0, end=None):
        for loaded, count, raw, high, _ in self.pieces[first:end]:
            act.wait_ge(loaded, count)
            act.activation(high, raw, ACT.Copy).then_inc(self.high_done, 1)

    def gpsimd(self, pool, first=0, end=None):
        for n, (_, _, raw, high, low) in list(enumerate(self.pieces))[first:end]:
            pool.wait_ge(self.high_done, n + 1)
            pool.tensor_tensor(low, raw, as_f32(high), ALU.subtract).then_inc(self.ready, 1)


def expert_layer(nc, sems, x, ident, gate_w, lora_a, lora_b):
    name, E = "moe", 8
    with ExitStack() as ctx:
        def sb(n, shape, dt=F32):
            return ctx.enter_context(nc.sbuf_tensor(f"{name}_{n}", shape, dt))

        def pb(n, shape):
            return ctx.enter_context(nc.psum_tensor(f"{name}_{n}", shape, F32))

        def sem(n):
            return sems.new(f"{name}_{n}")

        xT = sb("xT", [128, 2, KT, B * S], F32R)
        scratch = sb("scratch", [128, 2, D])
        gate_raw, gate = sb("gate_raw", [128, KT, E]), sb("gate", [128, 2, KT, E], F32R)
        a_raw, a = sb("a_raw", [128, KT, D]), sb("a", [128, 2, KT, D], F32R)
        b_raw, b_w = sb("b_raw", [128, KT, D]), sb("b_w", [128, 2, KT, D], F32R)
        rank_first = sb("rank_first", [128, B, E])
        shifted, prob = sb("shifted", [128, B, E]), sb("prob", [128, B, E])
        equal, key, rest = sb("equal", [128, B, E]), sb("key", [128, B, E]), sb("rest", [128, B, E])
        chosen = [sb("chosen0", [128, B, E]), sb("chosen1", [128, B, E])]
        expert_weight = sb("expert_weight", [128, B, E])
        best = [sb("best0", [128, B]), sb("best1", [128, B])]
        top, total, inverse, best_key = (sb(n, [128, B]) for n in ("top", "total", "inverse", "best_key"))
        hidden = sb("hidden", [128, 2, D])
        hiddenT = sb("hiddenT", [128, 2, 2, D], F32R)

        norm_bank = pb("norm_bank", [128, 2, 512])
        gate_bank = pb("gate_bank", [128, 512])
        hidden_bank = pb("hidden_bank", [128, 512])
        hiddenT_bank = pb("hiddenT_bank", [128, 512])
        y_bank = pb("y_bank", [128, 2, 512])

        norm = Norm(ctx, sems, nc, f"{name}_norm", x, xT, scratch, norm_bank, ident)
        split = Splitter(sems, nc, name)
        loaded = [sem(f"loaded{i}") for i in range(3)]
        split.add(loaded[0], 16, gate_raw[:], gate[:, HI], gate[:, LO])
        for k in range(KT):
            split.add(loaded[1], 16, a_raw[:, k, :], a[:, HI, k, :], a[:, LO, k, :])
        for k in range(KT):
            split.add(loaded[2], 16, b_raw[:, k, :], b_w[:, HI, k, :], b_w[:, LO, k, :])
        rank_set, gated, exped, small, weighted_ready = (sem(n) for n in (
            "rank_set", "gated", "exped", "small", "weighted_ready"))
        hidden_done, hidden_scaled, hidden_transposed = sem("hidden_done"), sem("hidden_scaled"), sem("hiddenT_done")
        hiddenT_hi, hiddenT_ready, y_done, y_added = (sem(n) for n in ("hiddenT_hi", "hiddenT_ready", "y_done", "y_added"))
        shifted_ready = sem("shifted_ready")
        block = ctx.enter_context(nc.Block())

        @block.sync
        def _(sp):
            sp.dma_start(gate_raw[:], gate_w).then_inc(loaded[0], 16)
            sp.dma_start(a_raw[:], lora_a).then_inc(loaded[1], 16)
            sp.dma_start(b_raw[:], lora_b).then_inc(loaded[2], 16)

        @block.gpsimd
        def _(pool):
            pool.iota(rank_first[:], pattern=[[0, B], [-1, E]], base=E, channel_multiplier=0,
                      allow_small_or_imprecise_dtypes=True).then_inc(rank_set, 1)
            split.gpsimd(pool)
            norm.gpsimd(pool)

        @block.scalar
        def _(act):
            split.scalar(act)
            norm.scalar(act)
            act.wait_ge(shifted_ready, 1)
            act.activation(prob[:], shifted[:], ACT.Exp).then_inc(exped, 1)
            for b in range(B):
                act.wait_ge(hidden_transposed, b + 1)
                act.activation(hiddenT[:, HI, b % 2, :], hiddenT_bank[:], ACT.Copy).then_inc(hiddenT_hi, 1)

        @block.tensor
        def _(pe):
            norm.tensor(pe)
            pe.wait_ge(split.ready, 1)
            pe.wait_ge(norm.ready, B)
            for b in range(B):
                tok = slice(b * S, (b + 1) * S)
                for k in range(KT):
                    last = matmul3(pe, gate_bank[:, b * E:(b + 1) * E], lambda p: xT[:, p, k, tok],
                                   lambda p: gate[:, p, k, :], k == 0, k == KT - 1)
            last.then_inc(gated, 1)
            pe.wait_ge(split.ready, 1 + 2 * KT)
            for b in range(B + 1):
                if b < B:
                    tok = slice(b * S, (b + 1) * S)
                    if b >= 1:
                        pe.wait_ge(hidden_scaled, b)
                    for k in range(KT):
                        last = matmul3(pe, hidden_bank[:], lambda p: xT[:, p, k, tok],
                                       lambda p: a[:, p, k, :], k == 0, k == KT - 1)
                    last.then_inc(hidden_done, 1)
                if b >= 1:
                    c = b - 1
                    pe.wait_ge(hiddenT_ready, c + 1)
                    if c >= 2:
                        pe.wait_ge(y_added, c - 1)
                    for k in range(KT):
                        last = matmul3(pe, y_bank[:, c % 2, :], lambda p: hiddenT[:, p, c % 2, k * 128:(k + 1) * 128],
                                       lambda p: b_w[:, p, k, :], k == 0, k == KT - 1)
                    last.then_inc(y_done, 1)
                if b < B:
                    pe.wait_ge(hidden_scaled, b + 1)
                    for k in range(KT):
                        last = pe.transpose(hiddenT_bank[:, k * 128:(k + 1) * 128],
                                            hidden[:, b % 2, k * 128:(k + 1) * 128], ident[:])
                    last.then_inc(hidden_transposed, 1)

        @block.vector
        def _(dve):
            norm.statistics(dve)
            norm.vector(dve)
            done = 0

            def chain(instruction):
                nonlocal done
                done += 1
                instruction.then_inc(small, 1)
                dve.wait_ge(small, done)

            def wide(ap):
                return ap[:].unsqueeze(2).broadcast_to([128, B, E])
            logits = gate_bank[:, 0:B * E].rearrange("p (b e) -> p b e", e=E)
            dve.wait_ge(gated, 1)
            chain(dve.tensor_reduce(top[:], logits, AX.X, ALU.max))
            dve.tensor_tensor(shifted[:], logits, wide(top), ALU.subtract).then_inc(shifted_ready, 1)
            dve.wait_ge(exped, 1)
            chain(dve.tensor_reduce(total[:], prob[:], AX.X, ALU.add))
            chain(dve.reciprocal(inverse[:], total[:]))
            chain(dve.tensor_tensor(prob[:], prob[:], wide(inverse), ALU.mult))
            dve.wait_ge(rank_set, 1)
            left = prob
            for n in range(2):
                chain(dve.tensor_reduce(best[n][:], left[:], AX.X, ALU.max))
                chain(dve.tensor_tensor(equal[:], left[:], wide(best[n]), ALU.is_equal))
                chain(dve.tensor_tensor(key[:], equal[:], rank_first[:], ALU.mult))
                chain(dve.tensor_reduce(best_key[:], key[:], AX.X, ALU.max))
                chain(dve.tensor_tensor(chosen[n][:], key[:], wide(best_key), ALU.is_equal))
                if n == 0:
                    chain(dve.scalar_tensor_tensor(rest[:], chosen[0][:], -2.0, prob[:], ALU.mult, ALU.add))
                    left = rest
            chain(dve.tensor_tensor(total[:], best[0][:], best[1][:], ALU.add))
            chain(dve.reciprocal(inverse[:], total[:]))
            for n in range(2):
                chain(dve.tensor_tensor(best[n][:], best[n][:], inverse[:], ALU.mult))
                chain(dve.tensor_tensor(chosen[n][:], chosen[n][:], wide(best[n]), ALU.mult))
            chain(dve.tensor_tensor(expert_weight[:], chosen[0][:], chosen[1][:], ALU.add))
            for b in range(B + 1):
                if b < B:
                    dve.wait_ge(hidden_done, b + 1)
                    if b >= 2:
                        dve.wait_ge(hidden_transposed, b - 1)
                    dve.tensor_tensor(hidden[:, b % 2, :].rearrange("p (e r) -> p e r", e=E),
                                      hidden_bank[:].rearrange("p (e r) -> p e r", e=E),
                                      expert_weight[:, b, :].unsqueeze(2).broadcast_to([128, E, D // E]),
                                      ALU.mult).then_inc(hidden_scaled, 1)
                    dve.wait_ge(hiddenT_hi, b + 1)
                    dve.tensor_tensor(hiddenT[:, LO, b % 2, :], hiddenT_bank[:], as_f32(hiddenT[:, HI, b % 2, :]),
                                      ALU.subtract).then_inc(hiddenT_ready, 1)
                if b >= 1:
                    dve.wait_ge(y_done, b)
                    dve.tensor_tensor(x[:, b - 1, :], y_bank[:, (b - 1) % 2, :], x[:, b - 1, :], ALU.add)\
                       .then_inc(y_added, 1)


def adapter_layer(nc, sems, x, ident, weight, bias, lora_a, lora_b, starts, out):
    name, N, R = "ffn", 3, 16
    with ExitStack() as ctx:
        def sb(n, shape, dt=F32):
            return ctx.enter_context(nc.sbuf_tensor(f"{name}_{n}", shape, dt))

        def pb(n, shape):
            return ctx.enter_context(nc.psum_tensor(f"{name}_{n}", shape, F32))

        def sem(n):
            return sems.new(f"{name}_{n}")

        n_starts = starts.shape[0]
        xT = sb("xT", [128, 2, KT, B * S], F32R)
        scratch = sb("scratch", [128, 2, D])
        w_raw, w = sb("w_raw", [128, KT, D]), sb("w", [128, 2, KT, D], F32R)
        a_raw, a = sb("a_raw", [128, KT, N * R]), sb("a", [128, 2, KT, N * R], F32R)
        b_w = sb("b_w", [N * R, D])
        bias_all = sb("bias_all", [128, D])
        starts_all = sb("starts_all", [128, n_starts], I32)
        starts_f = sb("starts_f", [128, n_starts])
        batch_number = sb("batch_number", [128, B, n_starts])
        begun = sb("begun", [128, B, n_starts])
        segment = sb("segment", [128, B])
        adapter_on = sb("adapter_on", [128, B, N])
        adapter_number = sb("adapter_number", [128, B, N])
        low = sb("low", [128, 2, N * R])
        lowT = sb("lowT", [N * R, 2, S])
        norm_bank = pb("norm_bank", [128, 2, 512])
        y_bank = pb("y_bank", [128, 2, 512])
        low_bank = pb("low_bank", [128, 2, 512])
        lowT_bank = pb("lowT_bank", [128, 2, 512])

        norm = Norm(ctx, sems, nc, f"{name}_norm", x, xT, scratch, norm_bank, ident)
        split = Splitter(sems, nc, name)
        loaded = [sem(f"loaded{i}") for i in range(2)]
        split.add(loaded[0], 16, a_raw[:], a[:, HI], a[:, LO])
        for k in range(KT):
            split.add(loaded[1], 16, w_raw[:, k, :], w[:, HI, k, :], w[:, LO, k, :])
        small_loaded, numbers_set, small = sem("small_loaded"), sem("numbers_set"), sem("small")
        low_done, low_scaled, low_transposed, lowT_ready = (sem(n) for n in (
            "low_done", "low_scaled", "low_transposed", "lowT_ready"))
        y_done, y_added, stored, biased = sem("y_done"), sem("y_added"), sem("stored"), sem("x_biased")
        block = ctx.enter_context(nc.Block())

        @block.sync
        def _(sp):
            sp.dma_start(starts_all[:], starts.partition_broadcast(128)).then_inc(small_loaded, 16)
            sp.dma_start(bias_all[:], bias.partition_broadcast(128)).then_inc(small_loaded, 16)
            sp.dma_start(b_w[:], lora_b).then_inc(small_loaded, 16)
            sp.dma_start(a_raw[:], lora_a).then_inc(loaded[0], 16)
            sp.dma_start(w_raw[:], weight).then_inc(loaded[1], 16)
            for b in range(B):
                sp.wait_ge(y_added, b + 1)
                sp.dma_start(out[b], x[:, b, :]).then_inc(stored, 16)
            sp.wait_ge(stored, 16 * B)

        @block.gpsimd
        def _(pool):
            pool.iota(batch_number[:], pattern=[[1, B], [0, n_starts]], base=0, channel_multiplier=0,
                      allow_small_or_imprecise_dtypes=True).then_inc(numbers_set, 1)
            pool.iota(adapter_number[:], pattern=[[0, B], [1, N]], base=2, channel_multiplier=0,
                      allow_small_or_imprecise_dtypes=True).then_inc(numbers_set, 1)
            norm.gpsimd(pool)
            split.gpsimd(pool)

        @block.scalar
        def _(act):
            split.scalar(act)
            norm.scalar(act)
            for b in range(B):
                act.wait_ge(low_transposed, b + 1)
                if b >= 2:
                    act.wait_ge(y_done, b - 1)
                act.activation(lowT[:, b % 2, :], lowT_bank[0:N * R, b % 2, 0:S], ACT.Copy).then_inc(lowT_ready, 1)

        @block.tensor
        def _(pe):
            norm.tensor(pe)
            pe.wait_ge(small_loaded, 48)
            pe.wait_ge(split.ready, 1 + KT)
            pe.wait_ge(norm.ready, B)

            def down(b):
                tok = slice(b * S, (b + 1) * S)
                for k in range(KT):
                    last = matmul3(pe, low_bank[:, b % 2, 0:N * R], lambda p: xT[:, p, k, tok],
                                   lambda p: a[:, p, k, :], k == 0, k == KT - 1)
                last.then_inc(low_done, 1)
            down(0)
            for b in range(B):
                tok = slice(b * S, (b + 1) * S)
                if b + 1 < B:
                    if b >= 1:
                        pe.wait_ge(low_scaled, b)
                    down(b + 1)
                pe.wait_ge(low_scaled, b + 1)
                if b >= 2:
                    pe.wait_ge(lowT_ready, b - 1)
                pe.transpose(lowT_bank[0:N * R, b % 2, 0:S], low[:, b % 2, :], ident[:]).then_inc(low_transposed, 1)
                if b >= 2:
                    pe.wait_ge(y_added, b - 1)
                for k in range(KT):
                    matmul3(pe, y_bank[:, b % 2, :], lambda p: xT[:, p, k, tok], lambda p: w[:, p, k, :], k == 0, False)
                pe.wait_ge(lowT_ready, b + 1)
                pe.matmul(y_bank[:, b % 2, :], lowT[:, b % 2, :], b_w[:], start=False, stop=True,
                          skip_group_check=True).then_inc(y_done, 1)

        @block.vector
        def _(dve):
            norm.statistics(dve)
            norm.vector(dve)
            dve.wait_ge(small_loaded, 48)
            dve.tensor_copy(starts_f[:], starts_all[:]).then_inc(small, 1)
            dve.wait_ge(small, 1)
            dve.wait_ge(numbers_set, 2)
            dve.tensor_tensor(begun[:], batch_number[:], starts_f[:].unsqueeze(1).broadcast_to([128, B, n_starts]),
                              ALU.is_ge).then_inc(small, 1)
            dve.wait_ge(small, 2)
            dve.tensor_reduce(segment[:], begun[:], AX.X, ALU.add).then_inc(small, 1)
            dve.wait_ge(small, 3)
            dve.tensor_tensor(adapter_on[:], segment[:].unsqueeze(2).broadcast_to([128, B, N]), adapter_number[:],
                              ALU.is_equal).then_inc(small, 1)
            dve.wait_ge(small, 4)
            for b in range(B):
                dve.tensor_tensor(x[:, b, :], x[:, b, :], bias_all[:], ALU.add).then_inc(biased, 1)

            def scale_low(b):
                dve.wait_ge(low_done, b + 1)
                if b >= 2:
                    dve.wait_ge(low_transposed, b - 1)
                dve.tensor_tensor(low[:, b % 2, :].rearrange("p (n r) -> p n r", n=N),
                                  low_bank[:, b % 2, 0:N * R].rearrange("p (n r) -> p n r", n=N),
                                  adapter_on[:, b, :].unsqueeze(2).broadcast_to([128, N, R]), ALU.mult)\
                   .then_inc(low_scaled, 1)
            scale_low(0)
            for b in range(B):
                if b + 1 < B:
                    scale_low(b + 1)
                dve.wait_ge(y_done, b + 1)
                dve.wait_ge(biased, b + 1)
                dve.tensor_tensor(x[:, b, :], y_bank[:, b % 2, :], x[:, b, :], ALU.add).then_inc(y_added, 1)


def small_attention(nc, sems, x, ident, w_q_dram, w_k_dram, w_v_dram, w_o_dram, rope_q, rope_k, causal, parities):
    name, T, HW, KV = "small", 4, 16, 8
    UNITS_OF_PAIR = 16
    BATCH_PAIRS = B // 2
    UNITS = UNITS_OF_PAIR * BATCH_PAIRS
    with ExitStack() as ctx:
        def sb(n, shape, dt=F32):
            return ctx.enter_context(nc.sbuf_tensor(f"{name}_{n}", shape, dt))

        def pb(n, shape):
            return ctx.enter_context(nc.psum_tensor(f"{name}_{n}", shape, F32))

        def sem(n):
            return sems.new(f"{name}_{n}")

        xT = sb("xT", [128, 2, KT, B * S], F32R)
        scratch = sb("scratch", [128, 2, D])
        probs = vT = scratch
        masked_scores = sb("masked_scores", [128, 2, D])
        raw = sb("raw", [128, KT, D])
        k_raw, v_raw = sb("k_raw", [128, KT, 128]), sb("v_raw", [128, KT, 128])
        w_q = sb("w_q", [128, 2, 2, KT, T * 128], F32R)
        w_k = sb("w_k", [128, 2, 2, KT, 128], F32R)
        w_v = sb("w_v", [128, 2, KT, 128], F32R)
        w_o = sb("w_o", [128, 2, KT, D], F32R)
        qT = sb("qT", [128, 2, T, B * S], F32R)
        kT = sb("kT", [128, 2, 2, B * S], F32R)
        v_tok = sb("v_tok", [128, B, KV * HW])
        cos_q, sin_q, cos_k, sin_k = (sb(n, [128, S]) for n in ("cos_q", "sin_q", "cos_k", "sin_k"))
        causal_add, parity = sb("causal_add", [128, S]), sb("parity", [128, 2])
        direct, crossed = sb("direct", [128, TOK]), sb("crossed", [128, TOK])
        neg_max, exp_sum = sb("neg_max", [128, 2, 4]), sb("exp_sum", [128, 2, 2, NH])
        inv_sum = sb("inv_sum", [128, 2, NH])
        probsT = sb("probsT", [128, 2, 512])
        heads_out = sb("heads_out", [128, 2, D])
        heads_outT = sb("heads_outT", [128, 2, D], F32R)

        pair_banks = [pb("proj_bank", [128, 2, 512]), pb("score_bank", [128, 2, 512]), pb("probsT_bank", [128, 2, 512])]
        proj_bank, score_bank, probsT_bank = pair_banks
        out_bank = pb("out_bank", [128, 2, 512])

        norm = Norm(ctx, sems, nc, f"{name}_norm", x, xT, scratch, proj_bank, ident)
        split = Splitter(sems, nc, name)
        k_loaded, v_loaded, q_loaded, o_loaded, const_loaded = (sem(n) for n in (
            "k_loaded", "v_loaded", "q_loaded", "o_loaded", "const_loaded"))
        half = HW // 2

        def rows(ap):
            return ap.rearrange("p k (j s d) -> p k j s d", s=2, d=half)
        split.add(k_loaded, 16, k_raw[:], w_k[:, HI, 0], w_k[:, LO, 0])
        for s in range(2):
            split.add(k_loaded, 16, rows(k_raw[:])[:, :, :, 1 - s], rows(w_k[:, HI, 1])[:, :, :, s],
                      rows(w_k[:, LO, 1])[:, :, :, s])
        split.add(v_loaded, 16, v_raw[:], w_v[:, HI], w_v[:, LO])
        for k in range(KT):
            def tiles(ap):
                return ap.rearrange("p (t j d) -> p t j d", t=T, j=KV)
            source = raw[:, k, :].rearrange("p (j t d) -> p t j d", t=T, j=KV)
            split.add(q_loaded, 16, source, tiles(w_q[:, HI, 0, k]), tiles(w_q[:, LO, 0, k]))
            for s in range(2):
                part = slice(s * half, (s + 1) * half)
                other = slice((1 - s) * half, (2 - s) * half)
                split.add(q_loaded, 16, source[..., other], tiles(w_q[:, HI, 1, k])[..., part],
                          tiles(w_q[:, LO, 1, k])[..., part])
        N_EARLY = len(split.pieces)
        for k in range(KT):
            split.add(o_loaded, 16, raw[:, k, :], w_o[:, HI, k], w_o[:, LO, k])
        tasks = [("k", 0, h) for h in range(2)] + [("q", t, h) for h in range(2) for t in range(T)]
        projected, products, rotated, part_hi, part_ready = (sem(n) for n in (
            "projected", "products", "rotated", "part_hi", "part_ready"))
        vT_done, vT_copied, v_done, v_ready = sem("vT_done"), sem("vT_copied"), sem("v_done"), sem("v_ready")
        scored, biased, maxed, exped, transposed, attended = (sem(n) for n in (
            "scored", "biased", "maxed", "exped", "transposed", "attended"))
        probsT_ready = [sem("probsT_even"), sem("probsT_odd")]
        inverted, out_scaled, outT_done, outT_hi, outT_ready, y_done, y_added = (sem(n) for n in (
            "inverted", "out_scaled", "outT_done", "outT_hi", "outT_ready", "y_done", "y_added"))
        block = ctx.enter_context(nc.Block())

        def unit(u):
            return u // UNITS_OF_PAIR, u // 4 % 4, u % 4

        def head(t, group, par):
            return 4 * (2 * group + par) + t

        def finishing(u):
            if u >= UNITS_OF_PAIR and u % UNITS_OF_PAIR < 5:
                return u // UNITS_OF_PAIR - 1, u % UNITS_OF_PAIR
            return None, None
        STEPS = range(-2, UNITS + 5)

        @block.sync
        def _(sp):
            sp.dma_start(k_raw[:], w_k_dram).then_inc(k_loaded, 16)
            sp.dma_start(v_raw[:], w_v_dram).then_inc(v_loaded, 16)
            sp.dma_start(raw[:], w_q_dram).then_inc(q_loaded, 16)
            for to, of in ((cos_q, rope_q[0]), (sin_q, rope_q[1]), (cos_k, rope_k[0]), (sin_k, rope_k[1]),
                           (causal_add, causal), (parity, parities)):
                sp.dma_start(to[:], of).then_inc(const_loaded, 16)
            sp.wait_ge(split.ready, N_EARLY)
            sp.dma_start(raw[:], w_o_dram).then_inc(o_loaded, 16)

        @block.tensor
        def _(pe):
            norm.tensor(pe)
            pe.wait_ge(norm.ready, B)
            pe.wait_ge(split.ready, N_EARLY)
            for h in range(2):
                for k in range(KT):
                    last = matmul3(pe, out_bank[:, h, :], lambda p: w_v[:, p, k, :],
                                   lambda p: xT[:, p, k, h * TOK:(h + 1) * TOK], k == 0, k == KT - 1)
                last.then_inc(vT_done, 1)
            for n, (kind, t, h) in enumerate(tasks):
                if n >= 3:
                    pe.wait_ge(products, n - 2)
                for swapped in range(2):
                    for k in range(KT):
                        last = matmul3(pe, pair_banks[n % 3][:, swapped, :],
                                       (lambda p: w_k[:, p, swapped, k, :]) if kind == "k" else
                                       (lambda p: w_q[:, p, swapped, k, t * 128:(t + 1) * 128]),
                                       lambda p: xT[:, p, k, h * TOK:(h + 1) * TOK], k == 0, k == KT - 1)
                last.then_inc(projected, 1)
                if n == 1:
                    pe.wait_ge(vT_copied, 2)
                    for b in range(B):
                        last = pe.transpose(out_bank[:, b // HALF, (b % HALF) * 128:(b % HALF + 1) * 128],
                                            vT[:, b // HALF, (b % HALF) * S:(b % HALF + 1) * S], ident[:])
                    last.then_inc(v_done, 1)
            pe.wait_ge(v_ready, 2)
            pe.wait_ge(part_ready, len(tasks))

            def step(u):
                if u + 2 < UNITS:
                    pair, t, group = unit(u + 2)
                    rows32 = slice(32 * group, 32 * group + 32)
                    wait_count(pe, biased, u + 1)
                    for bi in range(2):
                        tok = slice((2 * pair + bi) * S, (2 * pair + bi + 1) * S)
                        last = matmul3(pe, score_bank[:, u % 2, bi * 256:(bi + 1) * 256],
                                       lambda p: qT[rows32, p, t, tok], lambda p: kT[rows32, p, :, tok], True, True)
                    last.then_inc(scored, 1)
                if 0 <= u < UNITS:
                    pe.wait_ge(exped, u + 1)
                    wait_count(pe, probsT_ready[u % 2], u // 2)
                    for i in range(4):
                        last = pe.transpose(probsT_bank[:, u % 2, i * S:(i + 1) * S],
                                            probs[:, u % 2, i * S:(i + 1) * S], ident[:])
                    last.then_inc(transposed, 1)
                done_pair, stage = finishing(u)
                if stage in (1, 3):
                    n = 2 * done_pair + stage // 2
                    pe.wait_ge(out_scaled, n + 1)
                    wait_count(pe, outT_ready, n)
                    for k in range(KT):
                        last = pe.transpose(proj_bank[:, 0, k * 128:(k + 1) * 128],
                                            heads_out[:, n % 2, k * 128:(k + 1) * 128], ident[:])
                    last.then_inc(outT_done, 1)
                if stage in (2, 4):
                    n = 2 * done_pair + stage // 2 - 1
                    pe.wait_ge(outT_ready, n + 1)
                    wait_count(pe, y_added, n)
                    pe.wait_ge(split.ready, N_EARLY + KT)
                    for k in range(KT):
                        last = matmul3(pe, proj_bank[:, 1, :], lambda p: heads_outT[:, p, k * 128:(k + 1) * 128],
                                       lambda p: w_o[:, p, k, :], k == 0, k == KT - 1)
                    last.then_inc(y_done, 1)
                v = u - 1
                if 0 <= v < UNITS:
                    pair, t, group = unit(v)
                    pe.wait_ge(probsT_ready[v % 2], v // 2 + 1)
                    if v % UNITS_OF_PAIR == 0:
                        wait_count(pe, out_scaled, 2 * pair)
                    for i in range(4):
                        bi, par = i // 2, i % 2
                        h, kv = head(t, group, par), 2 * group + par
                        last = pe.matmul(out_bank[:, bi, h * HW:(h + 1) * HW], probsT[:, v % 2, i * S:(i + 1) * S],
                                         v_tok[:, 2 * pair + bi, kv * HW:(kv + 1) * HW], start=True, stop=True)
                    last.then_inc(attended, 1)

            for u in STEPS:
                step(u)

        @block.scalar
        def _(act):
            split.scalar(act, 0, N_EARLY)
            norm.scalar(act)
            for h in range(2):
                act.wait_ge(vT_done, h + 1)
                act.activation(vT[:, h, :], out_bank[:, h, :], ACT.Copy).then_inc(vT_copied, 1)
            act.wait_ge(const_loaded, 16 * 6)
            for n, (kind, t, h) in enumerate(tasks):
                tok = slice(h * TOK, (h + 1) * TOK)
                act.wait_ge(rotated, n + 1)
                if kind == "q":
                    last = act.activation(qT[:, HI, t, tok], direct[:], ACT.Copy)
                else:
                    for par in range(2):
                        last = act.activation(kT[:, HI, par, tok], direct[:], ACT.Copy, scale=parity[:, par:par + 1])
                last.then_inc(part_hi, 1)
                if n == 1:
                    act.wait_ge(v_done, 1)
                    for i in range(2):
                        act.activation(v_tok[:, i * HALF:(i + 1) * HALF, :],
                                       out_bank[:, i, :].rearrange("p (b n) -> p b n", b=HALF), ACT.Copy)\
                           .then_inc(v_ready, 1)
            split.scalar(act, N_EARLY)

            def step(u):
                if 0 <= u < UNITS and u % 2 == 0:
                    act.wait_ge(transposed, u + 1)
                    wait_count(act, attended, u - 1)
                    act.activation(probsT[:, 0, :], probsT_bank[:, 0, :], ACT.Copy).then_inc(probsT_ready[0], 1)
                if u + 2 < UNITS:
                    pair, t, group = unit(u + 2)
                    act.wait_ge(maxed, u + 3)
                    wait_count(act, transposed, u + 1)
                    for i in range(4):
                        h = head(t, group, i % 2)
                        last = act.activation(probs[:, u % 2, i * S:(i + 1) * S],
                                              masked_scores[:, u % 2, i * S:(i + 1) * S], ACT.Exp,
                                              bias=neg_max[:, u % 2, i:i + 1],
                                              accum_out=exp_sum[:, pair % 2, i // 2, h:h + 1])
                    last.then_inc(exped, 1)
                done_pair, stage = finishing(u)
                if stage in (1, 3):
                    act.wait_ge(outT_done, 2 * done_pair + stage // 2 + 1)
                    wait_count(act, y_done, 2 * done_pair + stage // 2)
                    act.activation(heads_outT[:, HI, :], proj_bank[:, 0, :], ACT.Copy).then_inc(outT_hi, 1)
            for u in STEPS:
                step(u)

        @block.vector
        def _(dve):
            norm.statistics(dve)
            norm.vector(dve)
            dve.wait_ge(const_loaded, 16 * 6)

            def four(ap):
                return ap.rearrange("p (b t) -> p b t", b=HALF)

            def table(ap):
                return ap[:].unsqueeze(1).broadcast_to([128, HALF, S])
            for n, (kind, t, h) in enumerate(tasks):
                cos, sin = (cos_q, sin_q) if kind == "q" else (cos_k, sin_k)
                dve.wait_ge(projected, n + 1)
                wait_count(dve, part_ready, n)
                dve.tensor_tensor(four(direct[:]), four(pair_banks[n % 3][:, 0, :]), table(cos), ALU.mult)
                dve.tensor_tensor(four(crossed[:]), four(pair_banks[n % 3][:, 1, :]), table(sin), ALU.mult)\
                   .then_inc(products, 1)
                tok = slice(h * TOK, (h + 1) * TOK)
                dve.wait_ge(part_hi, n + 1)
                if kind == "q":
                    dve.tensor_tensor(qT[:, LO, t, tok], direct[:], as_f32(qT[:, HI, t, tok]), ALU.subtract)\
                       .then_inc(part_ready, 1)
                else:
                    for par in range(2):
                        last = dve.scalar_tensor_tensor(kT[:, LO, par, tok], direct[:], parity[:, par:par + 1],
                                                        as_f32(kT[:, HI, par, tok]), ALU.mult, ALU.subtract)
                    last.then_inc(part_ready, 1)

            def step(u):
                if u + 2 < UNITS:
                    dve.wait_ge(scored, u + 3)
                    wait_count(dve, exped, u + 1)
                    scores = score_bank[:, u % 2, :].rearrange("p (i k) -> p i k", i=4)
                    out = masked_scores[:, u % 2, :].rearrange("p (i k) -> p i k", i=4)
                    dve.tensor_tensor(out, scores, causal_add[:].unsqueeze(1).broadcast_to([128, 4, S]), ALU.add)\
                       .then_inc(biased, 1)
                    dve.wait_ge(biased, u + 3)
                    dve.tensor_reduce(neg_max[:, u % 2, :], out, AX.X, ALU.max, negate=True).then_inc(maxed, 1)
                if 0 <= u < UNITS and u % 2 == 1:
                    dve.wait_ge(transposed, u + 1)
                    wait_count(dve, attended, u - 1)
                    dve.tensor_copy(probsT[:, 1, :], probsT_bank[:, 1, :]).then_inc(probsT_ready[1], 1)
                pair, stage = finishing(u)
                if stage == 0:
                    dve.wait_ge(exped, UNITS_OF_PAIR * (pair + 1))
                    dve.reciprocal(inv_sum[:], exp_sum[:, pair % 2]).then_inc(inverted, 1)
                    dve.wait_ge(inverted, pair + 1)
                    dve.wait_ge(attended, UNITS_OF_PAIR * (pair + 1))
                    for bi in range(2):
                        wait_count(dve, outT_done, 2 * pair + bi - 1)
                        dve.tensor_tensor(heads_out[:, bi, :].rearrange("p (h d) -> p h d", h=NH),
                                          out_bank[:, bi, :].rearrange("p (h d) -> p h d", h=NH),
                                          inv_sum[:, bi, :].unsqueeze(2).broadcast_to([128, NH, HW]), ALU.mult)\
                           .then_inc(out_scaled, 1)
                if stage in (1, 3):
                    dve.wait_ge(outT_hi, 2 * pair + stage // 2 + 1)
                    dve.tensor_tensor(heads_outT[:, LO, :], proj_bank[:, 0, :], as_f32(heads_outT[:, HI, :]),
                                      ALU.subtract).then_inc(outT_ready, 1)
                if stage in (2, 4):
                    n = 2 * pair + stage // 2 - 1
                    dve.wait_ge(y_done, n + 1)
                    dve.tensor_tensor(x[:, n, :], proj_bank[:, 1, :], x[:, n, :], ALU.add).then_inc(y_added, 1)
            for u in STEPS:
                step(u)

        @block.gpsimd
        def _(pool):
            norm.gpsimd(pool)
            split.gpsimd(pool, 0, N_EARLY)
            for n in range(len(tasks)):
                pool.wait_ge(products, n + 1)
                pool.tensor_tensor(direct[:], direct[:], crossed[:], ALU.add).then_inc(rotated, 1)
            split.gpsimd(pool, N_EARLY)


def decoder(nc, a, out):
    with ExitStack() as ctx:
        x = ctx.enter_context(nc.sbuf_tensor("x_stream", [128, B, D], F32))
        ident = ctx.enter_context(nc.sbuf_tensor("ident", [128, 128], F32))
        ident_loaded = ctx.enter_context(nc.semaphore("ident_loaded"))
        sems = Semaphores(nc)
        with nc.Block() as block:
            @block.sync
            def _(sp):
                sp.dma_start(ident[:], a["ident"]).then_inc(ident_loaded, 16)
                sp.wait_ge(ident_loaded, 16)
        attention(nc, sems, "a0", Plan(shared_kv=True), x, ident,
                  {"q": a["q0"], "k": a["k0"], "v": a["v0"], "o": a["o0"], "q_scales": a["q0_scales"],
                   "k_scales": a["k0_scales"], "v_scales": a["v0_scales"], "o_scales": a["o0_scales"]},
                  None, rope=(a["cos0"], a["sin0"]), causal=a["causal"], codes=True, scale=HD ** -0.5,
                  x_dram=a["x"])
        sems.clear()
        attention(nc, sems, "c0", Plan(shared_kv=False), x, ident,
                  {"q": a["cq0"], "k": a["ck0"], "v": a["cv0"], "o": a["co0"]}, a["context"],
                  pad_mask=a["mask"], position_bias=a["position_bias"], rms_weight=a["ln_weight"])
        sems.clear()
        expert_layer(nc, sems, x, ident, a["gate"], a["moe_a"], a["moe_b"])
        sems.clear()
        small_attention(nc, sems, x, ident, a["q1"], a["k1"], a["v1"], a["o1"], (a["cos1q"], a["sin1q"]),
                        (a["cos1k"], a["sin1k"]), a["causal"], a["parities"])
        sems.clear()
        attention(nc, sems, "c1", Plan(shared_kv=True), x, ident,
                  {"q": a["cq1"], "k": a["ck1"], "v": a["cv1"], "o": a["co1"]}, a["context"],
                  out_bias=a["bo1"], scale=HD ** -0.5)
        sems.clear()
        adapter_layer(nc, sems, x, ident, a["ffn_w"], a["ffn_bias"], a["ffn_a"], a["ffn_b"], a["starts"], out)


def _tables(np):
    f = np.float32
    pos = np.arange(S, dtype=f)
    inv = (f(1.0) / f(10000.0) ** (np.arange(0, HD, 2, dtype=f) / f(HD))).astype(f)
    angle = inv[:, None] * pos[None, :]
    cos0 = np.concatenate([np.cos(angle), np.cos(angle)]).astype(f)
    sin0 = np.concatenate([np.sin(angle), -np.sin(angle)]).astype(f)
    width = 16
    idx = np.arange(0, width, 2, dtype=f) / f(width)
    freq = (f(1.0 / (2.0 * np.pi)) * f(500000.0) ** (-idx)).astype(f)
    low, high, length, factor = 1.0, 4.0, 1024, 32.0
    scaled = np.where(freq < low / length, freq / f(factor), freq)
    smooth = np.clip((f(length) * freq - f(low)) / f(high - low), 0.0, 1.0).astype(f)
    mixed = (f(1.0) - smooth) * (freq / f(factor)) + smooth * freq
    freq = np.where((freq >= low / length) & (freq <= high / length), mixed, scaled).astype(f)
    phase = (f(2.0 * np.pi) * pos[:, None] * freq[None, :]).astype(f).T
    cos1 = np.tile(np.concatenate([np.cos(phase), np.cos(phase)]), (8, 1)).astype(f)
    sin1 = np.tile(np.concatenate([-np.sin(phase), np.sin(phase)]), (8, 1)).astype(f)
    causal = np.where(np.tril(np.ones((S, S), bool)), 0.0, MASKED).astype(f)
    kv = np.arange(128) // width
    parities = np.stack([kv % 2 == 0, kv % 2 == 1], axis=1).astype(f)
    quarter = f(width ** -0.5)
    return {"cos0": cos0, "sin0": sin0, "cos1q": cos1 * quarter, "sin1q": sin1 * quarter, "cos1k": cos1,
            "sin1k": sin1, "causal": causal, "ident": np.eye(128, dtype=f), "parities": parities}


def _layout(np, t):
    c = np.ascontiguousarray

    def chunks(w, heads):
        return c(w.reshape(KT, 128, heads, HD).transpose(2, 1, 0, 3).reshape(heads, 128, KT * HD))

    def rotary(w, heads):
        return w.reshape(w.shape[0], heads, HD // 2, 2).transpose(0, 1, 3, 2).reshape(w.shape[0], heads * HD)

    def scale_rows(s, heads):
        return c(s.reshape(KT, heads, HD).transpose(1, 0, 2).reshape(heads, KT * HD))

    def whole(w):
        return c(w.reshape(-1, 128, w.shape[1]).transpose(1, 0, 2))

    def with_bias(w, bias):
        return c(np.concatenate([w, bias.reshape(w.shape[0], 128, 1)], axis=2))
    wkv, bkv = t["L1_xattn_Wkv"], t["L1_xattn_bkv"]
    kv = wkv.shape[1] // 2
    context = t["ctx_4096"].transpose(2, 0, 1).reshape(KT, 128, 2, TOK)
    return {
        "x": c(t["x"]),
        "context": c(context.transpose(2, 0, 1, 3)),
        "mask": c(t["mask_BxSxS2_bk0"].transpose(1, 0, 2)),
        "q0": chunks(rotary(t["L0_attn_q_codes"], NH), NH), "k0": chunks(rotary(t["L0_attn_k_codes"], 8), 8),
        "v0": chunks(t["L0_attn_v_codes"], 8), "o0": c(t["L0_attn_o_codes"].reshape(NH, 128, D)),
        "q0_scales": scale_rows(rotary(t["L0_attn_q_scales"], NH), NH),
        "k0_scales": scale_rows(rotary(t["L0_attn_k_scales"], 8), 8),
        "v0_scales": scale_rows(t["L0_attn_v_scales"], 8), "o0_scales": c(t["L0_attn_o_scales"]),
        "position_bias": c(t["L0_xattn_position_bias"]),
        "ln_weight": c(t["L0_xattn_ln_weight"].reshape(KT, 128).T),
        "cq0": chunks(t["L0_xattn_w_q"].T, NH), "ck0": chunks(t["L0_xattn_w_k"].T, NH),
        "cv0": chunks(t["L0_xattn_w_v"].T, NH), "co0": c(t["L0_xattn_w_out"].T.reshape(NH, 128, D)),
        "gate": whole(t["L0_ffn_gate_w"].T), "moe_a": whole(t["L0_ffn_lora_A"].reshape(-1, D).T),
        "moe_b": whole(t["L0_ffn_lora_B"].transpose(0, 2, 1).reshape(-1, D)),
        "q1": whole(t["L1_attn_Wq"]), "k1": whole(t["L1_attn_Wk"]), "v1": whole(t["L1_attn_Wv"]),
        "o1": whole(t["L1_attn_Wo"]),
        "cq1": with_bias(chunks(t["L1_xattn_Wq"], NH), t["L1_xattn_bq"]),
        "ck1": with_bias(chunks(wkv[:, :kv], 8), bkv[:kv]), "cv1": with_bias(chunks(wkv[:, kv:], 8), bkv[kv:]),
        "co1": c(t["L1_xattn_Wo"].reshape(NH, 128, D)),
        "bo1": c(t["L1_xattn_bo"]),
        "ffn_w": whole(t["L1_ffn_weight"].T), "ffn_bias": c(t["L1_ffn_bias"]),
        "ffn_a": whole(t["L1_ffn_lora_A"].reshape(-1, D).T),
        "ffn_b": c(t["L1_ffn_lora_B"].transpose(0, 2, 1).reshape(-1, D)),
        "starts": c(t["L1_ffn_lora_start_indices"]),
    }


def kernel(**inputs):
    import numpy as _np
    import concourse.bacc as _bacc
    from concourse import mybir as _mybir
    from concourse.bass_utils import run_bass_kernel_spmd as _run

    arrays = _layout(_np, {name: _np.asarray(v) for name, v in inputs.items()})
    arrays.update(_tables(_np))
    nc = _bacc.Bacc("TRN2", target_bir_lowering=False, num_devices=1)
    handles = {name: nc.dram_tensor(f"in_{name}", v.shape, _mybir.dt.from_np(v.dtype), kind="ExternalInput").ap()
               for name, v in arrays.items()}
    out = nc.dram_tensor("out_x", (B, S, D), _mybir.dt.float32, kind="ExternalOutput").ap()
    decoder(nc, handles, out)
    r = _run(nc, [{f"in_{name}": v for name, v in arrays.items()}], core_ids=[0])
    return r.results[0]["out_x"]
```

```python
from contextlib import ExitStack

import numpy as np

import concourse.bass as bass
from concourse import mybir

F32 = mybir.dt.float32
F32R = mybir.dt.float32r
I32 = mybir.dt.int32
U8 = mybir.dt.uint8
ALU = mybir.AluOpType
ACT = mybir.ActivationFunctionType
AX = mybir.AxisListType

B = 8
S = 128
D = 512
KT = D // 128
NH = 32
HD = 128
HALF = 4
TOK = HALF * S
EPS = 1e-5
MASKED = -1e30
HI, LO = 0, 1


def matmul3(pe, out, stationary, moving, first, last):
    pe.matmul(out, stationary(HI), moving(HI), start=first, stop=False, skip_group_check=True)
    pe.matmul(out, stationary(HI), moving(LO), start=False, stop=False, skip_group_check=True)
    return pe.matmul(out, stationary(LO), moving(HI), start=False, stop=last, skip_group_check=True)


def wait_count(eng, sem, count):
    if isinstance(count, int) and count <= 0:
        return
    eng.wait_ge(sem, count)


class Semaphores:

    def __init__(self, nc):
        self.nc, self.handles = nc, []

    def new(self, name):
        self.handles.append(self.nc.alloc_semaphore(name=name))
        return self.handles[-1]

    def clear(self):
        self.nc.clear_and_free_semaphores(self.handles)
        self.handles = []
        self.nc.all_engine_barrier()


def as_f32(ap):
    return ap.bitcast(F32)


class Moments:

    def __init__(self, x, stats, mean_var):
        self.x, self.stats, self.mean_var = x, stats, mean_var

    def start_layer(self, sems, name):
        self.stats_taken = sems.new(f"{name}_measured")

    def batch_stats(self, dve, b, x_added, count):
        dve.wait_ge(x_added, count)
        dve.bn_stats(self.stats[:, b, :], self.x[:, b, :]).then_inc(self.stats_taken, 1)

    def mean_and_var(self, dve, batches):
        for b in batches:
            dve.wait_ge(self.stats_taken, b + 1)
            last = dve.bn_aggr(self.mean_var[:, b, :], self.stats[:, b, :])
        return last


class Norm:

    def __init__(self, ctx, sems, nc, name, moments, xT, scratch, banks, ident, rms_weight=None, rms_loaded=None):
        self.nc, self.moments, self.x, self.xT = nc, moments, moments.x, xT
        self.scratch, self.banks, self.ident = scratch, banks, ident
        self.rms_weight, self.rms_loaded = rms_weight, rms_loaded
        self.factors = 1 if rms_weight is None else 2

        def small(n, shape):
            return ctx.enter_context(nc.sbuf_tensor(f"{name}_{n}", shape, F32))

        def sem(n):
            return sems.new(f"{name}_{n}")

        self.mean_var = moments.mean_var
        self.radicand = small("radicand", [128, self.factors, B])
        self.minus_half = small("minus_half", [128, self.factors, B])
        self.factor = small("factor", [128, self.factors, B])
        if rms_weight is not None:
            self.one_plus = small("one_plus", [128, B])
            self.mean_rstd = small("mean_rstd", [128, B])
            self.update_ready = sem("update_ready")
        self.moments_ready = sem("moments_ready")
        self.var_ready = sem("var_ready")
        self.radicand_ready = sem("radicand_ready") if rms_weight is not None else self.var_ready
        self.half_set = sem("half_set")
        self.factor_ready = sem("factor_ready")
        self.normed = sem("normed")
        self.transposed = sem("transposed")
        self.hi_ready = sem("xt_hi_ready")
        self.ready = sem("xt_ready")

    def statistics(self, dve, x_ready=None):
        for h in range(2):
            if x_ready is not None:
                for b in range(h * HALF, (h + 1) * HALF):
                    self.moments.batch_stats(dve, b, x_ready[b], 16)
                self.moments.mean_and_var(dve, range(h * HALF, (h + 1) * HALF)).then_inc(self.moments_ready, 1)
                dve.wait_ge(self.moments_ready, h + 1)
            some = slice(h * HALF, (h + 1) * HALF)
            var, var_eps = self.mean_var[:, some, 1], self.radicand[:, 0, some]
            dve.tensor_scalar(var_eps, var, EPS, None, ALU.add).then_inc(self.var_ready, 1)
            if self.rms_weight is not None:
                dve.wait_ge(self.var_ready, h + 1)
                dve.scalar_tensor_tensor(self.radicand[:, 1, some], var_eps, EPS, var, ALU.mult, ALU.add)\
                   .then_inc(self.radicand_ready, 1)

    def vector(self, dve, after_batch=lambda b: None):
        if self.rms_weight is not None:
            dve.wait_ge(self.rms_loaded, 16)
        for b in range(B + 1):
            if b < B:
                if b % HALF == 0:
                    dve.wait_ge(self.factor_ready, b // HALF + 1)
                if b >= 2:
                    dve.wait_ge(self.transposed, b - 1)
                dve.tensor_scalar(self.scratch[:, b % 2, :], self.x[:, b, :], self.mean_var[:, b, 0:1],
                                  self.factor[:, self.factors - 1, b:b + 1], ALU.subtract, ALU.mult)\
                   .then_inc(self.normed, 1)
            if b >= 1:
                self.vector_low(dve, b - 1)
            after_batch(b)

    def vector_low(self, dve, b):
        bank = self.banks[:, b % 2, :].rearrange("p (k t) -> p k t", k=KT)
        tokens = slice(b * S, (b + 1) * S)
        dve.wait_ge(self.hi_ready, b + 1)
        if self.rms_weight is None:
            dve.tensor_tensor(self.xT[:, LO, :, tokens], bank, as_f32(self.xT[:, HI, :, tokens]), ALU.subtract)\
               .then_inc(self.ready, 1)
        else:
            for k in range(KT):
                last = dve.scalar_tensor_tensor(self.xT[:, LO, k, tokens], bank[:, k, :],
                                                self.rms_weight[:, k:k + 1],
                                                as_f32(self.xT[:, HI, k, tokens]), ALU.mult, ALU.subtract)
            last.then_inc(self.ready, 1)

    def update_x(self, dve):
        rstd = self.factor[:, 0, :]
        dve.tensor_scalar(self.one_plus[:], rstd, 1.0, None, ALU.add)
        dve.tensor_tensor(self.mean_rstd[:], self.mean_var[:, :, 0], rstd, ALU.mult).then_inc(self.update_ready, 1)
        dve.wait_ge(self.update_ready, 1)
        for b in range(B):
            last = dve.tensor_scalar(self.x[:, b, :], self.x[:, b, :], self.one_plus[:, b:b + 1],
                                     self.mean_rstd[:, b:b + 1], ALU.mult, ALU.subtract)
        last.then_inc(self.update_ready, 1)
        dve.wait_ge(self.update_ready, 2)

    def gpsimd(self, pool):
        pool.memset(self.minus_half[:], -0.5).then_inc(self.half_set, 1)
        pool.wait_ge(self.half_set, 1)
        for h in range(2):
            some = slice(h * HALF, (h + 1) * HALF)
            pool.wait_ge(self.radicand_ready, h + 1)
            pool.tensor_tensor(self.factor[:, :, some], self.radicand[:, :, some], self.minus_half[:, :, some],
                               ALU.pow).then_inc(self.factor_ready, 1)

    def tensor(self, pe, batches=range(B)):
        for b in batches:
            pe.wait_ge(self.normed, b + 1)
            if b >= 2:
                pe.wait_ge(self.ready, b - 1)
            for k in range(KT):
                last = pe.transpose(self.banks[:, b % 2, k * 128:(k + 1) * 128],
                                    self.scratch[:, b % 2, k * 128:(k + 1) * 128], self.ident[:])
            last.then_inc(self.transposed, 1)

    def scalar(self, act, batches=range(B)):
        if self.rms_weight is not None and batches[0] == 0:
            act.wait_ge(self.rms_loaded, 16)
        for b in batches:
            act.wait_ge(self.transposed, b + 1)
            bank = self.banks[:, b % 2, :].rearrange("p (k t) -> p k t", k=KT)
            tokens = slice(b * S, (b + 1) * S)
            if self.rms_weight is None:
                act.activation(self.xT[:, HI, :, tokens], bank, ACT.Copy).then_inc(self.hi_ready, 1)
            else:
                for k in range(KT):
                    last = act.activation(self.xT[:, HI, k, tokens], bank[:, k, :], ACT.Copy,
                                          scale=self.rms_weight[:, k:k + 1])
                last.then_inc(self.hi_ready, 1)


class Plan:

    PER_HALF = 6

    def __init__(self, shared_kv):
        self.shared_kv = shared_kv
        if shared_kv:
            self.heads, self.kv_heads, self.unit_batches = 4, 1, 1
            self.tasks = [("q", 0), ("k", 0), ("q", 1), ("q", 2), ("q", 3), ("v", 0)]
            self.phases = [[0, 1], [2, 3], [4], [5]]
            self.splits = {1: [("q", 0), ("k", 0)], 2: [("q", 1)], 3: [("q", 2)], 4: [("q", 3), ("v", 0)],
                           5: [("o", 0)], 6: [("o", 1), ("o", 2)], 7: [("o", 3)]}
        else:
            self.heads, self.kv_heads, self.unit_batches = 2, 2, 2
            self.tasks = [("q", 0), ("k", 0), ("q", 1), ("k", 1), ("v", 0), ("v", 1)]
            self.phases = [[0, 1, 2], [3, 4, 5]]
            self.splits = {0: [("q", 0), ("k", 0), ("q", 1)], 1: [("k", 1), ("v", 0), ("v", 1)],
                           2: [("o", 0)], 3: [("o", 1)]}
        self.groups = NH // self.heads
        self.half_units = HALF // self.unit_batches
        self.group_units = 2 * self.half_units
        self.units = self.groups * self.group_units
        self.order = [c for j in sorted(self.splits) for c in self.splits[j]]
        self.chunks = len(self.order)
        self.slots = self.chunks // 2
        self.first_step = self.group_units - self.half_units - 1
        self.qk_per_half = sum(kind != "v" for kind, _ in self.tasks)

    def chunk_number(self, chunk, cycle):
        return self.chunks * (cycle + 1) + self.order.index(chunk)

    def chunk_slot(self, chunk):
        return self.order.index(chunk) % self.slots

    def pairs(self, j):
        first = (j % self.half_units) * self.unit_batches
        if self.shared_kv:
            return [(first, h) for h in range(self.heads)]
        return [(first + b, h) for b in range(self.unit_batches) for h in range(self.heads)]

    def half_of(self, j):
        return (j // self.half_units) % 2

    def target(self, j):
        return (j + 1) // self.half_units + 1, self.phases[(j + 1) % self.half_units]

    def bank_of(self, task):
        return task % 3


def each_step(eng, plan, step):
    for j in range(plan.first_step, plan.group_units):
        step(-1, j, True, 1)
    for j in range(plan.group_units):
        step(0, j, True, 0)
    with eng.Fori(0, plan.groups // 2 - 1) as turn:
        for odd in (1, 0):
            for j in range(plan.group_units):
                step(turn * 2 + (2 - odd), j, False, odd)
    for j in range(plan.group_units):
        step(plan.groups - 1, j, True, (plan.groups - 1) % 2)
    step(plan.groups, 0, True, plan.groups % 2)


def attention(nc, sems, name, plan, moments, ident, weights, source, rope=None, causal=None, pad_mask=None,
              position_bias=None, rms_weight=None, codes=False, out_bias=None,
              scale=1.0, x_dram=None, ident_dram=None):
    P, x = plan, moments.x
    H, NK, BU, UG, UH = P.heads, P.kv_heads, P.unit_batches, P.group_units, P.half_units
    with_biases = out_bias is not None
    masked = causal is not None or pad_mask is not None
    with ExitStack() as ctx:
        def sb(n, shape, dt=F32):
            return ctx.enter_context(nc.sbuf_tensor(f"{name}_{n}", shape, dt))

        def pb(n, shape):
            return ctx.enter_context(nc.psum_tensor(f"{name}_{n}", shape, F32))

        def sem(n):
            return sems.new(f"{name}_{n}")

        xT = sb("xT", [128, 2, KT, B * S], F32R)
        scratch = sb("scratch", [128, 2, D])
        probs = scratch[:, 0, :]
        masked_scores = scratch[:, 1, :]
        w_q = sb("w_q", [128, 2, H, D], F32R)
        w_k = sb("w_k", [128, 2, NK, D], F32R)
        w_v = sb("w_v", [128, 2, NK, D], F32R)
        w_o = sb("w_o", [128, 2, 2, H, D], F32R)

        def weight(kind, i, part, odd):
            if kind == "o":
                return w_o[:, part, 1 - odd, i, :]
            return {"q": w_q, "k": w_k, "v": w_v}[kind][:, part, i, :]
        staged = sb("staged", [128, P.slots, D + with_biases], I32 if codes else F32)
        qT = sb("qT", [128, 2, 2, H, TOK], F32R)
        kT = sb("kT", [128, 2, 2, NK, TOK], F32R)
        v_tok = sb("v_tok", [128, 2, 2, HALF, NK * HD], F32R)
        probsT = sb("probsT", [128, 2, TOK], F32R)
        outT = sb("outT", [128, 2, TOK], F32R)
        vT = [sb(f"vT{i}", [128, TOK])[:] for i in range(NK)] if masked else [scratch[:, 1, :]]
        neg_max = sb("neg_max", [128, 4])
        exp_bias = sb("exp_bias", [128, 4]) if scale != 1.0 else neg_max
        exp_sum = sb("exp_sum", [128, 4])
        inv_sum = sb("inv_sum", [128, 4])

        proj_bank = pb("proj_bank", [128, 3, 512])
        score_bank = pb("score_bank", [128, 512])
        probsT_bank = pb("probsT_bank", [128, 512])
        outT_bank = pb("outT_bank", [128, 512])
        out_bank = pb("out_bank", [128, 2, 512])

        rms_cols = sb("rms_cols", [128, KT]) if rms_weight is not None else None
        rms_loaded = sem("rms_loaded") if rms_weight is not None else None
        norm = Norm(ctx, sems, nc, f"{name}_norm", moments, xT, scratch, out_bank, ident, rms_cols, rms_loaded)

        chunk_loaded = [sem(f"chunk_loaded{i}") for i in range(P.slots)]
        chunk_hi = sem("chunk_hi")
        chunk_ready = sem("chunk_ready")
        projected = sem("projected")
        v_projected = sem("v_projected")
        v_copied = sem("v_copied")
        task_hi = sem("task_hi")
        task_read = sem("task_read")
        scored = sem("scored")
        biased = sem("biased")
        row_max = sem("row_max")
        bias_ready = sem("exp_bias_ready") if scale != 1.0 else row_max
        exped = sem("exped")
        summed = sem("sum_inverted")
        inv_ready = sem("inv_ready") if pad_mask is not None else summed
        probs_ready = sem("probs_ready")
        probs_transposed = sem("probs_transposed")
        probsT_hi = sem("probsT_hi")
        probsT_ready = sem("probsT_ready")
        attended = sem("attended")
        outT_hi = sem("outT_hi")
        outT_ready = sem("outT_ready")
        out_done = sem("out_done")
        out_added = sem("out_added")
        x_loaded = [sem(f"x_loaded{b}") for b in range(B)] if x_dram is not None else None
        ident_loaded = sem("ident_loaded") if ident_dram is not None else None
        const_loaded = sem("const_loaded")
        dmas_of_chunk = 2 if codes else 1
        if codes:
            scales = sb("scales", [128, P.slots, D])
            dequantized = sem("dequantized")
        if rope is not None:
            cosine, sine = sb("cosine", [128, S]), sb("sine", [128, S])
            direct = sb("direct", [128, 2, TOK])
            crossed = sb("crossed", [128, 2, TOK])
            rotated, qk_ready = sem("rotated"), sem("qk_ready")
        if causal is not None:
            causal_add = sb("causal_add", [128, S])
        if with_biases:
            columns = {"q": sb("bias_q", [128, H]), "k": sb("bias_k", [128, NK]), "v": sb("bias_v", [128, NK])}
            bias_o = scratch[:, 0, :]
            out_bias_loaded, out_biased = sem("out_bias_loaded"), sem("out_biased")
        if pad_mask is not None:
            mask_bytes = sb("mask_bytes", [128, B, S], U8)
            pad_add = sb("pad_add", [128, B, S])
            row_any = sb("row_any", [128, B])
            head_bias = sb("head_bias", [128, H, S])
            mask_ready, head_bias_loaded = sem("mask_ready"), sem("head_bias_loaded")
        if source is not None:
            kvT = sb("kvT", [128, 2, KT, B * S], F32R)
            context_loaded = [sem(f"context_loaded{n}") for n in range(2 * KT)]
            context_hi, context_ready = sem("context_hi"), sem("context_ready")
        else:
            kvT = xT

        if source is not None:
            if pad_mask is not None:
                context_ring = vT + [pad_add[:, h * HALF:(h + 1) * HALF, :].rearrange("p b k -> p (b k)")
                                     for h in range(2)]
            else:
                context_ring = [staged[:, slot, 0:TOK] for slot in range(len(P.splits[1] + P.splits[2]), P.slots)]
            RING = len(context_ring)
            LATE = P.first_step if pad_mask is not None else max(
                j for j in P.splits if P.order.index(P.splits[j][-1]) < P.slots + 2)

        def late_context(g, j, fixed):
            return source is not None and fixed and g < 0 and j == LATE

        def context_piece(n):
            return context_ring[n % RING], (n % KT, slice(n // KT * TOK, (n // KT + 1) * TOK))
        n_consts = 2 * (rope is not None) + (causal is not None) + (pad_mask is not None)

        moments.start_layer(sems, name)
        next_moments = Moments(x, moments.stats, moments.mean_var)
        next_moments.start_layer(sems, name + "_next")
        block = ctx.enter_context(nc.Block())

        def unit_there(s, fixed):
            return not fixed or 0 <= s < P.units

        def half_there(h, fixed):
            return not fixed or 0 <= h < 2 * P.groups

        def splits_at(g, j, fixed):
            for kind, i in P.splits.get(j, []):
                of = g + 1
                if fixed and not 0 <= of < P.groups:
                    continue
                yield kind, i, P.chunk_number((kind, i), g), P.chunk_slot((kind, i)), of

        def first_splits():
            for j in sorted(P.splits):
                if j < P.first_step:
                    for kind, i in P.splits[j]:
                        yield kind, i, P.chunk_number((kind, i), -1), P.chunk_slot((kind, i)), 0

        def tasks_at(g, j, fixed):
            ahead, places = P.target(j)
            half = 2 * g + ahead
            if not half_there(half, fixed):
                return
            for k in places:
                yield P.tasks[k][0], P.tasks[k][1], k, half, P.PER_HALF * half + k, ahead % 2

        def last_task_use(kind, i, of):
            return P.PER_HALF * (2 * of - 1) + P.tasks.index((kind, i)) + 1

        def chunk_load_count(kind, i, cycle):
            return 16 * dmas_of_chunk * (2 * (cycle + 1) + P.order.index((kind, i)) // P.slots + 1)

        def turns_at(g, j, fixed):
            half = 2 * g + j // UH + 1
            if (j + 1) % UH == 0 and half_there(half, fixed):
                for k, (kind, i) in enumerate(P.tasks):
                    if kind == "v":
                        yield kind, i, k, half, P.PER_HALF * half + k, (j // UH + 1) % 2

        def qk_place(k):
            return [n for n, task in enumerate(P.tasks) if task[0] != "v"].index(k)

        def ring_of(k, slot):
            return (P.qk_per_half * slot + qk_place(k)) % 2

        @block.sync
        def _(sp):
            def load(kind, i, number, slot, of):
                wait_count(sp, chunk_ready, number - P.slots + 1)
                per_group = H if kind in "qo" else NK
                at = of * per_group + i
                width = weights[kind].shape[2]
                sp.dma_start(staged[:, slot, 0:width], weights[kind][bass.ds(at, 1)].rearrange("o p n -> (o p) n"))\
                  .then_inc(chunk_loaded[slot], 16)
                if codes:
                    sp.dma_start(scales[:, slot, :], weights[kind + "_scales"][bass.ds(at, 1)]
                                 .rearrange("o n -> (o n)").partition_broadcast(128))\
                      .then_inc(chunk_loaded[slot], 16)

            if x_dram is not None:
                for b in range(B):
                    if b == HALF:
                        sp.dma_start(ident[:], ident_dram).then_inc(ident_loaded, 16)
                    sp.dma_start(x[:, b, :], x_dram[b]).then_inc(x_loaded[b], 16)
            def load_context(h):
                for n in range(h * KT, (h + 1) * KT):
                    wait_count(sp, context_ready, n - RING + 1)
                    sp.dma_start(context_piece(n)[0], source[n // KT, n % KT]).then_inc(context_loaded[n], 16)

            for args in first_splits():
                load(*args)
            if rms_weight is not None:
                sp.dma_start(rms_cols[:], rms_weight).then_inc(rms_loaded, 16)
            if source is not None:
                load_context(0)
                if pad_mask is None:
                    sp.wait_ge(context_ready, KT)
            if rope is not None:
                sp.dma_start(cosine[:], rope[0]).then_inc(const_loaded, 16)
                sp.dma_start(sine[:], rope[1]).then_inc(const_loaded, 16)
            if causal is not None:
                sp.dma_start(causal_add[:], causal).then_inc(const_loaded, 16)
            if pad_mask is not None:
                sp.dma_start(mask_bytes[:], pad_mask).then_inc(const_loaded, 16)

            def load_head_bias(g):
                wait_count(sp, biased, 2 * UG * g)
                sp.dma_start(head_bias[:], position_bias[bass.ds(g * H, H)].rearrange("h q k -> q h k"))\
                  .then_inc(head_bias_loaded, 16)

            if position_bias is not None:
                load_head_bias(0)

            def step(g, j, fixed, odd):
                for args in splits_at(g, j, fixed):
                    load(*args)
                if late_context(g, j, fixed):
                    if pad_mask is None:
                        sp.wait_ge(chunk_ready, P.slots)
                    load_context(1)
                    if pad_mask is None:
                        sp.wait_ge(context_ready, 2 * KT)
                if fixed and g < 0 and j == P.first_step and out_bias is not None:
                    sp.wait_ge(norm.transposed, B)
                    sp.dma_start(bias_o, out_bias.partition_broadcast(128)).then_inc(out_bias_loaded, 16)
                if position_bias is not None and j == UG - 1 and (not fixed or 0 <= g < P.groups - 1):
                    load_head_bias(g + 1)
            each_step(sp, P, step)

        @block.tensor
        def _(pe):
            if ident_dram is not None:
                pe.wait_ge(ident_loaded, 16)
            norm.tensor(pe, range(HALF))

            def step(g, j, fixed, odd):
                s = g * UG + j
                if unit_there(s, fixed):
                    wait_count(pe, probs_ready, s + 1)
                    for i in range(4):
                        last = pe.transpose(probsT_bank[:, i * S:(i + 1) * S], probs[:, i * S:(i + 1) * S], ident[:])
                    last.then_inc(probs_transposed, 1)
                if unit_there(s + 1, fixed):
                    j1 = (j + 1) % UG
                    g1 = g + (j + 1) // UG
                    if j1 % UH == 0:
                        half = 2 * g1 + P.half_of(j1)
                        if rope is not None:
                            wait_count(pe, qk_ready, P.qk_per_half * (half + 1))
                        else:
                            wait_count(pe, task_read, P.PER_HALF * half + P.qk_per_half)
                    slot = P.half_of(j1)
                    for i, (b, h) in enumerate(P.pairs(j1)):
                        tok = slice(b * S, (b + 1) * S)
                        last = matmul3(pe, score_bank[:, i * S:(i + 1) * S], lambda p: qT[:, p, slot, h, tok],
                                       lambda p: kT[:, p, slot, 0 if P.shared_kv else h, tok], True, True)
                    last.then_inc(scored, 1)
                if unit_there(s - 1, fixed):
                    wait_count(pe, outT_ready, s)
                    if j == 1:
                        wait_count(pe, chunk_ready, P.chunk_number(("o", H - 1), g - 1) + 1)
                    slot = odd if j > 0 else 1 - odd
                    pairs = P.pairs((j - 1) % UG)
                    for bi in range(BU):
                        number = (s - 1) * BU + bi
                        bank = (j - 1 + bi) % 2 if BU == 1 else bi
                        wait_count(pe, out_added, number - 1)
                        mine = [i for i, (b, h) in enumerate(pairs) if b == pairs[0][0] + bi]
                        for n, i in enumerate(mine):
                            h = pairs[i][1]
                            last = matmul3(pe, out_bank[:, bank, :], lambda p: outT[:, p, i * S:(i + 1) * S],
                                           lambda p: w_o[:, p, slot, h, :], n == 0, n == len(mine) - 1)
                        last.then_inc(out_done, 1)
                if unit_there(s, fixed):
                    wait_count(pe, probsT_ready, s + 1)
                    slot = P.half_of(j)
                    if j % UH == 0:
                        wait_count(pe, task_read, P.PER_HALF * (2 * g + slot + 1))
                    if P.shared_kv:
                        b = P.pairs(j)[0][0]
                        last = matmul3(pe, outT_bank[:], lambda p: v_tok[:, p, slot, b, :],
                                       lambda p: probsT[:, p, :], True, True)
                    else:
                        for i, (b, h) in enumerate(P.pairs(j)):
                            last = matmul3(pe, outT_bank[:, i * S:(i + 1) * S],
                                           lambda p: v_tok[:, p, slot, b, h * HD:(h + 1) * HD],
                                           lambda p: probsT[:, p, i * S:(i + 1) * S], True, True)
                    last.then_inc(attended, 1)
                for kind, i, k, half, number, slot in turns_at(g, j, fixed):
                    wait_count(pe, v_copied, P.kv_heads * half + i + 1)
                    for b in range(HALF):
                        last = pe.transpose(proj_bank[:, P.bank_of(k), b * S:(b + 1) * S],
                                            vT[i][:, b * S:(b + 1) * S], ident[:])
                    last.then_inc(projected, 1)
                for kind, i, k, half, number, slot in tasks_at(g, j, fixed):
                    bank = proj_bank[:, P.bank_of(k), :]
                    wait_count(pe, task_read, number - 2)
                    if slot == 0:
                        of = g + P.target(j)[0] // 2
                        wait_count(pe, chunk_ready, P.chunk_number((kind, i), of - 1) + 1)
                    if fixed and half < 2:
                        if k == 0:
                            pe.wait_ge(norm.ready, HALF * (half + 1))
                        if source is not None and k == 1:
                            pe.wait_ge(context_ready, KT * (half + 1))
                    src, w = {"q": (xT, w_q), "k": (kvT, w_k), "v": (kvT, w_v)}[kind]
                    for kt in range(KT):
                        last = matmul3(pe, bank, lambda p: w[:, p, i, kt * 128:(kt + 1) * 128],
                                       lambda p: src[:, p, kt, slot * TOK:(slot + 1) * TOK], kt == 0, kt == KT - 1)
                    last.then_inc(v_projected if kind == "v" else projected, 1)
                    if fixed and g < 0 and j == P.first_step and k < 2:
                        norm.tensor(pe, range(HALF + 2 * k, HALF + 2 * k + 2))
            each_step(pe, P, step)

        def v_part(part, slot, i):
            return v_tok[:, part, slot, :, i * HD:(i + 1) * HD]

        def v_bank(k):
            return proj_bank[:, P.bank_of(k), :].rearrange("p (b n) -> p b n", n=HD)

        @block.scalar
        def _(act):
            def split_high(args, cycle, odd):
                kind, i, number, slot, of = args
                if kind == "o":
                    wait_count(act, out_done, cycle * UG * BU)
                else:
                    wait_count(act, projected, last_task_use(kind, i, of))
                if codes:
                    wait_count(act, dequantized, number + 1)
                else:
                    act.wait_ge(chunk_loaded[slot], chunk_load_count(kind, i, cycle))
                raw = as_f32(staged[:, slot, 0:D]) if codes else staged[:, slot, 0:D]
                if with_biases and kind != "o":
                    wait_count(act, task_read, last_task_use(kind, i, of))
                    act.activation(columns[kind][:, i:i + 1], staged[:, slot, D:D + 1], ACT.Copy)
                act.activation(weight(kind, i, HI, odd), raw, ACT.Copy).then_inc(chunk_hi, 1)

            def split_all(chunks, cycle, odd):
                for args in chunks:
                    split_high(args, cycle, odd)

            if not codes:
                split_all(list(first_splits()), -1, 1)

            def split_context(h):
                for n in range(h * KT, (h + 1) * KT):
                    raw, (k, tokens) = context_piece(n)
                    act.wait_ge(context_loaded[n], 16)
                    act.activation(kvT[:, HI, k, tokens], raw, ACT.Copy).then_inc(context_hi, 1)

            for b in range(HALF):
                norm.scalar(act, [b])
                if codes and b >= 1:
                    split_all(list(first_splits())[b - 1:b], -1, 1)
            if source is not None:
                split_context(0)
            norm.scalar(act, range(HALF, B))

            def tasks_high(g, j, fixed):
                for kind, i, k, half, number, slot in tasks_at(g, j, fixed):
                    bank = proj_bank[:, P.bank_of(k), :]
                    if kind in "qk":
                        out = (qT if kind == "q" else kT)[:, HI, slot, i, :]
                        if rope is not None:
                            act.wait_ge(rotated, P.qk_per_half * half + qk_place(k) + 1)
                            act.activation(out, direct[:, ring_of(k, slot), :], ACT.Copy)\
                               .then_inc(task_hi, 1)
                            continue
                        act.wait_ge(projected, number + 1)
                        done = task_hi
                    else:
                        out, done = vT[i], v_copied
                        act.wait_ge(v_projected, P.kv_heads * half + i + 1)
                        if pad_mask is not None and fixed and half == 0:
                            act.wait_ge(context_ready, 2 * KT)
                    if with_biases:
                        act.activation(out, bank, ACT.Identity, bias=columns[kind][:, i:i + 1]).then_inc(done, 1)
                    else:
                        act.activation(out, bank, ACT.Copy).then_inc(done, 1)

            def step(g, j, fixed, odd):
                s = g * UG + j
                before = fixed and g < 0 and j < P.first_step + 2
                if before:
                    split_all(list(splits_at(g, j, fixed)), g, odd)
                if unit_there(s, fixed):
                    act.wait_ge(probs_transposed, s + 1)
                    act.activation(probsT[:, HI, :], probsT_bank[:], ACT.Copy).then_inc(probsT_hi, 1)
                if rope is not None:
                    tasks_high(g - (j == 0), (j - 1) % UG, fixed)
                if unit_there(s + 1, fixed):
                    wait_count(act, bias_ready, s + 2)
                    scores = masked_scores if masked else score_bank[:]
                    for i in range(4):
                        last = act.activation(probs[:, i * S:(i + 1) * S], scores[:, i * S:(i + 1) * S], ACT.Exp,
                                              bias=exp_bias[:, i:i + 1], scale=scale, accum_out=exp_sum[:, i:i + 1])
                    last.then_inc(exped, 1)
                for kind, i, k, half, number, slot in turns_at(g, j, fixed):
                    act.wait_ge(projected, number + 1)
                    act.activation(v_part(HI, slot, i), v_bank(k), ACT.Copy).then_inc(task_hi, 1)
                if unit_there(s, fixed):
                    act.wait_ge(attended, s + 1)
                    wait_count(act, out_done, s * BU)
                    act.activation(outT[:, HI, :], outT_bank[:], ACT.Copy).then_inc(outT_hi, 1)
                if rope is None:
                    tasks_high(g, j, fixed)
                if not before:
                    split_all(list(splits_at(g, j, fixed)), g, odd)
                if late_context(g, j, fixed):
                    split_context(1)
            each_step(act, P, step)

        @block.vector
        def _(dve):
            def dequantize(chunks, cycle):
                for kind, i, number, slot, of in chunks:
                    dve.wait_ge(chunk_loaded[slot], chunk_load_count(kind, i, cycle))
                    dve.scalar_tensor_tensor(as_f32(staged[:, slot, :]), staged[:, slot, :], 8.0, scales[:, slot, :],
                                              ALU.subtract, ALU.mult).then_inc(dequantized, 1)

            norm.statistics(dve, x_loaded)
            norm.vector(dve, lambda b: dequantize(list(first_splits())[b - 1:b] if codes and b >= 1 else [], -1))

            def set_up_mask():
                dve.wait_ge(context_ready, 2 * KT)
                dve.tensor_scalar(pad_add[:], mask_bytes[:], 1.0, -MASKED, ALU.subtract, ALU.mult)
                dve.tensor_reduce(row_any[:], mask_bytes[:], AX.X, ALU.max).then_inc(mask_ready, 1)
                dve.wait_ge(mask_ready, 1)

            wait_count(dve, const_loaded, 16 * n_consts)

            def first_batch(j):
                return P.half_of((j - 1) % UG) * HALF + P.pairs((j - 1) % UG)[0][0]

            def add_output(g, j, fixed):
                s = g * UG + j
                if unit_there(s - 1, fixed):
                    first = first_batch(j)
                    for bi in range(BU):
                        bank = (j - 1 + bi) % 2 if BU == 1 else bi
                        dve.wait_ge(out_done, (s - 1) * BU + bi + 1)
                        xb = x[:, first + bi, :]
                        dve.tensor_tensor(xb, out_bank[:, bank, :], xb, ALU.add).then_inc(out_added, 1)

            def step(g, j, fixed, odd):
                s = g * UG + j
                before = fixed and g < 0 and j < P.first_step + 2
                if codes and before:
                    dequantize(list(splits_at(g, j, fixed)), g)
                if unit_there(s, fixed):
                    dve.wait_ge(probsT_hi, s + 1)
                    dve.tensor_tensor(probsT[:, LO, :], probsT_bank[:], as_f32(probsT[:, HI, :]), ALU.subtract)\
                       .then_inc(probsT_ready, 1)
                if unit_there(s + 1, fixed):
                    j1 = (j + 1) % UG
                    pairs = P.pairs(j1)
                    batch = P.half_of(j1) * HALF + pairs[0][0]
                    dve.wait_ge(scored, s + 2)
                    scores = score_bank[:].rearrange("p (i k) -> p i k", i=4)
                    out = masked_scores.rearrange("p (i k) -> p i k", i=4)
                    if causal is not None:
                        dve.tensor_tensor(out, scores, causal_add[:].unsqueeze(1).broadcast_to([128, 4, S]), ALU.add)\
                           .then_inc(biased, 1)
                        dve.wait_ge(biased, s + 2)
                        scores = out
                    if pad_mask is not None:
                        if j1 == 0:
                            dve.wait_ge(head_bias_loaded, 16 * (g + (j + 1) // UG + 1))
                        b4 = [128, BU, H, S]
                        dve.tensor_tensor(out.rearrange("p (b h) k -> p b h k", b=BU),
                                          scores.rearrange("p (b h) k -> p b h k", b=BU),
                                          head_bias[:].unsqueeze(1).broadcast_to(b4), ALU.add).then_inc(biased, 1)
                        wait_count(dve, biased, 2 * s + 3)
                        o4 = out.rearrange("p (b h) k -> p b h k", b=BU)
                        dve.tensor_tensor(o4, o4, pad_add[:, batch:batch + BU, :].unsqueeze(2).broadcast_to(b4),
                                          ALU.add).then_inc(biased, 1)
                        dve.wait_ge(biased, 2 * s + 4)
                        scores = out
                    dve.tensor_reduce(neg_max[:], scores, AX.X, ALU.max, negate=True).then_inc(row_max, 1)
                    if scale != 1.0:
                        dve.wait_ge(row_max, s + 2)
                        dve.tensor_scalar(exp_bias[:], neg_max[:], scale, None, ALU.mult).then_inc(bias_ready, 1)
                closing = P.shared_kv and fixed and g >= P.groups - 1
                if not closing:
                    add_output(g, j, fixed)
                if codes and not before:
                    dequantize(list(splits_at(g, j, fixed)), g)
                if unit_there(s + 1, fixed):
                    dve.wait_ge(exped, s + 2)
                    dve.reciprocal(inv_sum[:], exp_sum[:]).then_inc(summed, 1)
                    if pad_mask is not None:
                        dve.wait_ge(summed, s + 2)
                        inv2 = inv_sum[:].rearrange("p (b h) -> p b h", b=BU)
                        dve.tensor_tensor(inv2, inv2, row_any[:, batch:batch + BU].unsqueeze(2)
                                          .broadcast_to([128, BU, H]), ALU.mult).then_inc(inv_ready, 1)
                    wait_count(dve, inv_ready, s + 2)
                    dve_probs = probs.rearrange("p (i k) -> p i k", i=4)
                    dve.tensor_tensor(dve_probs, dve_probs, inv_sum[:].unsqueeze(2).broadcast_to([128, 4, S]),
                                      ALU.mult).then_inc(probs_ready, 1)
                if closing:
                    add_output(g, j, fixed)
                for kind, i, k, half, number, slot in turns_at(g, j, fixed):
                    dve.wait_ge(task_hi, number + 1)
                    dve.tensor_tensor(v_part(LO, slot, i), v_bank(k), as_f32(v_part(HI, slot, i)),
                                      ALU.subtract).then_inc(task_read, 1)
                if unit_there(s, fixed):
                    dve.wait_ge(outT_hi, s + 1)
                    dve.tensor_tensor(outT[:, LO, :], outT_bank[:], as_f32(outT[:, HI, :]), ALU.subtract)\
                       .then_inc(outT_ready, 1)
                if fixed and (P.groups - 1) * UG <= s - 1 < P.units:
                    first = first_batch(j)
                    for bi in range(BU):
                        next_moments.batch_stats(dve, first + bi, out_added, (s - 1) * BU + bi + 1)
                for kind, i, k, half, number, slot in tasks_at(g, j, fixed):
                    bank = proj_bank[:, P.bank_of(k), :]
                    if kind in "qk" and rope is not None:
                        ring = ring_of(k, slot)
                        wait_count(dve, qk_ready, P.qk_per_half * half + qk_place(k) - 1)
                        dve.wait_ge(projected, number + 1)

                        def four(ap):
                            return ap.rearrange("p (b t) -> p b t", b=HALF)
                        for a, z, out in ((0, 128, direct), (64, 128, crossed), (0, 64, crossed)):
                            to = (a, z) if out is direct else ((a + 64) % 128, (a + 64) % 128 + 64)
                            table = cosine if out is direct else sine
                            last = dve.tensor_tensor(four(out[to[0]:to[1], ring, :]), four(bank[a:z]),
                                                     table[a:z, :].unsqueeze(1).broadcast_to([z - a, HALF, S]),
                                                     ALU.mult)
                        last.then_inc(task_read, 1)
                        continue
                    if kind == "v":
                        continue
                    dve.wait_ge(task_hi, number + 1)
                    out = qT if kind == "q" else kT
                    if with_biases:
                        dve.scalar_tensor_tensor(out[:, LO, slot, i, :], bank, columns[kind][:, i:i + 1],
                                                 as_f32(out[:, HI, slot, i, :]), ALU.add, ALU.subtract)\
                           .then_inc(task_read, 1)
                    else:
                        dve.tensor_tensor(out[:, LO, slot, i, :], bank, as_f32(out[:, HI, slot, i, :]),
                                          ALU.subtract).then_inc(task_read, 1)
                if fixed and g < 0 and j == P.first_step and rms_weight is not None:
                    norm.update_x(dve)
                if fixed and g < 0 and j == P.first_step + 1 and pad_mask is not None:
                    set_up_mask()
                if fixed and g < 0 and j < P.first_step + 2 and out_bias is not None:
                    h = j - P.first_step
                    dve.wait_ge(out_bias_loaded, 16)
                    for b in range(h * HALF, (h + 1) * HALF):
                        last = dve.tensor_tensor(x[:, b, :], x[:, b, :], bias_o, ALU.add)
                    last.then_inc(out_biased, 1)
                    dve.wait_ge(out_biased, h + 1)
            each_step(dve, P, step)
            next_moments.mean_and_var(dve, range(B))

        @block.gpsimd
        def _(pool):
            def split_low(args, odd):
                kind, i, number, slot, of = args
                raw = as_f32(staged[:, slot, 0:D]) if codes else staged[:, slot, 0:D]
                wait_count(pool, chunk_hi, number + 1)
                pool.tensor_tensor(weight(kind, i, LO, odd), raw, as_f32(weight(kind, i, HI, odd)), ALU.subtract)\
                    .then_inc(chunk_ready, 1)

            norm.gpsimd(pool)
            for args in first_splits():
                split_low(args, 1)

            def split_context(h):
                for n in range(h * KT, (h + 1) * KT):
                    raw, (k, tokens) = context_piece(n)
                    pool.wait_ge(context_hi, n + 1)
                    pool.tensor_tensor(kvT[:, LO, k, tokens], raw, as_f32(kvT[:, HI, k, tokens]),
                                       ALU.subtract).then_inc(context_ready, 1)

            if source is not None:
                split_context(0)

            def rotate_low(g, j, fixed):
                for kind, i, k, half, number, slot in tasks_at(g, j, fixed):
                    if kind in "qk":
                        out = qT if kind == "q" else kT
                        pool.wait_ge(task_hi, number + 1)
                        pool.tensor_tensor(out[:, LO, slot, i, :], direct[:, ring_of(k, slot), :],
                                           as_f32(out[:, HI, slot, i, :]), ALU.subtract).then_inc(qk_ready, 1)

            def split_chunks(g, j, fixed, odd):
                for args in splits_at(g, j, fixed):
                    split_low(args, odd)

            def step(g, j, fixed, odd):
                before = fixed and g < 0 and j < P.first_step + 2
                if before:
                    split_chunks(g, j, fixed, odd)
                if rope is not None:
                    rotate_low(g - (j == 0), (j - 1) % UG, fixed)
                    for kind, i, k, half, number, slot in tasks_at(g, j, fixed):
                        if kind in "qk":
                            ring = ring_of(k, slot)
                            pool.wait_ge(task_read, number + 1)
                            pool.tensor_tensor(direct[:, ring, :], direct[:, ring, :], crossed[:, ring, :], ALU.add)\
                                .then_inc(rotated, 1)
                if not before:
                    split_chunks(g, j, fixed, odd)
                if late_context(g, j, fixed):
                    split_context(1)
            each_step(pool, P, step)


class Splitter:

    def __init__(self, sems, nc, name):
        self.pieces = []
        self.high_done = sems.new(f"{name}_weight_hi")
        self.ready = sems.new(f"{name}_weight_ready")

    def add(self, loaded, count, raw, high, low):
        self.pieces.append((loaded, count, raw, high, low))

    def scalar(self, act, first=0, end=None):
        for loaded, count, raw, high, _ in self.pieces[first:end]:
            act.wait_ge(loaded, count)
            act.activation(high, raw, ACT.Copy).then_inc(self.high_done, 1)

    def gpsimd(self, pool, first=0, end=None):
        for n, (_, _, raw, high, low) in list(enumerate(self.pieces))[first:end]:
            pool.wait_ge(self.high_done, n + 1)
            pool.tensor_tensor(low, raw, as_f32(high), ALU.subtract).then_inc(self.ready, 1)


def expert_layer(nc, sems, moments, ident, gate_w, lora_a, lora_b):
    name, E, x = "moe", 8, moments.x
    with ExitStack() as ctx:
        def sb(n, shape, dt=F32):
            return ctx.enter_context(nc.sbuf_tensor(f"{name}_{n}", shape, dt))

        def pb(n, shape):
            return ctx.enter_context(nc.psum_tensor(f"{name}_{n}", shape, F32))

        def sem(n):
            return sems.new(f"{name}_{n}")

        xT = sb("xT", [128, 2, KT, B * S], F32R)
        scratch = sb("scratch", [128, 2, D])
        gate_raw, gate = sb("gate_raw", [128, KT, E]), sb("gate", [128, 2, KT, E], F32R)
        a_raw, a = sb("a_raw", [128, KT, D]), sb("a", [128, 2, KT, D], F32R)
        b_raw, b_w = sb("b_raw", [128, KT, D]), sb("b_w", [128, 2, KT, D], F32R)
        rank_first = sb("rank_first", [128, B, E])
        shifted, prob = sb("shifted", [128, B, E]), sb("prob", [128, B, E])
        equal, key, rest = sb("equal", [128, B, E]), sb("key", [128, B, E]), sb("rest", [128, B, E])
        chosen = [sb("chosen0", [128, B, E]), sb("chosen1", [128, B, E])]
        expert_weight = sb("expert_weight", [128, B, E])
        best = [sb("best0", [128, B]), sb("best1", [128, B])]
        top, total, inverse, best_key = (sb(n, [128, B]) for n in ("top", "total", "inverse", "best_key"))
        gateT = sb("gateT", [E, B * S])
        hidden_raw = sb("hidden_raw", [128, B, D])
        hidden = sb("hidden", [128, 2, D])
        hiddenT = sb("hiddenT", [128, 2, 2, D], F32R)

        norm_bank = pb("norm_bank", [128, 2, 512])
        gate_bank = pb("gate_bank", [128, 512])
        hidden_bank = pb("hidden_bank", [128, 2, 512])
        hiddenT_bank = pb("hiddenT_bank", [128, 512])
        y_bank = pb("y_bank", [128, 2, 512])

        norm = Norm(ctx, sems, nc, f"{name}_norm", moments, xT, scratch, norm_bank, ident)
        split = Splitter(sems, nc, name)
        loaded = [sem(f"loaded{i}") for i in range(3)]
        split.add(loaded[0], 16, gate_raw[:], gate[:, HI], gate[:, LO])
        for k in range(KT):
            split.add(loaded[1], 16, a_raw[:, k, :], a[:, HI, k, :], a[:, LO, k, :])
        for k in range(KT):
            split.add(loaded[2], 16, b_raw[:, k, :], b_w[:, HI, k, :], b_w[:, LO, k, :])
        rank_set, gated, exped, small, weighted_ready = (sem(n) for n in (
            "rank_set", "gated", "exped", "small", "weighted_ready"))
        gateT_done, gateT_copied, hidden_copied = sem("gateT_done"), sem("gateT_copied"), sem("hidden_copied")
        hidden_done, hidden_scaled, hidden_transposed = sem("hidden_done"), sem("hidden_scaled"), sem("hiddenT_done")
        hiddenT_hi, hiddenT_ready, y_done, y_added = (sem(n) for n in ("hiddenT_hi", "hiddenT_ready", "y_done", "y_added"))
        shifted_ready = sem("shifted_ready")
        moments.start_layer(sems, name)
        block = ctx.enter_context(nc.Block())

        @block.sync
        def _(sp):
            sp.dma_start(gate_raw[:], gate_w).then_inc(loaded[0], 16)
            sp.dma_start(a_raw[:], lora_a).then_inc(loaded[1], 16)
            sp.dma_start(b_raw[:], lora_b).then_inc(loaded[2], 16)

        @block.gpsimd
        def _(pool):
            pool.iota(rank_first[:], pattern=[[0, B], [-1, E]], base=E, channel_multiplier=0,
                      allow_small_or_imprecise_dtypes=True).then_inc(rank_set, 1)
            norm.gpsimd(pool)
            split.gpsimd(pool)

        @block.scalar
        def _(act):
            split.scalar(act, 0, 1)
            for h in range(2):
                norm.scalar(act, range(h * HALF, (h + 1) * HALF))
                if h == 0:
                    split.scalar(act, 1, 1 + KT)
                act.wait_ge(gateT_done, h + 1)
                act.activation(gateT[:, h * TOK:(h + 1) * TOK], y_bank[0:E, h, :], ACT.Copy).then_inc(gateT_copied, 1)
            split.scalar(act, 1 + KT)
            for b in range(B):
                act.wait_ge(hidden_done, b + 1)
                act.activation(hidden_raw[:, b, :], hidden_bank[:, b % 2, :], ACT.Copy).then_inc(hidden_copied, 1)
                if b == 0:
                    act.wait_ge(shifted_ready, 1)
                    act.activation(prob[:], shifted[:], ACT.Exp).then_inc(exped, 1)
            for b in range(B):
                act.wait_ge(hidden_transposed, b + 1)
                wait_count(act, y_done, b - 1)
                act.activation(hiddenT[:, HI, b % 2, :], hiddenT_bank[:], ACT.Copy).then_inc(hiddenT_hi, 1)

        @block.tensor
        def _(pe):
            for h in range(2):
                norm.tensor(pe, range(h * HALF, (h + 1) * HALF))
                pe.wait_ge(split.ready, 1)
                pe.wait_ge(norm.ready, HALF * (h + 1))
                for k in range(KT):
                    last = matmul3(pe, y_bank[0:E, h, :], lambda p: gate[:, p, k, :],
                                   lambda p: xT[:, p, k, h * TOK:(h + 1) * TOK], k == 0, k == KT - 1)
                last.then_inc(gateT_done, 1)

            def hidden_product(b):
                if b >= 2:
                    pe.wait_ge(hidden_copied, b - 1)
                tok = slice(b * S, (b + 1) * S)
                for k in range(KT):
                    last = matmul3(pe, hidden_bank[:, b % 2, :], lambda p: xT[:, p, k, tok],
                                   lambda p: a[:, p, k, :], k == 0, k == KT - 1)
                last.then_inc(hidden_done, 1)
            pe.wait_ge(gateT_copied, 2)
            for b in range(B):
                last = pe.transpose(gate_bank[:, b * E:(b + 1) * E], gateT[:, b * S:(b + 1) * S], ident[0:E, 0:E])
            last.then_inc(gated, 1)
            pe.wait_ge(split.ready, 1 + KT)
            for b in range(B):
                hidden_product(b)
            pe.wait_ge(split.ready, 1 + 2 * KT)
            for b in range(B + 1):
                if b < B:
                    pe.wait_ge(hidden_scaled, b + 1)
                    wait_count(pe, hiddenT_ready, b)
                    for k in range(KT):
                        last = pe.transpose(hiddenT_bank[:, k * 128:(k + 1) * 128],
                                            hidden[:, b % 2, k * 128:(k + 1) * 128], ident[:])
                    last.then_inc(hidden_transposed, 1)
                if b >= 1:
                    c = b - 1
                    pe.wait_ge(hiddenT_ready, c + 1)
                    wait_count(pe, y_added, c - 1)
                    for k in range(KT):
                        last = matmul3(pe, y_bank[:, c % 2, :], lambda p: hiddenT[:, p, c % 2, k * 128:(k + 1) * 128],
                                       lambda p: b_w[:, p, k, :], k == 0, k == KT - 1)
                    last.then_inc(y_done, 1)

        @block.vector
        def _(dve):
            norm.statistics(dve)
            norm.vector(dve)
            done = 0

            def chain(instruction):
                nonlocal done
                done += 1
                instruction.then_inc(small, 1)
                dve.wait_ge(small, done)

            def wide(ap):
                return ap[:].unsqueeze(2).broadcast_to([128, B, E])
            logits = gate_bank[:, 0:B * E].rearrange("p (b e) -> p b e", e=E)
            dve.wait_ge(gated, 1)
            chain(dve.tensor_reduce(top[:], logits, AX.X, ALU.max))
            dve.tensor_tensor(shifted[:], logits, wide(top), ALU.subtract).then_inc(shifted_ready, 1)
            dve.wait_ge(exped, 1)
            chain(dve.tensor_reduce(total[:], prob[:], AX.X, ALU.add))
            chain(dve.reciprocal(inverse[:], total[:]))
            chain(dve.tensor_tensor(prob[:], prob[:], wide(inverse), ALU.mult))
            dve.wait_ge(rank_set, 1)
            left = prob
            for n in range(2):
                chain(dve.tensor_reduce(best[n][:], left[:], AX.X, ALU.max))
                chain(dve.tensor_tensor(equal[:], left[:], wide(best[n]), ALU.is_equal))
                chain(dve.tensor_tensor(key[:], equal[:], rank_first[:], ALU.mult))
                chain(dve.tensor_reduce(best_key[:], key[:], AX.X, ALU.max))
                chain(dve.tensor_tensor(chosen[n][:], key[:], wide(best_key), ALU.is_equal))
                if n == 0:
                    chain(dve.scalar_tensor_tensor(rest[:], chosen[0][:], -2.0, prob[:], ALU.mult, ALU.add))
                    left = rest
            chain(dve.tensor_tensor(total[:], best[0][:], best[1][:], ALU.add))
            chain(dve.reciprocal(inverse[:], total[:]))
            for n in range(2):
                chain(dve.tensor_tensor(best[n][:], best[n][:], inverse[:], ALU.mult))
                chain(dve.tensor_tensor(chosen[n][:], chosen[n][:], wide(best[n]), ALU.mult))
            chain(dve.tensor_tensor(expert_weight[:], chosen[0][:], chosen[1][:], ALU.add))

            def scale_hidden(b):
                dve.wait_ge(hidden_copied, b + 1)
                wait_count(dve, hidden_transposed, b - 1)
                dve.tensor_tensor(hidden[:, b % 2, :].rearrange("p (e r) -> p e r", e=E),
                                  hidden_raw[:, b, :].rearrange("p (e r) -> p e r", e=E),
                                  expert_weight[:, b, :].unsqueeze(2).broadcast_to([128, E, D // E]),
                                  ALU.mult).then_inc(hidden_scaled, 1)
            scale_hidden(0)
            for b in range(B + 1):
                if b < B:
                    dve.wait_ge(hiddenT_hi, b + 1)
                    dve.tensor_tensor(hiddenT[:, LO, b % 2, :], hiddenT_bank[:], as_f32(hiddenT[:, HI, b % 2, :]),
                                      ALU.subtract).then_inc(hiddenT_ready, 1)
                if b + 1 < B:
                    scale_hidden(b + 1)
                if b >= 1:
                    dve.wait_ge(y_done, b)
                    dve.tensor_tensor(x[:, b - 1, :], y_bank[:, (b - 1) % 2, :], x[:, b - 1, :], ALU.add)\
                       .then_inc(y_added, 1)
                    moments.batch_stats(dve, b - 1, y_added, b)
            moments.mean_and_var(dve, range(B))


def adapter_layer(nc, sems, moments, ident, weight, bias, lora_a, lora_b, starts, out):
    name, N, R, x = "ffn", 3, 16, moments.x
    with ExitStack() as ctx:
        def sb(n, shape, dt=F32):
            return ctx.enter_context(nc.sbuf_tensor(f"{name}_{n}", shape, dt))

        def pb(n, shape):
            return ctx.enter_context(nc.psum_tensor(f"{name}_{n}", shape, F32))

        def sem(n):
            return sems.new(f"{name}_{n}")

        n_starts = starts.shape[0]
        xT = sb("xT", [128, 2, KT, B * S], F32R)
        scratch = sb("scratch", [128, 2, D])
        w_raw, w = sb("w_raw", [128, KT, D]), sb("w", [128, 2, KT, D], F32R)
        a_raw, a = sb("a_raw", [128, KT, N * R]), sb("a", [128, 2, KT, N * R], F32R)
        b_w = sb("b_w", [N * R, D])
        bias_all = sb("bias_all", [128, D])
        starts_all = sb("starts_all", [128, n_starts], I32)
        starts_f = sb("starts_f", [128, n_starts])
        batch_number = sb("batch_number", [128, B, n_starts])
        begun = sb("begun", [128, B, n_starts])
        segment = sb("segment", [128, B])
        adapter_on = sb("adapter_on", [128, B, N])
        adapter_number = sb("adapter_number", [128, B, N])
        low = sb("low", [128, 2, N * R])
        lowT = sb("lowT", [N * R, 2, S])
        norm_bank = pb("norm_bank", [128, 2, 512])
        y_bank = pb("y_bank", [128, 2, 512])
        low_bank = pb("low_bank", [128, 2, 512])
        lowT_bank = pb("lowT_bank", [128, 2, 512])

        norm = Norm(ctx, sems, nc, f"{name}_norm", moments, xT, scratch, norm_bank, ident)
        split = Splitter(sems, nc, name)
        loaded = [sem(f"loaded{i}") for i in range(2)]
        split.add(loaded[0], 16, a_raw[:], a[:, HI], a[:, LO])
        for k in range(KT):
            split.add(loaded[1], 16, w_raw[:, k, :], w[:, HI, k, :], w[:, LO, k, :])
        small_loaded, numbers_set, small = sem("small_loaded"), sem("numbers_set"), sem("small")
        low_done, low_scaled, low_transposed, lowT_ready = (sem(n) for n in (
            "low_done", "low_scaled", "low_transposed", "lowT_ready"))
        y_done, y_added, stored, biased = sem("y_done"), sem("y_added"), sem("stored"), sem("x_biased")
        block = ctx.enter_context(nc.Block())

        @block.sync
        def _(sp):
            sp.dma_start(starts_all[:], starts.partition_broadcast(128)).then_inc(small_loaded, 16)
            sp.dma_start(bias_all[:], bias.partition_broadcast(128)).then_inc(small_loaded, 16)
            sp.dma_start(b_w[:], lora_b).then_inc(small_loaded, 16)
            sp.dma_start(a_raw[:], lora_a).then_inc(loaded[0], 16)
            sp.dma_start(w_raw[:], weight).then_inc(loaded[1], 16)
            for b in range(B):
                sp.wait_ge(y_added, b + 1)
                sp.dma_start(out[b], x[:, b, :]).then_inc(stored, 16)
            sp.wait_ge(stored, 16 * B)

        @block.gpsimd
        def _(pool):
            pool.iota(batch_number[:], pattern=[[1, B], [0, n_starts]], base=0, channel_multiplier=0,
                      allow_small_or_imprecise_dtypes=True).then_inc(numbers_set, 1)
            pool.iota(adapter_number[:], pattern=[[0, B], [1, N]], base=2, channel_multiplier=0,
                      allow_small_or_imprecise_dtypes=True).then_inc(numbers_set, 1)
            norm.gpsimd(pool)
            split.gpsimd(pool)
            pool.wait_ge(small_loaded, 48)
            for b in range(B):
                pool.wait_ge(norm.ready, b + 1)
                pool.tensor_tensor(x[:, b, :], x[:, b, :], bias_all[:], ALU.add).then_inc(biased, 1)

        @block.scalar
        def _(act):
            split.scalar(act, 0, 1)
            norm.scalar(act, range(HALF))
            split.scalar(act, 1)
            norm.scalar(act, range(HALF, B))
            for b in range(B):
                act.wait_ge(low_transposed, b + 1)
                if b >= 2:
                    act.wait_ge(y_done, b - 1)
                act.activation(lowT[:, b % 2, :], lowT_bank[0:N * R, b % 2, 0:S], ACT.Copy).then_inc(lowT_ready, 1)

        @block.tensor
        def _(pe):
            norm.tensor(pe, range(HALF))
            pe.wait_ge(split.ready, 1)
            pe.wait_ge(norm.ready, HALF)

            def down(b):
                tok = slice(b * S, (b + 1) * S)
                for k in range(KT):
                    last = matmul3(pe, low_bank[:, b % 2, 0:N * R], lambda p: xT[:, p, k, tok],
                                   lambda p: a[:, p, k, :], k == 0, k == KT - 1)
                last.then_inc(low_done, 1)
            down(0)
            norm.tensor(pe, range(HALF, HALF + 2))
            down(1)
            norm.tensor(pe, range(HALF + 2, B))
            pe.wait_ge(small_loaded, 48)
            pe.wait_ge(split.ready, 1 + KT)
            pe.wait_ge(norm.ready, B)
            for b in range(B):
                tok = slice(b * S, (b + 1) * S)
                if 1 <= b < B - 1:
                    pe.wait_ge(low_scaled, b)
                    down(b + 1)
                pe.wait_ge(low_scaled, b + 1)
                if b >= 2:
                    pe.wait_ge(lowT_ready, b - 1)
                pe.transpose(lowT_bank[0:N * R, b % 2, 0:S], low[:, b % 2, :], ident[:]).then_inc(low_transposed, 1)
                if b >= 2:
                    pe.wait_ge(y_added, b - 1)
                for k in range(KT):
                    matmul3(pe, y_bank[:, b % 2, :], lambda p: xT[:, p, k, tok], lambda p: w[:, p, k, :], k == 0, False)
                pe.wait_ge(lowT_ready, b + 1)
                pe.matmul(y_bank[:, b % 2, :], lowT[:, b % 2, :], b_w[:], start=False, stop=True,
                          skip_group_check=True).then_inc(y_done, 1)

        @block.vector
        def _(dve):
            norm.statistics(dve)

            def find_adapters(b):
                if b != HALF:
                    return
                dve.wait_ge(small_loaded, 48)
                dve.tensor_copy(starts_f[:], starts_all[:]).then_inc(small, 1)
                dve.wait_ge(small, 1)
                dve.wait_ge(numbers_set, 2)
                dve.tensor_tensor(begun[:], batch_number[:], starts_f[:].unsqueeze(1).broadcast_to([128, B, n_starts]),
                                  ALU.is_ge).then_inc(small, 1)
                dve.wait_ge(small, 2)
                dve.tensor_reduce(segment[:], begun[:], AX.X, ALU.add).then_inc(small, 1)
                dve.wait_ge(small, 3)
                dve.tensor_tensor(adapter_on[:], segment[:].unsqueeze(2).broadcast_to([128, B, N]), adapter_number[:],
                                  ALU.is_equal).then_inc(small, 1)
                dve.wait_ge(small, 4)
            norm.vector(dve, find_adapters)

            def scale_low(b):
                dve.wait_ge(low_done, b + 1)
                if b >= 2:
                    dve.wait_ge(low_transposed, b - 1)
                dve.tensor_tensor(low[:, b % 2, :].rearrange("p (n r) -> p n r", n=N),
                                  low_bank[:, b % 2, 0:N * R].rearrange("p (n r) -> p n r", n=N),
                                  adapter_on[:, b, :].unsqueeze(2).broadcast_to([128, N, R]), ALU.mult)\
                   .then_inc(low_scaled, 1)
            scale_low(0)
            for b in range(B):
                if b + 1 < B:
                    scale_low(b + 1)
                dve.wait_ge(y_done, b + 1)
                dve.wait_ge(biased, b + 1)
                dve.tensor_tensor(x[:, b, :], y_bank[:, b % 2, :], x[:, b, :], ALU.add).then_inc(y_added, 1)


def small_attention(nc, sems, moments, ident, w_q_dram, w_k_dram, w_v_dram, w_o_dram, rope_q, rope_k, causal,
                    parities, swap_dram):
    name, T, HW, KV = "small", 4, 16, 8
    UNITS_OF_PAIR = 16
    x = moments.x
    BATCH_PAIRS = B // 2
    UNITS = UNITS_OF_PAIR * BATCH_PAIRS
    with ExitStack() as ctx:
        def sb(n, shape, dt=F32):
            return ctx.enter_context(nc.sbuf_tensor(f"{name}_{n}", shape, dt))

        def pb(n, shape):
            return ctx.enter_context(nc.psum_tensor(f"{name}_{n}", shape, F32))

        def sem(n):
            return sems.new(f"{name}_{n}")

        xT = sb("xT", [128, 2, KT, B * S], F32R)
        probs = sb("probs", [128, 3, D])
        scratch = vT = probs[:, 0:2, :]
        mask, identity = sb("mask", [128, 4 * S], F32R), sb("identity", [128, 128], F32R)
        raw = sb("raw", [128, KT, D])
        k_raw, v_raw = sb("k_raw", [128, KT, 128]), sb("v_raw", [128, KT, 128])
        w_q = sb("w_q", [128, 2, KT, T * 128], F32R)
        w_k = sb("w_k", [128, 2, KT, 128], F32R)
        swap = sb("swap", [128, 128])
        plain = sb("plain", [128, 3, TOK])
        w_v = sb("w_v", [128, 2, KT, 128], F32R)
        w_o = sb("w_o", [128, 2, KT, D], F32R)
        qT = sb("qT", [128, 2, T, B * S], F32R)
        kT = sb("kT", [128, 2, 2, B * S], F32R)
        v_tok = sb("v_tok", [128, B, 2, KV * HW])
        cos_q, sin_q, cos_k, sin_k = (sb(n, [128, S]) for n in ("cos_q", "sin_q", "cos_k", "sin_k"))
        causal_add, parity = sb("causal_add", [128, S]), sb("parity", [128, 2])
        direct, crossed = sb("direct", [128, 2, TOK]), sb("crossed", [128, 2, TOK])
        neg_max = sb("neg_max", [128, 3, 4])
        exp_sum, inv_sum = sb("exp_sum", [128, 3, 4]), sb("inv_sum", [128, 3, 4])
        probsT = sb("probsT", [128, 2, 512])
        heads_outT = sb("heads_outT", [128, 2, T, 2 * S], F32R)

        pair_banks = [pb("proj_bank", [128, 2, 512]), pb("score_bank", [128, 2, 512]), pb("probsT_bank", [128, 2, 512])]
        proj_bank, score_bank, probsT_bank = pair_banks
        out_bank = pb("out_bank", [128, 2, 512])

        norm = Norm(ctx, sems, nc, f"{name}_norm", moments, xT, scratch, proj_bank, ident)
        split = Splitter(sems, nc, name)
        k_loaded, v_loaded, q_loaded, o_loaded, const_loaded = (sem(n) for n in (
            "k_loaded", "v_loaded", "q_loaded", "o_loaded", "const_loaded"))
        split.add(k_loaded, 16, k_raw[:], w_k[:, HI], w_k[:, LO])
        split.add(v_loaded, 16, v_raw[:], w_v[:, HI], w_v[:, LO])
        N_KV = len(split.pieces)
        for k in range(KT):
            def tiles(ap):
                return ap.rearrange("p (t j d) -> p t j d", t=T, j=KV)
            split.add(q_loaded, 16, raw[:, k, :].rearrange("p (j t d) -> p t j d", t=T, j=KV),
                      tiles(w_q[:, HI, k]), tiles(w_q[:, LO, k]))
        N_EARLY = len(split.pieces)
        for k in range(KT):
            split.add(o_loaded, 16, raw[:, k, :], w_o[:, HI, k], w_o[:, LO, k])
        tasks = [("k", 0, h) for h in range(2)] + [("q", t, h) for h in range(2) for t in range(T)]
        projected, copied, swapped, products, rotated, part_hi, part_ready = (sem(n) for n in (
            "projected", "copied", "swapped", "products", "rotated", "part_hi", "part_ready"))
        vT_done, vT_copied, v_done, v_ready = sem("vT_done"), sem("vT_copied"), sem("v_done"), sem("v_ready")
        scored, maxed, exped, transposed, attended = (sem(n) for n in (
            "scored", "maxed", "exped", "transposed", "attended"))
        v_zeroed, inverted, scaled = sem("v_zeroed"), sem("inverted"), sem("scaled")
        mask_set, probsT_ready = sem("mask_set"), sem("probsT_ready")
        tile_hi, tile_ready, y_done, y_added = (sem(n) for n in ("tile_hi", "tile_ready", "y_done", "y_added"))
        moments.start_layer(sems, name)
        block = ctx.enter_context(nc.Block())

        def unit(u):
            return u // UNITS_OF_PAIR, u // 4 % 4, u % 4

        def scores_of(u):
            return proj_bank[:, 1, :] if u % 3 == 2 else score_bank[:, u % 3, :]

        def tile_at(u):
            return u // 4 - 1 if 4 < u <= UNITS + 1 and u % 4 == 1 else None

        def y_at(u):
            done = u - UNITS_OF_PAIR
            return 2 * (done // UNITS_OF_PAIR) + done % UNITS_OF_PAIR // 2 - 1 \
                if done > 0 and done % UNITS_OF_PAIR in (3, 5) else None
        STEPS = range(-3, UNITS + 7)

        @block.sync
        def _(sp):
            sp.dma_start(k_raw[:], w_k_dram).then_inc(k_loaded, 16)
            sp.dma_start(v_raw[:], w_v_dram).then_inc(v_loaded, 16)
            sp.dma_start(raw[:], w_q_dram).then_inc(q_loaded, 16)
            for to, of in ((cos_q, rope_q[0]), (sin_q, rope_q[1]), (cos_k, rope_k[0]), (sin_k, rope_k[1]),
                           (causal_add, causal), (parity, parities), (swap, swap_dram)):
                sp.dma_start(to[:], of).then_inc(const_loaded, 16)
            sp.wait_ge(split.ready, N_EARLY)
            sp.dma_start(raw[:], w_o_dram).then_inc(o_loaded, 16)

        @block.tensor
        def _(pe):
            def project_values(h):
                pe.wait_ge(norm.ready, HALF * (h + 1))
                for k in range(KT):
                    last = matmul3(pe, out_bank[:, h, :], lambda p: w_v[:, p, k, :],
                                   lambda p: xT[:, p, k, h * TOK:(h + 1) * TOK], k == 0, k == KT - 1)
                last.then_inc(vT_done, 1)
            norm.tensor(pe, range(HALF))
            pe.wait_ge(split.ready, N_KV)
            project_values(0)
            norm.tensor(pe, range(HALF, B))
            pe.wait_ge(norm.ready, B)
            pe.wait_ge(const_loaded, 16 * 7)
            for n in range(len(tasks) + 1):
                if n < len(tasks):
                    kind, t, h = tasks[n]
                    if n == 2:
                        pe.wait_ge(split.ready, N_EARLY)
                    wait_count(pe, products, n - 2)
                    for k in range(KT):
                        last = matmul3(pe, pair_banks[n % 3][:, 0, :],
                                       (lambda p: w_k[:, p, k, :]) if kind == "k" else
                                       (lambda p: w_q[:, p, k, t * 128:(t + 1) * 128]),
                                       lambda p: xT[:, p, k, h * TOK:(h + 1) * TOK], k == 0, k == KT - 1)
                    last.then_inc(projected, 1)
                if n >= 1:
                    pe.wait_ge(copied, n)
                    pe.matmul(pair_banks[(n - 1) % 3][:, 1, :], swap[:], plain[:, (n - 1) % 3, :], start=True,
                              stop=True).then_inc(swapped, 1)
            project_values(1)
            pe.wait_ge(mask_set, 2)
            pe.wait_ge(part_ready, len(tasks) - 2)

            def step(u):
                if u + 3 < UNITS:
                    pair, t, group = unit(u + 3)
                    rows32 = slice(32 * group, 32 * group + 32)
                    if u + 3 == 2:
                        pe.wait_ge(vT_copied, 2)
                        for b in range(B):
                            last = pe.transpose(out_bank[:, b // HALF, (b % HALF) * 128:(b % HALF + 1) * 128],
                                                vT[:, b // HALF, (b % HALF) * S:(b % HALF + 1) * S], ident[:])
                        last.then_inc(v_done, 1)
                        pe.wait_ge(part_ready, len(tasks))
                    wait_count(pe, exped, u + 1)
                    pe.matmul(scores_of(u + 3), identity[:], mask[:], start=True, stop=False,
                              skip_group_check=True)
                    for bi in range(2):
                        tok = slice((2 * pair + bi) * S, (2 * pair + bi + 1) * S)
                        last = matmul3(pe, scores_of(u + 3)[:, bi * 256:(bi + 1) * 256],
                                       lambda p: qT[rows32, p, t, tok], lambda p: kT[rows32, p, :, tok], False, True)
                    last.then_inc(scored, 1)
                if 0 <= u < UNITS:
                    pe.wait_ge(scaled, u + 1)
                    wait_count(pe, probsT_ready, u - 1)
                    for i in range(4):
                        last = pe.transpose(probsT_bank[:, u % 2, i * S:(i + 1) * S],
                                            probs[:, u % 3, i * S:(i + 1) * S], ident[:])
                    last.then_inc(transposed, 1)
                v = u - 1
                if 0 <= v < UNITS:
                    pair, t, group = unit(v)
                    tile = v // 4
                    rows32 = slice(32 * group, 32 * group + 32)
                    pe.wait_ge(v_ready, 2)
                    pe.wait_ge(probsT_ready, v + 1)
                    wait_count(pe, tile_ready, tile - 1)
                    for bi in range(2):
                        for par in range(2):
                            last = pe.matmul(out_bank[rows32, tile % 2, bi * S:(bi + 1) * S],
                                             v_tok[:, 2 * pair + bi, par, rows32],
                                             probsT[:, v % 2, (2 * bi + par) * S:(2 * bi + par + 1) * S],
                                             start=par == 0, stop=par == 1, skip_group_check=True)
                    last.then_inc(attended, 1)
                n = y_at(u)
                if n is not None:
                    pe.wait_ge(tile_ready, T * (n // 2 + 1))
                    wait_count(pe, y_added, n)
                    pe.wait_ge(split.ready, N_EARLY + KT)
                    for t in range(T):
                        last = matmul3(pe, proj_bank[:, 0, :],
                                       lambda p: heads_outT[:, p, t, (n % 2) * S:(n % 2 + 1) * S],
                                       lambda p: w_o[:, p, t, :], t == 0, t == T - 1)
                    last.then_inc(y_done, 1)
            for u in STEPS:
                step(u)

        @block.scalar
        def _(act):
            split.scalar(act, 0, N_KV)
            norm.scalar(act)
            split.scalar(act, N_KV, N_EARLY)

            def copy_values(h):
                act.wait_ge(vT_done, h + 1)
                act.activation(vT[:, h, :], out_bank[:, h, :], ACT.Copy).then_inc(vT_copied, 1)
            act.wait_ge(const_loaded, 16 * 7)
            act.activation(identity[:], ident[:], ACT.Copy).then_inc(mask_set, 1)
            act.activation(mask[:].rearrange("p (i k) -> p i k", i=4),
                           causal_add[:].unsqueeze(1).broadcast_to([128, 4, S]), ACT.Copy).then_inc(mask_set, 1)

            def copy_plain(n):
                act.wait_ge(projected, n + 1)
                wait_count(act, products, n - 2)
                act.activation(plain[:, n % 3, :], pair_banks[n % 3][:, 0, :], ACT.Copy).then_inc(copied, 1)
            copy_plain(0)
            for n, (kind, t, h) in enumerate(tasks):
                if n + 1 < len(tasks):
                    copy_plain(n + 1)
                tok = slice(h * TOK, (h + 1) * TOK)
                act.wait_ge(rotated, n + 1)
                if kind == "q":
                    last = act.activation(qT[:, HI, t, tok], direct[:, n % 2, :], ACT.Copy)
                else:
                    for par in range(2):
                        last = act.activation(kT[:, HI, par, tok], direct[:, n % 2, :], ACT.Copy,
                                              scale=parity[:, par:par + 1])
                last.then_inc(part_hi, 1)
                if n in (1, len(tasks) - 1):
                    copy_values(n > 1)
                if n == 4:
                    split.scalar(act, N_EARLY)

            def place_values():
                def heads(ap):
                    return ap.rearrange("p b (j s d) -> p b j s d", s=2, d=HW)
                act.wait_ge(v_zeroed, 1)
                for i in range(2):
                    for par in range(2):
                        last = act.activation(heads(v_tok[:, i * HALF:(i + 1) * HALF, par, :])[:, :, :, par, :],
                                              heads(out_bank[:, i, :].rearrange("p (b n) -> p b n", b=HALF))
                                              [:, :, :, par, :], ACT.Copy)
                    last.then_inc(v_ready, 1)
            act.wait_ge(v_done, 1)

            def step(u):
                tile = tile_at(u)
                if tile is not None:
                    act.wait_ge(attended, 4 * (tile + 1))
                    wait_count(act, y_done, 2 * (tile // T))
                    act.activation(heads_outT[:, HI, tile % T, :], out_bank[:, tile % 2, 0:2 * S], ACT.Copy)\
                       .then_inc(tile_hi, 1)
                if u + 3 < UNITS:
                    act.wait_ge(maxed, u + 4)
                    wait_count(act, transposed, u + 1)
                    for i in range(4):
                        last = act.activation(probs[:, u % 3, i * S:(i + 1) * S],
                                              scores_of(u + 3)[:, i * S:(i + 1) * S], ACT.Exp,
                                              bias=neg_max[:, u % 3, i:i + 1],
                                              accum_out=exp_sum[:, u % 3, i:i + 1])
                    last.then_inc(exped, 1)
                if u + 3 == 1:
                    place_values()
            for u in STEPS:
                step(u)

        @block.vector
        def _(dve):
            norm.statistics(dve)
            norm.vector(dve)
            dve.wait_ge(const_loaded, 16 * 7)

            def four(ap):
                return ap.rearrange("p (b t) -> p b t", b=HALF)

            def table(ap):
                return ap[:].unsqueeze(1).broadcast_to([128, HALF, S])
            def low_part(n):
                kind, t, h = tasks[n]
                tok = slice(h * TOK, (h + 1) * TOK)
                dve.wait_ge(part_hi, n + 1)
                if kind == "q":
                    dve.tensor_tensor(qT[:, LO, t, tok], direct[:, n % 2, :], as_f32(qT[:, HI, t, tok]),
                                      ALU.subtract).then_inc(part_ready, 1)
                else:
                    for par in range(2):
                        last = dve.scalar_tensor_tensor(kT[:, LO, par, tok], direct[:, n % 2, :],
                                                        parity[:, par:par + 1],
                                                        as_f32(kT[:, HI, par, tok]), ALU.mult, ALU.subtract)
                    last.then_inc(part_ready, 1)

            for n, (kind, t, h) in enumerate(tasks):
                cos, sin = (cos_q, sin_q) if kind == "q" else (cos_k, sin_k)
                dve.wait_ge(swapped, n + 1)
                wait_count(dve, part_ready, n - 1)
                dve.tensor_tensor(four(direct[:, n % 2, :]), four(plain[:, n % 3, :]), table(cos), ALU.mult)
                dve.tensor_tensor(four(crossed[:, n % 2, :]), four(pair_banks[n % 3][:, 1, :]), table(sin),
                                  ALU.mult).then_inc(products, 1)
                if n >= 1:
                    low_part(n - 1)
            low_part(len(tasks) - 1)

            def step(u):
                if u + 3 < UNITS:
                    dve.wait_ge(scored, u + 4)
                    dve.tensor_reduce(neg_max[:, u % 3, :],
                                      scores_of(u + 3).rearrange("p (i k) -> p i k", i=4), AX.X,
                                      ALU.max, negate=True).then_inc(maxed, 1)
                if 0 <= u + 2 < UNITS:
                    dve.wait_ge(exped, u + 3)
                    wait_count(dve, scaled, u)
                    dve.reciprocal(inv_sum[:, (u + 2) % 3, :], exp_sum[:, (u + 2) % 3, :]).then_inc(inverted, 1)
                if 0 <= u < UNITS:
                    dve.wait_ge(transposed, u + 1)
                    wait_count(dve, attended, u - 1)
                    dve.tensor_copy(probsT[:, u % 2, :], probsT_bank[:, u % 2, :]).then_inc(probsT_ready, 1)
                tile = tile_at(u)
                if tile is not None:
                    dve.wait_ge(tile_hi, tile + 1)
                    dve.tensor_tensor(heads_outT[:, LO, tile % T, :], out_bank[:, tile % 2, 0:2 * S],
                                      as_f32(heads_outT[:, HI, tile % T, :]), ALU.subtract).then_inc(tile_ready, 1)
                n = y_at(u - 1)
                if n is not None:
                    dve.wait_ge(y_done, n + 1)
                    dve.tensor_tensor(x[:, n, :], proj_bank[:, 0, :], x[:, n, :], ALU.add).then_inc(y_added, 1)
                    moments.batch_stats(dve, n, y_added, n + 1)
            for u in STEPS:
                step(u)
            moments.mean_and_var(dve, range(B))

        @block.gpsimd
        def _(pool):
            norm.gpsimd(pool)
            split.gpsimd(pool, 0, N_EARLY)
            pool.memset(v_tok[:], 0.0).then_inc(v_zeroed, 1)
            for n in range(len(tasks)):
                pool.wait_ge(products, n + 1)
                pool.tensor_tensor(direct[:, n % 2, :], direct[:, n % 2, :], crossed[:, n % 2, :], ALU.add)\
                    .then_inc(rotated, 1)
                if 5 <= n < 5 + KT:
                    split.gpsimd(pool, N_EARLY + n - 5, N_EARLY + n - 4)
            for u in range(UNITS):
                pool.wait_ge(inverted, u + 1)
                p4 = probs[:, u % 3, :].rearrange("p (i k) -> p i k", i=4)
                pool.tensor_tensor(p4, p4, inv_sum[:, u % 3, :].unsqueeze(2).broadcast_to([128, 4, S]), ALU.mult)\
                    .then_inc(scaled, 1)


def decoder(nc, a, out):
    with ExitStack() as ctx:
        x = ctx.enter_context(nc.sbuf_tensor("x_stream", [128, B, D], F32))
        ident = ctx.enter_context(nc.sbuf_tensor("ident", [128, 128], F32))
        moments = Moments(x, ctx.enter_context(nc.sbuf_tensor("moments_stats", [128, B, 6], F32)),
                          ctx.enter_context(nc.sbuf_tensor("moments_mean_var", [128, B, 2], F32)))
        sems = Semaphores(nc)
        attention(nc, sems, "a0", Plan(shared_kv=True), moments, ident,
                  {"q": a["q0"], "k": a["k0"], "v": a["v0"], "o": a["o0"], "q_scales": a["q0_scales"],
                   "k_scales": a["k0_scales"], "v_scales": a["v0_scales"], "o_scales": a["o0_scales"]},
                  None, rope=(a["cos0"], a["sin0"]), causal=a["causal"], codes=True, scale=HD ** -0.5,
                  x_dram=a["x"], ident_dram=a["ident"])
        sems.clear()
        attention(nc, sems, "c0", Plan(shared_kv=False), moments, ident,
                  {"q": a["cq0"], "k": a["ck0"], "v": a["cv0"], "o": a["co0"]}, a["context"],
                  pad_mask=a["mask"], position_bias=a["position_bias"], rms_weight=a["ln_weight"])
        sems.clear()
        expert_layer(nc, sems, moments, ident, a["gate"], a["moe_a"], a["moe_b"])
        sems.clear()
        small_attention(nc, sems, moments, ident, a["q1"], a["k1"], a["v1"], a["o1"], (a["cos1q"], a["sin1q"]),
                        (a["cos1k"], a["sin1k"]), a["causal"], a["parities"], a["swap"])
        sems.clear()
        attention(nc, sems, "c1", Plan(shared_kv=True), moments, ident,
                  {"q": a["cq1"], "k": a["ck1"], "v": a["cv1"], "o": a["co1"]}, a["context"],
                  out_bias=a["bo1"], scale=HD ** -0.5)
        sems.clear()
        adapter_layer(nc, sems, moments, ident, a["ffn_w"], a["ffn_bias"], a["ffn_a"], a["ffn_b"], a["starts"], out)


def _tables(np):
    f = np.float32
    pos = np.arange(S, dtype=f)
    inv = (f(1.0) / f(10000.0) ** (np.arange(0, HD, 2, dtype=f) / f(HD))).astype(f)
    angle = inv[:, None] * pos[None, :]
    cos0 = np.concatenate([np.cos(angle), np.cos(angle)]).astype(f)
    sin0 = np.concatenate([np.sin(angle), -np.sin(angle)]).astype(f)
    width = 16
    idx = np.arange(0, width, 2, dtype=f) / f(width)
    freq = (f(1.0 / (2.0 * np.pi)) * f(500000.0) ** (-idx)).astype(f)
    low, high, length, factor = 1.0, 4.0, 1024, 32.0
    scaled = np.where(freq < low / length, freq / f(factor), freq)
    smooth = np.clip((f(length) * freq - f(low)) / f(high - low), 0.0, 1.0).astype(f)
    mixed = (f(1.0) - smooth) * (freq / f(factor)) + smooth * freq
    freq = np.where((freq >= low / length) & (freq <= high / length), mixed, scaled).astype(f)
    phase = (f(2.0 * np.pi) * pos[:, None] * freq[None, :]).astype(f).T
    cos1 = np.tile(np.concatenate([np.cos(phase), np.cos(phase)]), (8, 1)).astype(f)
    sin1 = np.tile(np.concatenate([-np.sin(phase), np.sin(phase)]), (8, 1)).astype(f)
    causal = np.where(np.tril(np.ones((S, S), bool)), 0.0, MASKED).astype(f)
    kv = np.arange(128) // width
    parities = np.stack([kv % 2 == 0, kv % 2 == 1], axis=1).astype(f)
    swap = np.eye(128, dtype=f)[np.arange(128) ^ (width // 2)]
    quarter = f(width ** -0.5)
    return {"cos0": cos0, "sin0": sin0, "cos1q": cos1 * quarter, "sin1q": sin1 * quarter, "cos1k": cos1,
            "sin1k": sin1, "causal": causal, "ident": np.eye(128, dtype=f), "parities": parities,
            "swap": swap}


def _layout(np, t):
    c = np.ascontiguousarray

    def chunks(w, heads):
        return c(w.reshape(KT, 128, heads, HD).transpose(2, 1, 0, 3).reshape(heads, 128, KT * HD))

    def rotary(w, heads):
        return w.reshape(w.shape[0], heads, HD // 2, 2).transpose(0, 1, 3, 2).reshape(w.shape[0], heads * HD)

    def scale_rows(s, heads):
        return c(s.reshape(KT, heads, HD).transpose(1, 0, 2).reshape(heads, KT * HD))

    def whole(w):
        return c(w.reshape(-1, 128, w.shape[1]).transpose(1, 0, 2))

    def with_bias(w, bias):
        return c(np.concatenate([w, bias.reshape(w.shape[0], 128, 1)], axis=2))
    wkv, bkv = t["L1_xattn_Wkv"], t["L1_xattn_bkv"]
    kv = wkv.shape[1] // 2
    context = t["ctx_4096"].transpose(2, 0, 1).reshape(KT, 128, 2, TOK)
    return {
        "x": c(t["x"]),
        "context": c(context.transpose(2, 0, 1, 3)),
        "mask": c(t["mask_BxSxS2_bk0"].transpose(1, 0, 2)),
        "q0": chunks(rotary(t["L0_attn_q_codes"], NH), NH), "k0": chunks(rotary(t["L0_attn_k_codes"], 8), 8),
        "v0": chunks(t["L0_attn_v_codes"], 8), "o0": c(t["L0_attn_o_codes"].reshape(NH, 128, D)),
        "q0_scales": scale_rows(rotary(t["L0_attn_q_scales"], NH), NH),
        "k0_scales": scale_rows(rotary(t["L0_attn_k_scales"], 8), 8),
        "v0_scales": scale_rows(t["L0_attn_v_scales"], 8), "o0_scales": c(t["L0_attn_o_scales"]),
        "position_bias": c(t["L0_xattn_position_bias"]),
        "ln_weight": c(t["L0_xattn_ln_weight"].reshape(KT, 128).T),
        "cq0": chunks(t["L0_xattn_w_q"].T, NH), "ck0": chunks(t["L0_xattn_w_k"].T, NH),
        "cv0": chunks(t["L0_xattn_w_v"].T, NH), "co0": c(t["L0_xattn_w_out"].T.reshape(NH, 128, D)),
        "gate": whole(t["L0_ffn_gate_w"].T), "moe_a": whole(t["L0_ffn_lora_A"].reshape(-1, D).T),
        "moe_b": whole(t["L0_ffn_lora_B"].transpose(0, 2, 1).reshape(-1, D)),
        "q1": whole(t["L1_attn_Wq"]), "k1": whole(t["L1_attn_Wk"]), "v1": whole(t["L1_attn_Wv"]),
        "o1": whole(t["L1_attn_Wo"].reshape(8, 4, 16, D).transpose(1, 0, 2, 3).reshape(512, D)),
        "cq1": with_bias(chunks(t["L1_xattn_Wq"], NH), t["L1_xattn_bq"]),
        "ck1": with_bias(chunks(wkv[:, :kv], 8), bkv[:kv]), "cv1": with_bias(chunks(wkv[:, kv:], 8), bkv[kv:]),
        "co1": c(t["L1_xattn_Wo"].reshape(NH, 128, D)),
        "bo1": c(t["L1_xattn_bo"]),
        "ffn_w": whole(t["L1_ffn_weight"].T), "ffn_bias": c(t["L1_ffn_bias"]),
        "ffn_a": whole(t["L1_ffn_lora_A"].reshape(-1, D).T),
        "ffn_b": c(t["L1_ffn_lora_B"].transpose(0, 2, 1).reshape(-1, D)),
        "starts": c(t["L1_ffn_lora_start_indices"]),
    }


def kernel(**inputs):
    import numpy as _np
    import concourse.bacc as _bacc
    from concourse import mybir as _mybir
    from concourse.bass_utils import run_bass_kernel_spmd as _run

    arrays = _layout(_np, {name: _np.asarray(v) for name, v in inputs.items()})
    arrays.update(_tables(_np))
    nc = _bacc.Bacc("TRN2", target_bir_lowering=False, num_devices=1)
    handles = {name: nc.dram_tensor(f"in_{name}", v.shape, _mybir.dt.from_np(v.dtype), kind="ExternalInput").ap()
               for name, v in arrays.items()}
    out = nc.dram_tensor("out_x", (B, S, D), _mybir.dt.float32, kind="ExternalOutput").ap()
    decoder(nc, handles, out)
    r = _run(nc, [{f"in_{name}": v for name, v in arrays.items()}], core_ids=[0])
    return r.results[0]["out_x"]
```
